# Optimizing a Trainium2 kernel written in Bass

```python
import numpy as np
import jax
import jax.numpy as jnp

def _softmax(x, axis=-1):
    return jax.nn.softmax(x, axis=axis)

def _gelu(x):
    return jax.nn.gelu(x, approximate=True)

def _silu(x):
    return jax.nn.silu(x)

def _sigmoid(x):
    return jax.nn.sigmoid(x)

def _layernorm(x, axis=-1, eps=1e-05):
    m = jnp.mean(x, axis=axis, keepdims=True)
    v = jnp.var(x, axis=axis, keepdims=True)
    return (x - m) / jnp.sqrt(v + eps)

def _scatter_add(tgt, idx, src, axis=0):
    return tgt.at[idx].add(src)

def _segment_sum(src, seg, n):
    return jax.ops.segment_sum(src, seg, n)
kernel_name = 'mk_sandwich_d2_jaxref_r4_b7c72c'

def setup_inputs(seed: int=0):
    np.random.seed(seed)
    _w = jnp.asarray

    def _L0_attn_setup():
        import jax, jax.numpy as jnp
        import numpy as np
        key = jax.random.key(seed)
        B, C, N = (8, 64, 512)
        x = jax.random.normal(key, (B, C, N), dtype=jnp.float32)
        return {'x': x}
    _L0_attn_in = _L0_attn_setup()

    def _L0_ffn_setup():
        import math
        import jax, jax.numpy as jnp
        import numpy as np
        DIM = 512
        RANK = 8
        B, T = (4, 1024)

        def _orthogonal(key, n):
            a = jax.random.normal(key, (n, n), dtype=jnp.float32)
            q, r = jnp.linalg.qr(a)
            q = q * jnp.sign(jnp.diagonal(r))[None, :]
            return q
        key = jax.random.key(seed)
        kx, kf = jax.random.split(key)
        x = jax.random.normal(kx, (B, T, DIM), dtype=jnp.float32)
        fkeys = jax.random.split(kf, RANK)
        factors = jnp.stack([_orthogonal(fkeys[r], DIM) * (r + 1) ** (-0.5) for r in range(RANK)])
        bias = jnp.zeros((DIM,), dtype=jnp.float32)
        return {'x': x, 'factors': factors, 'bias': bias}
    _L0_ffn_in = _L0_ffn_setup()

    def _L1_attn_setup():
        import jax, jax.numpy as jnp
        import numpy as np
        DIMS = 512
        HEAD_DIM = 64
        NUM_HEADS = DIMS // HEAD_DIM
        GQA_HEADS = 2
        EPS = 1e-08
        key = jax.random.key(seed)
        ks = jax.random.split(key, 6)
        b, s = (2, 512)
        kv_dims = HEAD_DIM * GQA_HEADS
        x = jax.random.normal(ks[0], (b, s, DIMS), dtype=jnp.float32)
        Wq = jax.random.normal(ks[1], (DIMS, DIMS), dtype=jnp.float32) * 0.02
        Wk = jax.random.normal(ks[2], (kv_dims, DIMS), dtype=jnp.float32) * 0.02
        Wv = jax.random.normal(ks[3], (kv_dims, DIMS), dtype=jnp.float32) * 0.02
        Wo = jax.random.normal(ks[4], (DIMS, DIMS), dtype=jnp.float32) * 0.02
        norm_scale = jnp.ones((DIMS,), dtype=jnp.float32)
        split_scale = jnp.full((DIMS,), 0.1, dtype=jnp.float32)
        return {'x': x, 'norm_scale': norm_scale, 'split_scale': split_scale, 'Wq': Wq, 'Wk': Wk, 'Wv': Wv, 'Wo': Wo}
    _L1_attn_in = _L1_attn_setup()

    def _L1_ffn_setup():
        import jax, jax.numpy as jnp
        import numpy as np
        HIDDEN = 512
        INTER = 1408
        B, S = (2, 512)

        def _ternary(key, shape):
            return jax.random.randint(key, shape, -1, 2).astype(jnp.float32)
        key = jax.random.key(seed)
        ks = jax.random.split(key, 7)
        x = jax.random.normal(ks[0], (B, S, HIDDEN), dtype=jnp.float32)
        gate_w = _ternary(ks[1], (INTER, HIDDEN))
        up_w = _ternary(ks[2], (INTER, HIDDEN))
        down_w = _ternary(ks[3], (HIDDEN, INTER))
        gate_s = jax.random.uniform(ks[4], (INTER,), minval=0.01, maxval=0.1, dtype=jnp.float32)
        up_s = jax.random.uniform(ks[5], (INTER,), minval=0.01, maxval=0.1, dtype=jnp.float32)
        down_s = jax.random.uniform(ks[6], (HIDDEN,), minval=0.01, maxval=0.1, dtype=jnp.float32)
        return {'x': x, 'gate_w': gate_w, 'up_w': up_w, 'down_w': down_w, 'gate_s': gate_s, 'up_s': up_s, 'down_s': down_s}
    _L1_ffn_in = _L1_ffn_setup()
    _d = {'L0_attn_x': _L0_attn_in['x'], 'L0_ffn_factors': _L0_ffn_in['factors'], 'L0_ffn_bias': _L0_ffn_in['bias'], 'L1_attn_norm_scale': _L1_attn_in['norm_scale'], 'L1_attn_split_scale': _L1_attn_in['split_scale'], 'L1_attn_Wq': _L1_attn_in['Wq'], 'L1_attn_Wk': _L1_attn_in['Wk'], 'L1_attn_Wv': _L1_attn_in['Wv'], 'L1_attn_Wo': _L1_attn_in['Wo'], 'L1_ffn_gate_w': _L1_ffn_in['gate_w'], 'L1_ffn_up_w': _L1_ffn_in['up_w'], 'L1_ffn_down_w': _L1_ffn_in['down_w'], 'L1_ffn_gate_s': _L1_ffn_in['gate_s'], 'L1_ffn_up_s': _L1_ffn_in['up_s'], 'L1_ffn_down_s': _L1_ffn_in['down_s']}
    _x0 = _d['L0_attn_x']
    _d['L0_attn_x'] = jax.random.normal(jax.random.fold_in(jax.random.key(seed), 1), (8, 512, 512), dtype=_x0.dtype)
    del _x0
    return _d

def reference(L0_attn_x, L0_ffn_factors, L0_ffn_bias, L1_attn_norm_scale, L1_attn_split_scale, L1_attn_Wq, L1_attn_Wk, L1_attn_Wv, L1_attn_Wo, L1_ffn_gate_w, L1_ffn_up_w, L1_ffn_down_w, L1_ffn_gate_s, L1_ffn_up_s, L1_ffn_down_s):

    def _L0_attn_ref(x):
        import jax, jax.numpy as jnp
        import numpy as np
        scores = jnp.einsum('bci,bcj->bij', x, x)
        weights = jax.nn.softmax(scores, axis=-1)
        context = jnp.einsum('bij,bcj->bci', weights, x)
        return context

    def _L0_ffn_ref(x, factors, bias):
        import math
        import jax, jax.numpy as jnp
        import numpy as np
        DIM = 512
        RANK = 8
        B, T = (4, 1024)

        def _orthogonal(key, n):
            a = jax.random.normal(key, (n, n), dtype=jnp.float32)
            q, r = jnp.linalg.qr(a)
            q = q * jnp.sign(jnp.diagonal(r))[None, :]
            return q
        rank = factors.shape[0]
        mixed = jnp.einsum('btd,rde->bte', x, factors)
        mixed = mixed / math.sqrt(rank) + bias
        return mixed

    def _L1_attn_ref(x, norm_scale, split_scale, Wq, Wk, Wv, Wo):
        import jax, jax.numpy as jnp
        import numpy as np
        DIMS = 512
        HEAD_DIM = 64
        NUM_HEADS = DIMS // HEAD_DIM
        GQA_HEADS = 2
        EPS = 1e-08
        b, s, d = x.shape
        H, G, dh = (NUM_HEADS, GQA_HEADS, HEAD_DIM)
        hpg = H // G
        nrm = jnp.linalg.norm(x, axis=-1, keepdims=True) * d ** (-0.5)
        h = norm_scale * x / (nrm + EPS) * split_scale
        q = (h @ Wq.T).reshape(b, s, H, dh)
        k = (h @ Wk.T).reshape(b, s, G, dh)
        v = (h @ Wv.T).reshape(b, s, G, dh)
        q = q.transpose(0, 2, 1, 3).reshape(b, G, hpg, s, dh)
        k = k.transpose(0, 2, 1, 3)
        v = v.transpose(0, 2, 1, 3)
        scores = jnp.einsum('bghsd,bgtd->bghst', q, k) / np.float32(np.sqrt(dh))
        attn = jax.nn.softmax(scores, axis=-1)
        out = jnp.einsum('bghst,bgtd->bghsd', attn, v)
        out = out.reshape(b, H, s, dh).transpose(0, 2, 1, 3).reshape(b, s, H * dh)
        return x + out @ Wo.T

    def _L1_ffn_ref(x, gate_w, up_w, down_w, gate_s, up_s, down_s):
        import jax, jax.numpy as jnp
        import numpy as np
        HIDDEN = 512
        INTER = 1408
        B, S = (2, 512)

        def _ternary(key, shape):
            return jax.random.randint(key, shape, -1, 2).astype(jnp.float32)
        b, s, h = x.shape
        xf = x.reshape(b * s, h)
        g = jnp.einsum('th,ih->ti', xf, gate_w) * gate_s
        u = jnp.einsum('th,ih->ti', xf, up_w) * up_s
        hdn = jax.nn.silu(g) * u
        out = jnp.einsum('ti,hi->th', hdn, down_w) * down_s
        return out.reshape(b, s, -1)
    x = L0_attn_x
    x = x + _layernorm(_L0_attn_ref(_layernorm(x, axis=-1)), axis=-1)
    x = x + _layernorm(_L0_ffn_ref(_layernorm(x, axis=-1), L0_ffn_factors, L0_ffn_bias), axis=-1)
    x = x + _layernorm(_L1_attn_ref(_layernorm(x, axis=-1), L1_attn_norm_scale, L1_attn_split_scale, L1_attn_Wq, L1_attn_Wk, L1_attn_Wv, L1_attn_Wo), axis=-1)
    x = x + _layernorm(_L1_ffn_ref(_layernorm(x, axis=-1), L1_ffn_gate_w, L1_ffn_up_w, L1_ffn_down_w, L1_ffn_gate_s, L1_ffn_up_s, L1_ffn_down_s), axis=-1)
    return x

_drawn_inputs = setup_inputs


def setup_inputs(seed=0):
    import zlib

    import numpy as np

    out = dict(_drawn_inputs(seed))
    spreads = {'L0_ffn_bias': (0.0, 0.1),
     'L1_attn_norm_scale': (1.0, 0.6),
     'L1_attn_split_scale': (0.10000000149011612, 0.6)}
    factors = {'L1_attn_Wq': 8.0, 'L1_attn_Wk': 8.0, 'L1_attn_Wv': 8.0, 'L1_attn_Wo': 8.0}
    for name, (base, spread) in spreads.items():
        noise = np.random.default_rng([zlib.crc32(name.encode()), seed]).standard_normal(out[name].shape)
        drawn = base * np.exp(spread * noise) if base else spread * noise
        out[name] = jnp.asarray(drawn.astype(out[name].dtype))
    for name, factor in factors.items():
        out[name] = (out[name] * factor).astype(out[name].dtype)
    return out
```

```python
from contextlib import ExitStack

import concourse.bass as bass
from concourse import mybir

P = 128
B = 8
N = 512
T = N // P
HEADS = 8
GROUPS = 2
DH = 64
HPG = HEADS // GROUPS
INTER = 1408
IT = INTER // P
RANK = 8
EPS = 1e-5
EPS_RMS = 1e-8

F32 = mybir.dt.float32
F32R = mybir.dt.float32r
I32 = mybir.dt.int32
ALU = mybir.AluOpType
ACT = mybir.ActivationFunctionType
AX = mybir.AxisListType.X


def tile_of(t, i):
    if isinstance(i, int):
        return t[:, i, :]
    return t[:, bass.ds(i, 1), :].rearrange("p a n -> p (a n)")


def rows_of(dram, b):
    if isinstance(b, int):
        return dram[b, :, :].rearrange("(t p) n -> p t n", p=P)
    return dram[bass.ds(b, 1), :, :].rearrange("a (t p) n -> p (a t) n", p=P)


def blocks_of(row):
    return row.rearrange("p (t c) -> p t c", t=T)


def products(nc, out, pairs):
    for n, (lhsT, rhs) in enumerate(pairs):
        last = nc.tensor.matmul(out, lhsT, rhs, start=(n == 0), stop=(n == len(pairs) - 1))
    return last


def wait_alone(eng, s, sem, value):
    eng.wait_ge(sem, value)
    if not isinstance(value, int):
        eng.sem_inc(s.waits_passed, 1)


def over_batches(eng, body):
    body(0, 0, True, False)
    with eng.Fori(0, (B - 2) // 2) as i:
        body(i * 2 + 1, 1, False, False)
        body(i * 2 + 2, 0, False, False)
    body(B - 1, 1, False, True)


class Shared:
    pass


def row_scales(nc, s, pool, mv, ve, rs, shift, exponent, step, at):
    nc.gpsimd.tensor_scalar(ve, mv[:, :, 1], EPS, None, ALU.add)
    nc.gpsimd.tensor_scalar(shift, mv[:, :, 0], -1.0, None, ALU.mult).then_inc(step, 1)
    pool.wait_ge(step, at + 1)
    nc.gpsimd.tensor_tensor(rs, ve, exponent, ALU.pow).then_inc(step, 1)
    pool.wait_ge(step, at + 2)
    return nc.gpsimd.tensor_tensor(shift, shift, rs, ALU.mult)


def column_attention(nc, s, x_in, factors):
    with ExitStack() as ctx:
        def sb(name, shape, dt=F32):
            return ctx.enter_context(nc.sbuf_tensor(name, shape, dt))

        def sem(name):
            return s.stack.enter_context(nc.semaphore("a0_" + name))

        xn = sb("xn", [P, 2, T, N])
        xh = sb("xh", [P, 2, T, N], F32R)
        xl = sb("xl", [P, 2, T, N], F32R)
        xth = sb("xth", [P, 2, T, N], F32R)
        xtl = sb("xtl", [P, 2, T, N], F32R)
        pth = sb("pth", [P, 2, T, N], F32R)
        ptl = sb("ptl", [P, 2, T, N], F32R)
        prob = sb("prob", [P, T, N])
        normed = sb("normed", [P, 2, N])
        factor = sb("factor", [P, T, N])
        bn = sb("bn", [P, T, 6])
        mv = sb("mv", [P, T, 2])
        ve = sb("ve", [P, T])
        rs = sb("rs", [P, T])
        shift = sb("shift", [P, T])
        obn = sb("obn", [P, T, 6])
        omv = sb("omv", [P, T, 2])
        ove = sb("ove", [P, T])
        ors = sb("ors", [P, T])
        oshift = sb("oshift", [P, T])
        neg_max = sb("neg_max", [P, 2 * T])
        row_sum = sb("row_sum", [P, 2 * T])
        inv_sum = sb("inv_sum", [P, 2 * T])

        score = [ctx.enter_context(nc.psum_tensor(f"score{i}", [P, N], F32)) for i in range(2)]
        turned = [ctx.enter_context(nc.psum_tensor(f"turned{i}", [P, N], F32)) for i in range(2)]
        context = [ctx.enter_context(nc.psum_tensor(f"context{i}", [P, N], F32)) for i in range(T)]

        x_loaded = [sem("x_loaded0"), sem("x_loaded1")]
        factor_loaded, factor_used = sem("factor_loaded"), sem("factor_used")
        own_bn, stats = sem("own_bn"), sem("stats")
        pool_step, scales = sem("pool_step"), sem("scales")
        xn_ready, xh_ready, xl_ready = sem("xn_ready"), sem("xh_ready"), sem("xl_ready")
        scored, max_ready, exp_ready = sem("scored"), sem("max_ready"), sem("exp_ready")
        inv_ready, prob_ready = sem("inv_ready"), sem("prob_ready")
        turn_ready, hi_ready, lo_ready = sem("turn_ready"), sem("hi_ready"), sem("lo_ready")
        ctx_ready, own_obn, ostats, opool, oscales = (
            sem("ctx_ready"), sem("own_obn"), sem("ostats"), sem("opool"), sem("oscales"))
        ctx_normed, added = sem("ctx_normed"), sem("added")

        block = ctx.enter_context(nc.Block())

        @block.sync
        def _(sp):
            def load(b, p, first, last):
                if not first:
                    sp.wait_ge(x_loaded[p], ((b - p) * 8))
                if isinstance(b, int):
                    dst = s.x[:, b * T:(b + 1) * T, :]
                else:
                    dst = s.x[:, bass.ds(b * T, T), :]
                sp.dma_start(dst, rows_of(x_in, b)).then_inc(x_loaded[p], 16)
                if first:
                    sp.dma_start(s.factor_sum[:, :, :], rows_of(factors, b)).then_inc(factor_loaded, 16)
                else:
                    sp.wait_ge(factor_loaded, b * 16)
                    sp.wait_ge(factor_used, b)
                    sp.dma_start(factor[:, :, :], rows_of(factors, b)).then_inc(factor_loaded, 16)

            over_batches(sp, load)

        @block.gpsimd
        def _(pool):
            pool.sem_inc(added, 2)

            def scales_of(b):
                wait_alone(pool, s, stats, b + 1)
                row_scales(nc, s, pool, mv, ve[:, :], rs[:, :], shift[:, :], s.minus_half[:, :],
                           pool_step, b * 2).then_inc(scales, 1)

            def lo_of(b, p, t):
                pool.wait_ge(xh_ready, b * T + t + 1)
                nc.gpsimd.tensor_tensor(xl[:, p, t, :], xn[:, p, t, :], xh[:, p, t, :].bitcast(F32),
                                        ALU.subtract).then_inc(xl_ready, 1)

            def normalise(b, p, t):
                wait_alone(pool, s, inv_ready, b * T + t + 1)
                nc.gpsimd.tensor_scalar(prob[:, t, :], prob[:, t, :], inv_sum[:, p * T + t:p * T + t + 1],
                                        1.0, ALU.mult, ALU.mult).then_inc(prob_ready, 1)

            def output_scales(b):
                wait_alone(pool, s, ostats, b + 1)
                row_scales(nc, s, pool, omv, ove[:, :], ors[:, :], oshift[:, :], s.minus_half[:, :],
                           opool, b * 2).then_inc(oscales, 1)

            def add(b, t):
                pool.wait_ge(ctx_normed, b * T + t + 1 + T)
                x = tile_of(s.x, b * T + t)
                nc.gpsimd.tensor_tensor(x, x, normed[:, t % 2, :], ALU.add).then_inc(added, 1)

            scales_of(0)
            for t in range(T):
                lo_of(0, 0, t)

            def body(b, p, first, last):
                normalise(b, p, 0)
                if not last:
                    scales_of(b + 1)
                normalise(b, p, 1)
                normalise(b, p, 2)
                if not last:
                    lo_of(b + 1, 1 - p, 0)
                    lo_of(b + 1, 1 - p, 1)
                normalise(b, p, 3)
                if not last:
                    lo_of(b + 1, 1 - p, 2)
                    lo_of(b + 1, 1 - p, 3)
                if not first:
                    output_scales(b - 1)
                    for t in range(T):
                        add(b - 1, t)

            over_batches(pool, body)
            output_scales(B - 1)
            for t in range(T):
                add(B - 1, t)

        @block.scalar
        def _(act):
            act.sem_inc(ctx_normed, T)

            def exp(b, p, t):
                act.wait_ge(max_ready, b * T + t + 1)
                if not (isinstance(b, int) and b == 0):
                    act.wait_ge(turn_ready, b * 8 - 4 + t + 1 )
                nc.scalar.activation(prob[:, t, :], score[t % 2][:, :], ACT.Exp,
                                     bias=neg_max[:, p * T + t:p * T + t + 1], scale=1.0,
                                     accum_out=row_sum[:, p * T + t:p * T + t + 1]).then_inc(exp_ready, 1)

            def hi_of(b, p, g, first):
                act.wait_ge(turn_ready, b * 8 + g + 1)
                if not first and g % T == 0:
                    act.wait_ge(ctx_ready, b * T - T)
                dst = (xth if g < T else pth)[:, p, :, (g % T) * P:(g % T + 1) * P]
                nc.scalar.copy(dst, blocks_of(turned[g % 2][:, :])).then_inc(hi_ready, 1)

            def norm(b, t):
                if t == 0:
                    act.wait_ge(oscales, b + 1)
                act.wait_ge(added, b * T + t + 1)
                nc.scalar.activation(normed[:, t % 2, :], context[t][:, :], ACT.Identity,
                                     bias=oshift[:, t:t + 1], scale=ors[:, t:t + 1]).then_inc(ctx_normed, 1)

            def body(b, p, first, last):
                for t in range(T):
                    exp(b, p, t)
                for g in range(2 * T):
                    hi_of(b, p, g, first)
                if not first:
                    for t in range(T):
                        norm(b - 1, t)

            over_batches(act, body)
            for t in range(T):
                norm(B - 1, t)

        @block.vector
        def _(dve):
            def stats_of(b, p):
                n = b // 2 if isinstance(b, int) else None
                dve.wait_ge(x_loaded[p], (b - p) * 8 + 16)
                for t in range(T):
                    last = nc.vector.bn_stats(bn[:, t, :], tile_of(s.x, b * T + t))
                last.then_inc(own_bn, 1)
                wait_alone(dve, s, own_bn, b + 1)
                for t in range(T):
                    last = nc.vector.bn_aggr(mv[:, t, :], bn[:, t, :])
                last.then_inc(stats, 1)

            def normalised(b, p):
                dve.wait_ge(scales, b + 1)
                for t in range(T):
                    nc.vector.tensor_scalar(xn[:, p, t, :], tile_of(s.x, b * T + t), mv[:, t, 0:1],
                                            rs[:, t:t + 1], ALU.subtract, ALU.mult).then_inc(xn_ready, 1)
                for t in range(T):
                    dve.wait_ge(xn_ready, b * T + t + 1)
                    nc.vector.tensor_copy(xh[:, p, t, :], xn[:, p, t, :]).then_inc(xh_ready, 1)

            def maximum(b, p, t):
                dve.wait_ge(scored, b * T + t + 1)
                nc.vector.reduce_max(neg_max[:, p * T + t:p * T + t + 1], score[t % 2][:, :], AX,
                                     negate=True).then_inc(max_ready, 1)

            def inverse(b, p, t):
                dve.wait_ge(exp_ready, b * T + t + 1)
                nc.vector.reciprocal(inv_sum[:, p * T + t:p * T + t + 1],
                                     row_sum[:, p * T + t:p * T + t + 1]).then_inc(inv_ready, 1)

            def lo_of(b, p, g):
                dve.wait_ge(hi_ready, b * 8 + g + 1)
                at = slice((g % T) * P, (g % T + 1) * P)
                hi, lo = ((xth, xtl) if g < T else (pth, ptl))
                nc.vector.tensor_tensor(lo[:, p, :, at], blocks_of(turned[g % 2][:, :]),
                                        hi[:, p, :, at].bitcast(F32), ALU.subtract).then_inc(lo_ready, 1)

            def output_stats(b, t):
                dve.wait_ge(ctx_ready, b * T + t + 1)
                last = nc.vector.bn_stats(obn[:, t, :], context[t][:, :])
                if t == T - 1:
                    last.then_inc(own_obn, 1)
                    wait_alone(dve, s, own_obn, b + 1)
                    for t in range(T):
                        last = nc.vector.bn_aggr(omv[:, t, :], obn[:, t, :])
                    last.then_inc(ostats, 1)

            stats_of(0, 0)
            normalised(0, 0)

            def body(b, p, first, last):
                maximum(b, p, 0)
                inverse(b, p, 0)
                if not last:
                    stats_of(b + 1, 1 - p)
                maximum(b, p, 1)
                inverse(b, p, 1)
                maximum(b, p, 2)
                inverse(b, p, 2)
                if not last:
                    normalised(b + 1, 1 - p)
                maximum(b, p, 3)
                inverse(b, p, 3)
                if first:
                    for g in range(2 * T):
                        lo_of(b, p, g)
                else:
                    output_stats(b - 1, 0)
                    lo_of(b, p, 0)
                    lo_of(b, p, 1)
                    dve.wait_ge(factor_loaded, b * 16 + 16)
                    output_stats(b - 1, 1)
                    lo_of(b, p, 2)
                    lo_of(b, p, 3)
                    output_stats(b - 1, 2)
                    lo_of(b, p, 4)
                    lo_of(b, p, 5)
                    output_stats(b - 1, 3)
                    lo_of(b, p, 6)
                    lo_of(b, p, 7)
                    dve.wait_ge(factor_used, b)
                    nc.vector.tensor_tensor(s.factor_sum[:, :, :], s.factor_sum[:, :, :], factor[:, :, :],
                                            ALU.add).then_inc(factor_used, 1)
                if first:
                    dve.wait_ge(factor_loaded, 16)
                    dve.sem_inc(factor_used, 1)

            over_batches(dve, body)
            for t in range(T):
                output_stats(B - 1, t)

        @block.tensor
        def _(pe):
            def scores(b, p, t, first):
                if t == 0:
                    pe.wait_ge(xh_ready, (b + 1) * T)
                    pe.wait_ge(xl_ready, (b + 1) * T)
                if not (first and t < 2):
                    pe.wait_ge(exp_ready, b * T + t - 1)
                at = slice(t * P, (t + 1) * P)
                products(nc, score[t % 2][:, :],
                         [(l[:, p, k, at], r[:, p, k, :])
                          for k in range(T) for l, r in ((xh, xh), (xl, xh), (xh, xl))]).then_inc(scored, 1)

            def turn(b, p, g, first):
                if g < T:
                    pe.wait_ge(xn_ready, b * T + g + 1)
                else:
                    pe.wait_ge(prob_ready, b * T + g - T + 1)
                if not (first and g < 2):
                    pe.wait_ge(lo_ready, b * 8 + g - 1)
                for k in range(T):
                    at = slice(k * P, (k + 1) * P)
                    src = xn[:, p, g, at] if g < T else prob[:, g - T, at]
                    last = nc.tensor.transpose(turned[g % 2][:, at], src, s.identity[:, :])
                last.then_inc(turn_ready, 1)

            def contexts(b, p, t):
                if t == 0:
                    pe.wait_ge(lo_ready, (b + 1) * 8)
                pe.wait_ge(ctx_normed, b * T + t + 1)
                at = slice(t * P, (t + 1) * P)
                products(nc, context[t][:, :],
                         [(l[:, p, k, at], r[:, p, k, :])
                          for k in range(T) for l, r in ((xth, pth), (xtl, pth), (xth, ptl))]).then_inc(ctx_ready, 1)

            def body(b, p, first, last):
                for t in range(T):
                    scores(b, p, t, first)
                for t in range(T):
                    if not first:
                        contexts(b - 1, 1 - p, t)
                    turn(b, p, 2 * t, first)
                    turn(b, p, 2 * t + 1, first)

            over_batches(pe, body)
            for t in range(T):
                contexts(B - 1, (B - 1) % 2, t)


def linear_map(nc, s, bias, x_out):
    with ExitStack() as ctx:
        def sb(name, shape, dt=F32):
            return ctx.enter_context(nc.sbuf_tensor(name, shape, dt))

        def sem(name):
            return s.stack.enter_context(nc.semaphore("f0_" + name))

        mh = sb("mh", [P, T, N], F32R)
        ml = sb("ml", [P, T, N], F32R)
        bias_rows = sb("bias_rows", [P, N])
        xn = sb("xn2", [P, 2, T, N])
        xth = sb("xth2", [P, 2, T, N], F32R)
        xtl = sb("xtl2", [P, 2, T, N], F32R)
        mixed = sb("mixed", [P, T, N])
        normed = sb("normed2", [P, 2, N])
        bn = sb("bn2", [P, T, 6])
        mv = sb("mv2", [P, T, 2])
        ve = sb("ve2", [P, T])
        rs = sb("rs2", [P, T])
        shift = sb("shift2", [P, T])
        obn = sb("obn2", [P, T, 6])
        omv = sb("omv2", [P, T, 2])
        ove = sb("ove2", [P, T])
        ors = sb("ors2", [P, T])
        oshift = sb("oshift2", [P, T])
        turned = [ctx.enter_context(nc.psum_tensor(f"turned2_{i}", [P, N], F32)) for i in range(2)]
        mix = [ctx.enter_context(nc.psum_tensor(f"mix{i}", [P, N], F32)) for i in range(T)]

        bias_loaded, weights = sem("bias_loaded"), sem("weights")
        own_bn, stats = sem("own_bn"), sem("stats")
        pool_step, scales = sem("pool_step"), sem("scales")
        xn_ready, turn_ready, hi_ready, lo_ready = (
            sem("xn_ready"), sem("turn_ready"), sem("hi_ready"), sem("lo_ready"))
        mix_ready, mixed_ready, own_obn, ostats, opool, oscales = (
            sem("mix_ready"), sem("mixed_ready"), sem("own_obn"), sem("ostats"), sem("opool"), sem("oscales"))
        normed_ready, added = sem("normed_ready"), sem("added")
        stored = sem("stored")

        block = ctx.enter_context(nc.Block())

        @block.sync
        def _(sp):
            sp.dma_start(bias_rows[:, :], bias.partition_broadcast(P)).then_inc(bias_loaded, 16)

            def store(b, p, first, last):
                sp.wait_ge(added, (b + 1) * T + 2)
                src = s.x[:, b * T:(b + 1) * T, :] if isinstance(b, int) else s.x[:, bass.ds(b * T, T), :]
                sp.dma_start(rows_of(x_out, b), src).then_inc(stored, 16)

            over_batches(sp, store)
            sp.wait_ge(stored, B * 16)

        @block.gpsimd
        def _(pool):
            pool.sem_inc(added, 2)

            def scales_of(b):
                if not (isinstance(b, int) and b == 0):
                    pool.wait_ge(xn_ready, b * T)
                wait_alone(pool, s, stats, b + 1)
                row_scales(nc, s, pool, mv, ve[:, :], rs[:, :], shift[:, :], s.minus_half[:, :],
                           pool_step, b * 2).then_inc(scales, 1)

            def output(b):
                wait_alone(pool, s, ostats, b + 1)
                row_scales(nc, s, pool, omv, ove[:, :], ors[:, :], oshift[:, :], s.minus_half[:, :],
                           opool, b * 2).then_inc(oscales, 1)
                for t in range(T):
                    pool.wait_ge(normed_ready, b * T + t + 1 + T)
                    x = tile_of(s.x, b * T + t)
                    nc.gpsimd.tensor_tensor(x, x, normed[:, t % 2, :], ALU.add).then_inc(added, 1)

            scales_of(0)

            def body(b, p, first, last):
                if not last:
                    scales_of(b + 1)
                if not first:
                    output(b - 1)

            over_batches(pool, body)
            output(B - 1)

        @block.scalar
        def _(act):
            act.sem_inc(normed_ready, T)

            def normalised(b, p):
                act.wait_ge(scales, b + 1)
                if not (isinstance(b, int) and b < 2):
                    act.wait_ge(turn_ready, (b - 1) * T)
                for t in range(T):
                    nc.scalar.activation(xn[:, p, t, :], tile_of(s.x, b * T + t), ACT.Identity,
                                         bias=shift[:, t:t + 1], scale=rs[:, t:t + 1]).then_inc(xn_ready, 1)

            def hi_of(b, p, t, first):
                act.wait_ge(turn_ready, b * T + t + 1)
                if not first and t == 0:
                    act.wait_ge(mix_ready, b * T - T)
                nc.scalar.copy(xth[:, p, :, t * P:(t + 1) * P],
                               blocks_of(turned[t % 2][:, :])).then_inc(hi_ready, 1)

            def norm(b, t):
                if t == 0:
                    act.wait_ge(oscales, b + 1)
                act.wait_ge(added, b * T + t + 1)
                nc.scalar.activation(normed[:, t % 2, :], mixed[:, t, :], ACT.Identity,
                                     bias=oshift[:, t:t + 1], scale=ors[:, t:t + 1]).then_inc(normed_ready, 1)

            nc.scalar.copy(mh[:, :, :], s.factor_sum[:, :, :]).then_inc(weights, 1)
            normalised(0, 0)

            def body(b, p, first, last):
                for t in range(T):
                    hi_of(b, p, t, first)
                if not last:
                    normalised(b + 1, 1 - p)
                if not first:
                    for t in range(T):
                        norm(b - 1, t)

            over_batches(act, body)
            for t in range(T):
                norm(B - 1, t)

        @block.vector
        def _(dve):
            def stats_of(b, p):
                if not (isinstance(b, int) and b == 0):
                    dve.wait_ge(stats, b)
                for t in range(T):
                    last = nc.vector.bn_stats(bn[:, t, :], tile_of(s.x, b * T + t))
                last.then_inc(own_bn, 1)
                if not (isinstance(b, int) and b == 0):
                    dve.wait_ge(scales, b)
                wait_alone(dve, s, own_bn, b + 1)
                for t in range(T):
                    last = nc.vector.bn_aggr(mv[:, t, :], bn[:, t, :])
                last.then_inc(stats, 1)

            def lo_of(b, p, t):
                dve.wait_ge(hi_ready, b * T + t + 1)
                at = slice(t * P, (t + 1) * P)
                nc.vector.tensor_tensor(xtl[:, p, :, at], blocks_of(turned[t % 2][:, :]),
                                        xth[:, p, :, at].bitcast(F32), ALU.subtract).then_inc(lo_ready, 1)

            def mixed_of(b, t):
                if t == 0:
                    dve.wait_ge(bias_loaded, 16)
                dve.wait_ge(mix_ready, b * T + t + 1)
                dve.wait_ge(normed_ready, b * T + t + 1)
                nc.vector.scalar_tensor_tensor(out=mixed[:, t, :], in0=mix[t][:, :], scalar=RANK ** -0.5,
                                               in1=bias_rows[:, :], op0=ALU.mult, op1=ALU.add).then_inc(mixed_ready, 1)

            def output_stats(b):
                for t in range(T):
                    dve.wait_ge(mixed_ready, b * T + t + 1 + T)
                    last = nc.vector.bn_stats(obn[:, t, :], mixed[:, t, :])
                last.then_inc(own_obn, 1)
                wait_alone(dve, s, own_obn, b + 1)
                for t in range(T):
                    last = nc.vector.bn_aggr(omv[:, t, :], obn[:, t, :])
                last.then_inc(ostats, 1)

            dve.sem_inc(mixed_ready, T)
            stats_of(0, 0)
            dve.wait_ge(weights, 1)
            nc.vector.tensor_tensor(ml[:, :, :], s.factor_sum[:, :, :], mh[:, :, :].bitcast(F32),
                                    ALU.subtract).then_inc(weights, 1)

            def body(b, p, first, last):
                if not last:
                    stats_of(b + 1, 1 - p)
                for t in range(T):
                    if not first:
                        mixed_of(b - 1, t)
                    lo_of(b, p, t)
                if not first:
                    output_stats(b - 1)

            over_batches(dve, body)
            for t in range(T):
                mixed_of(B - 1, t)
            output_stats(B - 1)

        @block.tensor
        def _(pe):
            def turn(b, p, t, first):
                pe.wait_ge(xn_ready, b * T + t + 1)
                if not (first and t < 2):
                    pe.wait_ge(lo_ready, b * T + t - 1)
                for k in range(T):
                    at = slice(k * P, (k + 1) * P)
                    last = nc.tensor.transpose(turned[t % 2][:, at], xn[:, p, t, at], s.identity[:, :])
                last.then_inc(turn_ready, 1)

            def mixes(b, p, t):
                if t == 0:
                    pe.wait_ge(weights, 2)
                    pe.wait_ge(lo_ready, (b + 1) * T)
                pe.wait_ge(mixed_ready, b * T + t + 1)
                at = slice(t * P, (t + 1) * P)
                products(nc, mix[t][:, :],
                         [(l[:, p, k, at], r[:, k, :])
                          for k in range(T) for l, r in ((xth, mh), (xtl, mh), (xth, ml))]).then_inc(mix_ready, 1)

            def body(b, p, first, last):
                for t in range(T):
                    if not first:
                        mixes(b - 1, 1 - p, t)
                    turn(b, p, t, first)

            over_batches(pe, body)
            for t in range(T):
                mixes(B - 1, (B - 1) % 2, t)


def prepare(nc, s):
    s.identity = s.stack.enter_context(nc.sbuf_tensor("identity", [P, P], F32))
    s.minus_half = s.stack.enter_context(nc.sbuf_tensor("minus_half", [P, T], F32))
    s.minus_one = s.stack.enter_context(nc.sbuf_tensor("minus_one", [P, T], F32))
    s.eps_rms = s.stack.enter_context(nc.sbuf_tensor("eps_rms", [P, T], F32))
    s.plus_half = s.stack.enter_context(nc.sbuf_tensor("plus_half", [P, T], F32))
    s.waits_passed = s.stack.enter_context(nc.semaphore("waits_passed"))
    zeroed = s.stack.enter_context(nc.semaphore("identity_zeroed"))
    with nc.Block() as block:
        @block.gpsimd
        def _(pool):
            nc.gpsimd.memset(s.minus_half[:, :], -0.5)
            nc.gpsimd.memset(s.plus_half[:, :], 0.5)
            nc.gpsimd.memset(s.minus_one[:, :], -1.0)
            nc.gpsimd.memset(s.eps_rms[:, :], EPS_RMS)
            nc.gpsimd.memset(s.identity[:, :], 0.0).then_inc(zeroed, 1)
            pool.wait_ge(zeroed, 1)
            nc.gpsimd.affine_select(out=s.identity[:, :], in_=s.identity[:, :], compare_op=ALU.not_equal,
                                    fill=1.0, base=0, pattern=[[-1, P]], channel_multiplier=1)


HALF = (slice(0, DH), slice(DH, P))
UNITS = HEADS * T
TURN_LAG = 3
OUT_LAG = 8
SIDE = 14
Q_AT = {2: 1, 6: 2, 18: 3}
WO_AT = {9: 0, 11: 1, 13: 2, 14: 3}
H_AT = {26: 0, 27: 1, 28: 2, 29: 3}
SIDE_OF = {"k": 0, "q0": 1, "v": 2, "q1": 3, "q2": 4, "wo0": 5, "wo1": 6, "wo2": 7, "wo3": 8,
           "q3": 9, "h0": 10, "h1": 11, "h2": 12, "h3": 13}


def side_use(b, name):
    j = SIDE_OF[name]
    if isinstance(b, int) and b == 0 and j < 5:
        j += 4
    return b * SIDE + j, j % 2


def grouped_attention(nc, s, norm_scale, split_scale, wq_t, wk_t, wv_t, wo_t, x_in, x_out):
    with ExitStack() as ctx:
        def sb(name, shape, dt=F32):
            return ctx.enter_context(nc.sbuf_tensor("g_" + name, shape, dt))

        def sem(name):
            return s.stack.enter_context(nc.semaphore("a1_" + name))

        def bank(name):
            return ctx.enter_context(nc.psum_tensor("g_" + name, [P, N], F32))

        KV = GROUPS * DH
        wqh, wql = sb("wqh", [P, T, N], F32R), sb("wql", [P, T, N], F32R)
        wkh, wkl = sb("wkh", [P, T, KV], F32R), sb("wkl", [P, T, KV], F32R)
        wvh, wvl = sb("wvh", [P, T, KV], F32R), sb("wvl", [P, T, KV], F32R)
        woh, wol = sb("woh", [P, T, N], F32R), sb("wol", [P, T, N], F32R)
        feature = sb("feature", [P, 3, T])
        x = sb("x", [P, 2, T, N])
        res = sb("res", [P, T, N])
        h = sb("h", [P, T, N])
        hth, htl = sb("hth", [P, T, N], F32R), sb("htl", [P, T, N], F32R)
        q = sb("q", [P, HEADS, N], F32R)
        kh, kl = sb("kh", [P, GROUPS, N], F32R), sb("kl", [P, GROUPS, N], F32R)
        v = sb("v", [P, 2, T, GROUPS, 2 * DH], F32R)
        prob = sb("prob", [P, T, N])
        pth, ptl = sb("pth", [P, 2, T, N], F32R), sb("ptl", [P, 2, T, N], F32R)
        v_lo_part = sb("v_lo_part", [DH, 2, N])
        out_sum = sb("out_sum", [P, 2, N])
        oh, ol = sb("oh", [P, T, N], F32R), sb("ol", [P, T, N], F32R)
        xn = sb("xn", [P, 2, N])
        total = sb("total", [P, T, N])
        normed = sb("normed", [P, 2, N])
        bn, mv = sb("bn", [P, T, 6]), sb("mv", [P, T, 2])
        ve, rs, shift = sb("ve", [P, T]), sb("rs", [P, 2, T]), sb("shift", [P, 2, T])
        root, rms, inv_rms = sb("root", [P, T]), sb("rms", [P, T]), sb("inv_rms", [P, T])
        hs, hshift = sb("hs", [P, T]), sb("hshift", [P, T])
        obn, omv = sb("obn", [P, T, 6]), sb("omv", [P, T, 2])
        ove, ors, oshift = sb("ove", [P, T]), sb("ors", [P, T]), sb("oshift", [P, T])
        neg_max, row_sum, inv_sum = sb("neg_max", [P, 4]), sb("row_sum", [P, 4]), sb("inv_sum", [P, 4])

        score = [bank("score0"), bank("score1")]
        turned = [bank("turned0"), bank("turned1")]
        output = [bank("output0"), bank("output1")]
        side = [bank("side0"), bank("side1")]

        w_loaded, scaled, w_ready = sem("w_loaded"), sem("scaled"), sem("w_ready")
        scaled_step = sem("scaled_step")
        x_loaded = [sem("x_loaded0"), sem("x_loaded1")]
        res_loaded, stored = sem("res_loaded"), sem("stored")
        own_bn, stats, pool_step, scales = sem("own_bn"), sem("stats"), sem("pool_step"), sem("scales")
        h_ready = sem("h_ready")
        side_ready, side_hi, side_free = sem("side_ready"), sem("side_hi"), sem("side_free")
        scored, max_ready, exp_ready = sem("scored"), sem("max_ready"), sem("exp_ready")
        inv_ready, prob_ready = sem("inv_ready"), sem("prob_ready")
        turn_ready, hi_ready, lo_ready = sem("turn_ready"), sem("hi_ready"), sem("lo_ready")
        out_ready, part_ready, sum_ready = sem("out_ready"), sem("part_ready"), sem("sum_ready")
        oh_ready, ol_ready = sem("oh_ready"), sem("ol_ready")
        xn_ready, total_ready = sem("xn_ready"), sem("total_ready")
        ostats, opool, oscales = sem("ostats"), sem("opool"), sem("oscales")
        normed_ready, added = sem("normed_ready"), sem("added")

        block = ctx.enter_context(nc.Block())

        def is_first(b):
            return isinstance(b, int) and b == 0

        @block.sync
        def _(sp):
            sp.dma_start(x[:, 0, :, :], rows_of(x_in, 0)).then_inc(x_loaded[0], 16)
            for dst, src in ((prob[:, :, :], wq_t.rearrange("(k p) n -> p k n", p=P)),
                             (total[:, :, :], wo_t.rearrange("(k p) n -> p k n", p=P)),
                             (out_sum[:, 0, :].rearrange("p (k n) -> p k n", k=T), wk_t.rearrange("(k p) n -> p k n", p=P)),
                             (out_sum[:, 1, :].rearrange("p (k n) -> p k n", k=T), wv_t.rearrange("(k p) n -> p k n", p=P)),
                             (feature[:, 0, :], norm_scale), (feature[:, 1, :], split_scale)):
                sp.dma_start(dst, src).then_inc(w_loaded, 16)

            def store(b):
                sp.wait_ge(added, (b + 1) * T + 2)
                sp.dma_start(rows_of(x_out, b), res[:, :, :]).then_inc(stored, 16)

            def body(b, p, first, last):
                if not last:
                    if not first:
                        sp.wait_ge(h_ready, b * T)
                        sp.wait_ge(x_loaded[1 - p], (b + 1 - (1 - p)) * 8)
                    sp.dma_start(x[:, 1 - p, :, :], rows_of(x_in, b + 1)).then_inc(x_loaded[1 - p], 16)
                if not first:
                    sp.wait_ge(stored, b * 16 - 16)
                    sp.dma_start(res[:, :, :], rows_of(x_in, b - 1)).then_inc(res_loaded, 16)
                    store(b - 1)

            over_batches(sp, body)
            sp.wait_ge(stored, B * 16 - 16)
            sp.dma_start(res[:, :, :], rows_of(x_in, B - 1)).then_inc(res_loaded, 16)
            store(B - 1)
            sp.wait_ge(stored, B * 16)

        @block.gpsimd
        def _(pool):
            pool.sem_inc(added, 2)

            def scales_of(b, p, part):
                at = b * 7
                if part == 0:
                    if not is_first(b):
                        pool.wait_ge(h_ready, b * T)
                    wait_alone(pool, s, stats, b + 1)
                    row_scales(nc, s, pool, mv, ve[:, :], rs[:, p, :], shift[:, p, :], s.minus_half[:, :],
                               pool_step, at)
                elif part == 1:
                    nc.gpsimd.tensor_tensor(root[:, :], mv[:, :, 1], s.plus_half[:, :],
                                            ALU.pow).then_inc(pool_step, 1)
                    pool.wait_ge(pool_step, at + 3)
                    nc.gpsimd.tensor_tensor(rms[:, :], root[:, :], rs[:, p, :], ALU.mult).then_inc(pool_step, 1)
                    pool.wait_ge(pool_step, at + 4)
                    nc.gpsimd.tensor_tensor(rms[:, :], rms[:, :], s.eps_rms[:, :], ALU.add).then_inc(pool_step, 1)
                else:
                    pool.wait_ge(pool_step, at + 5)
                    nc.gpsimd.tensor_tensor(inv_rms[:, :], rms[:, :], s.minus_one[:, :],
                                            ALU.pow).then_inc(pool_step, 1)
                    pool.wait_ge(pool_step, at + 6)
                    nc.gpsimd.tensor_tensor(hs[:, :], rs[:, p, :], inv_rms[:, :], ALU.mult).then_inc(pool_step, 1)
                    nc.gpsimd.tensor_tensor(hshift[:, :], shift[:, p, :], inv_rms[:, :],
                                            ALU.mult).then_inc(scales, 1)

            def normalise(g, u):
                wait_alone(pool, s, inv_ready, g + 1)
                at = u % 4
                nc.gpsimd.tensor_scalar(prob[:, at, :], prob[:, at, :], inv_sum[:, at:at + 1],
                                        1.0, ALU.mult, ALU.mult).then_inc(prob_ready, 1)

            def lo_of_output(b, m):
                pool.wait_ge(oh_ready, b * T + m + 1)
                nc.gpsimd.tensor_tensor(ol[:, m, :], out_sum[:, m % 2, :], oh[:, m, :].bitcast(F32),
                                        ALU.subtract).then_inc(ol_ready, 1)

            def residual(b, p, t):
                if t == 0:
                    pool.wait_ge(res_loaded, b * 16 + 16)
                pool.wait_ge(total_ready, b * T + t + 1)
                pool.wait_ge(scales, b + 1)
                pool.sem_inc(s.waits_passed, 1)
                nc.gpsimd.tensor_scalar(xn[:, t % 2, :], res[:, t, :], rs[:, p, t:t + 1],
                                        shift[:, p, t:t + 1], ALU.mult, ALU.add).then_inc(xn_ready, 1)

            def output_scales(b):
                wait_alone(pool, s, ostats, b + 1)
                row_scales(nc, s, pool, omv, ove[:, :], ors[:, :], oshift[:, :], s.minus_half[:, :],
                           opool, b * 2).then_inc(oscales, 1)

            def add(b, t):
                pool.wait_ge(normed_ready, b * T + t + 1 + T)
                nc.gpsimd.tensor_tensor(res[:, t, :], res[:, t, :], normed[:, t % 2, :],
                                        ALU.add).then_inc(added, 1)

            for part in range(3):
                scales_of(0, 0, part)

            def step(b, p, u, first, last, drain):
                if u > 0 or not first:
                    if not drain or u == 0:
                        normalise(b * UNITS + u - 1, u + 3)
                done = u - OUT_LAG - T
                if done % (2 * T) == T and not (first and done < 0) and not (drain and done >= 0):
                    pair = done // (2 * T)
                    lo_of_output(b + (-1 if pair < 0 else 0), pair % T)
                if u in WO_AT and not first:
                    residual(b - 1, 1 - p, WO_AT[u])
                if u == 16 and not first:
                    output_scales(b - 1)
                if u in (19, 20, 21, 22) and not first:
                    add(b - 1, u - 19)
                if u in (21, 22, 23) and not last and not drain:
                    scales_of(b + 1, 1 - p, u - 21)

            def body(b, p, first, last):
                for u in range(UNITS):
                    step(b, p, u, first, last, False)

            over_batches(pool, body)
            for u in range(23):
                step(B, 0, u, False, True, True)

        @block.scalar
        def _(act):
            act.sem_inc(normed_ready, T)

            def h_of(b, p, t):
                if t == 0:
                    act.wait_ge(scales, b + 1)
                    if not is_first(b):
                        act.wait_ge(side_ready, b * SIDE - SIDE + 4)
                nc.scalar.activation(h[:, t, :], x[:, p, t, :], ACT.Identity, bias=hshift[:, t:t + 1],
                                     scale=hs[:, t:t + 1]).then_inc(h_ready, 1)

            def hi_of_h(use, at, t):
                act.wait_ge(side_ready, use + 1)
                nc.scalar.copy(hth[:, :, t * P:(t + 1) * P], blocks_of(side[at][:, :])).then_inc(side_hi, 1)

            def hi_of_q(b, m):
                use, at = side_use(b, f"q{m}")
                act.wait_ge(side_ready, use + 1)
                for e, half in enumerate(HALF):
                    last = nc.scalar.copy(q[half, 2 * m + e, :], side[at][half, :])
                last.then_inc(side_hi, 1)

            def hi_of_k(b):
                use, at = side_use(b, "k")
                act.wait_ge(side_ready, use + 1)
                for g in range(GROUPS):
                    for half in HALF:
                        last = nc.scalar.copy(kh[half, g, :], side[at][HALF[g], :])
                last.then_inc(side_hi, 1)

            def hi_of_v(b, p):
                use, at = side_use(b, "v")
                act.wait_ge(side_ready, use + 1)
                src = side[at][:, :].rearrange("p (t g d) -> p t g d", t=T, g=GROUPS)
                nc.scalar.copy(v[:, p, :, :, 0:DH], src).then_inc(side_hi, 1)

            def exp(g, u, first):
                act.wait_ge(max_ready, g + 1)
                if not (first and u < 4):
                    act.wait_ge(turn_ready, g - 3)
                at = u % 4
                nc.scalar.activation(prob[:, at, :], score[u % 2][:, :], ACT.Exp, bias=neg_max[:, at:at + 1],
                                     scale=1.0, accum_out=row_sum[:, at:at + 1]).then_inc(exp_ready, 1)

            def v_lo_of(head, hd):
                act.wait_ge(out_ready, head + 1)
                nc.scalar.copy(v_lo_part[:, hd % 2, :], output[hd % 2][HALF[1], :]).then_inc(part_ready, 1)

            def norm(b, t):
                if t == 0:
                    act.wait_ge(oscales, b + 1)
                act.wait_ge(added, b * T + t + 1)
                nc.scalar.activation(normed[:, t % 2, :], total[:, t, :], ACT.Identity,
                                     bias=oshift[:, t:t + 1], scale=ors[:, t:t + 1]).then_inc(normed_ready, 1)

            for t in range(T):
                h_of(0, 0, t)
            act.wait_ge(scaled, 1)
            nc.scalar.copy(wqh[:, :, :], prob[:, :, :])
            nc.scalar.copy(wkh[:, :, :], out_sum[:, 0, :].rearrange("p (k n) -> p k n", k=T))
            nc.scalar.copy(wvh[:, :, :], out_sum[:, 1, :].rearrange("p (k n) -> p k n", k=T))
            nc.scalar.copy(woh[:, :, :], total[:, :, :]).then_inc(w_ready, 1)
            for t in range(T):
                hi_of_h(t, t % 2, t)

            def step(b, p, u, first, last, drain):
                g = b * UNITS + u
                if not drain:
                    exp(g, u, first)
                done = u - OUT_LAG - (T - 1)
                if done % T == 0 and not (first and done < 0) and not (drain and done >= 0):
                    v_lo_of(b * HEADS + done // T, done // T)
                turn_u = u - TURN_LAG
                if not (first and turn_u < 0) and not (drain and turn_u >= 0):
                    if turn_u % T == 0 and not (first and turn_u < 2 * T):
                        act.wait_ge(out_ready, b * HEADS + turn_u // T - 1)
                    act.wait_ge(turn_ready, g - TURN_LAG + 1)
                    at = turn_u % T
                    nc.scalar.copy(pth[:, (turn_u // T) % 2, :, at * P:(at + 1) * P],
                                   blocks_of(turned[turn_u % 2][:, :])).then_inc(hi_ready, 1)
                if u in Q_AT and not drain:
                    hi_of_q(b, Q_AT[u])
                if u in (18, 19, 20, 21) and not first:
                    norm(b - 1, u - 18)
                if u in (24, 25, 26, 27) and not last and not drain:
                    h_of(b + 1, 1 - p, u - 24)
                if u in H_AT and not last and not drain:
                    hi_of_h(*side_use(b, f"h{H_AT[u]}"), H_AT[u])
            def body(b, p, first, last):
                hi_of_k(b)
                hi_of_q(b, 0)
                hi_of_v(b, p)
                for u in range(UNITS):
                    step(b, p, u, first, last, False)

            over_batches(act, body)
            for u in range(22):
                step(B, 0, u, False, True, True)

        @block.vector
        def _(dve):
            def stats_of(b, p, t):
                if t == 0:
                    dve.wait_ge(x_loaded[p], (b - p) * 8 + 16)
                    if not is_first(b):
                        dve.wait_ge(stats, b)
                last = nc.vector.bn_stats(bn[:, t, :], x[:, p, t, :])
                if t == T - 1:
                    last.then_inc(own_bn, 1)
                    if not is_first(b):
                        dve.wait_ge(scales, b)
                    wait_alone(dve, s, own_bn, b + 1)
                    for t in range(T):
                        last = nc.vector.bn_aggr(mv[:, t, :], bn[:, t, :])
                    last.then_inc(stats, 1)

            def lo_of_q(b, m):
                use, at = side_use(b, f"q{m}")
                dve.wait_ge(side_hi, hi_count(b, f"q{m}"))
                for e, half in enumerate(HALF):
                    last = nc.vector.tensor_tensor(q[HALF[1 - e], 2 * m + e, :], side[at][half, :],
                                                   q[half, 2 * m + e, :].bitcast(F32), ALU.subtract)
                last.then_inc(side_free, 1)

            def lo_of_k(b):
                use, at = side_use(b, "k")
                dve.wait_ge(side_hi, hi_count(b, "k"))
                for g in range(GROUPS):
                    for half in HALF:
                        last = nc.vector.tensor_tensor(kl[half, g, :], side[at][HALF[g], :],
                                                       kh[HALF[g], g, :].bitcast(F32), ALU.subtract)
                last.then_inc(side_free, 1)

            def lo_of_v(b, p):
                use, at = side_use(b, "v")
                dve.wait_ge(side_hi, hi_count(b, "v"))
                src = side[at][:, :].rearrange("p (t g d) -> p t g d", t=T, g=GROUPS)
                nc.vector.tensor_tensor(v[:, p, :, :, DH:], src, v[:, p, :, :, 0:DH].bitcast(F32),
                                        ALU.subtract).then_inc(side_free, 1)

            def total_of(b, use, at, t):
                dve.wait_ge(side_ready, use + 1)
                dve.wait_ge(xn_ready, b * T + t + 1)
                dve.wait_ge(normed_ready, b * T + t + 1)
                nc.vector.tensor_tensor(total[:, t, :], side[at][:, :], xn[:, t % 2, :],
                                        ALU.add).then_inc(total_ready, 1)
                dve.wait_ge(total_ready, b * T + t + 1 + 2)
                nc.vector.bn_stats(obn[:, t, :], total[:, t, :]).then_inc(side_free, 1)
                if t == T - 1:
                    wait_alone(dve, s, side_free, use + 1)
                    for t in range(T):
                        last = nc.vector.bn_aggr(omv[:, t, :], obn[:, t, :])
                    last.then_inc(ostats, 1)

            def sum_of(b, hd):
                dve.wait_ge(part_ready, b * HEADS + hd + 1)
                m = hd // 2
                if hd % 2 == 0 and not (is_first(b) and m < 2):
                    dve.wait_ge(ol_ready, b * T + m - 1)
                nc.vector.tensor_tensor(out_sum[HALF[hd % 2], m % 2, :], output[hd % 2][HALF[0], :],
                                        v_lo_part[:, hd % 2, :], ALU.add).then_inc(sum_ready, 1)

            def hi_of_output(head, b, m):
                dve.wait_ge(sum_ready, head + 1)
                nc.vector.tensor_copy(oh[:, m, :], out_sum[:, m % 2, :]).then_inc(oh_ready, 1)

            def hi_count(b, name):
                use, _ = side_use(b, name)
                if isinstance(b, int) and b == 0:
                    return use + 1
                done = T if SIDE_OF[name] > SIDE_OF["wo3"] else 0
                return b * (SIDE - T) + (SIDE_OF[name] + 1 + T - done)

            dve.sem_inc(total_ready, 2)
            for t in range(T):
                stats_of(0, 0, t)
            dve.wait_ge(w_loaded, 6 * 16)
            nc.vector.tensor_tensor(feature[:, 2, :], feature[:, 0, :], feature[:, 1, :],
                                    ALU.mult).then_inc(scaled_step, 1)
            dve.wait_ge(scaled_step, 1)
            raw_k = out_sum[:, 0, :].rearrange("p (k n) -> p k n", k=T)
            raw_v = out_sum[:, 1, :].rearrange("p (k n) -> p k n", k=T)
            for k in range(T):
                nc.vector.tensor_scalar(prob[:, k, :], prob[:, k, :], feature[:, 2, k:k + 1], DH ** -0.5,
                                        ALU.mult, ALU.mult)
                for w in (raw_k, raw_v):
                    last = nc.vector.tensor_scalar(w[:, k, :], w[:, k, :], feature[:, 2, k:k + 1], None, ALU.mult)
            last.then_inc(scaled, 1)
            dve.wait_ge(w_ready, 1)
            nc.vector.tensor_tensor(wql[:, :, :], prob[:, :, :], wqh[:, :, :].bitcast(F32), ALU.subtract)
            nc.vector.tensor_tensor(wkl[:, :, :], raw_k, wkh[:, :, :].bitcast(F32), ALU.subtract)
            nc.vector.tensor_tensor(wvl[:, :, :], raw_v, wvh[:, :, :].bitcast(F32), ALU.subtract)
            nc.vector.tensor_tensor(wol[:, :, :], total[:, :, :], woh[:, :, :].bitcast(F32),
                                    ALU.subtract).then_inc(w_ready, 1)
            for t in range(T):
                dve.wait_ge(side_hi, t + 1)
                cols = slice(t * P, (t + 1) * P)
                nc.vector.tensor_tensor(htl[:, :, cols], blocks_of(side[t % 2][:, :]),
                                        hth[:, :, cols].bitcast(F32), ALU.subtract).then_inc(side_free, 1)

            def step(b, p, u, first, last, drain):
                g = b * UNITS + u
                if not drain:
                    dve.wait_ge(scored, g + 1)
                    at = u % 4
                    nc.vector.reduce_max(neg_max[:, at:at + 1], score[u % 2][:, :], AX,
                                         negate=True).then_inc(max_ready, 1)
                if (u > 0 or not first) and (not drain or u == 0):
                    at = (u - 1) % 4
                    dve.wait_ge(exp_ready, g)
                    nc.vector.reciprocal(inv_sum[:, at:at + 1], row_sum[:, at:at + 1]).then_inc(inv_ready, 1)
                turn_u = u - TURN_LAG
                if not (first and turn_u < 0) and not (drain and turn_u >= 0):
                    dve.wait_ge(hi_ready, g - TURN_LAG + 1)
                    cols = slice(turn_u % T * P, (turn_u % T + 1) * P)
                    at = (turn_u // T) % 2
                    nc.vector.tensor_tensor(ptl[:, at, :, cols], blocks_of(turned[turn_u % 2][:, :]),
                                            pth[:, at, :, cols].bitcast(F32), ALU.subtract).then_inc(lo_ready, 1)
                done = u - OUT_LAG - (T - 1)
                if done % T == 0 and not (first and done < 0) and not (drain and done >= 0):
                    hd = done // T
                    sum_of(b, hd)
                    if hd % 2 == 1:
                        before = 1 if hd < 0 else 0
                        hi_of_output(b * HEADS + hd, b - before, (hd % HEADS) // 2)
                if u in Q_AT and not drain:
                    lo_of_q(b, Q_AT[u])
                if u in WO_AT and not first:
                    t = WO_AT[u]
                    if drain:
                        total_of(b - 1, (B - 1) * SIDE + SIDE_OF["h0"] + t, t % 2, t)
                    else:
                        total_of(b - 1, *side_use(b, f"wo{t}"), t)
                if u in (17, 18, 19, 20) and not last and not drain:
                    stats_of(b + 1, 1 - p, u - 17)
                if u in H_AT and not last and not drain:
                    t = H_AT[u]
                    use, at = side_use(b, f"h{t}")
                    dve.wait_ge(side_hi, hi_count(b, f"h{t}"))
                    cols = slice(t * P, (t + 1) * P)
                    nc.vector.tensor_tensor(htl[:, :, cols], blocks_of(side[at][:, :]),
                                            hth[:, :, cols].bitcast(F32), ALU.subtract).then_inc(side_free, 1)

            def body(b, p, first, last):
                lo_of_k(b)
                lo_of_q(b, 0)
                lo_of_v(b, p)
                for u in range(UNITS):
                    step(b, p, u, first, last, False)

            over_batches(dve, body)
            for u in range(15):
                step(B, 0, u, False, True, True)

        @block.tensor
        def _(pe):
            def side_bank(use):
                if not (isinstance(use, int) and use < 2):
                    pe.wait_ge(side_free, use - 1)
            def turn_h(b, use, at, t):
                side_bank(use)
                pe.wait_ge(h_ready, b * T + t + 1)
                for k in range(T):
                    cols = slice(k * P, (k + 1) * P)
                    last = nc.tensor.transpose(side[at][:, cols], h[:, t, cols], s.identity[:, :])
                last.then_inc(side_ready, 1)

            def split(lh, ll, rh, rl):
                return ((lh, rh), (ll, rh), (lh, rl))

            def q_of(b, m):
                use, at = side_use(b, f"q{m}")
                side_bank(use)
                cols = slice(m * P, (m + 1) * P)
                products(nc, side[at][:, :],
                         [pair for k in range(T)
                          for pair in split(wqh[:, k, cols], wql[:, k, cols], hth[:, k, :], htl[:, k, :])]
                         ).then_inc(side_ready, 1)

            def k_of(b):
                use, at = side_use(b, "k")
                side_bank(use)
                products(nc, side[at][:, :],
                         [pair for k in range(T)
                          for pair in split(wkh[:, k, :], wkl[:, k, :], hth[:, k, :], htl[:, k, :])]
                         ).then_inc(side_ready, 1)

            def v_of(b):
                use, at = side_use(b, "v")
                side_bank(use)
                for t in range(T):
                    cols = slice(t * P, (t + 1) * P)
                    last = products(nc, side[at][:, cols],
                                    [pair for k in range(T)
                                     for pair in split(hth[:, k, cols], htl[:, k, cols], wvh[:, k, :], wvl[:, k, :])])
                last.then_inc(side_ready, 1)

            def wo_of(b, use, at, t):
                side_bank(use)
                if t == 0:
                    pe.wait_ge(ol_ready, (b + 1) * T)
                cols = slice(t * P, (t + 1) * P)
                products(nc, side[at][:, :],
                         [pair for m in range(T)
                          for pair in split(oh[:, m, cols], ol[:, m, cols], woh[:, m, :], wol[:, m, :])]
                         ).then_inc(side_ready, 1)

            for t in range(T):
                turn_h(0, t, t % 2, t)
            pe.wait_ge(w_ready, 2)

            def step(b, p, u, first, last, drain):
                g = b * UNITS + u
                if not drain:
                    hd, row = u // T, u % T
                    if u % (2 * T) == 0:
                        pe.wait_ge(side_free, side_use(b, f"q{u // (2 * T)}")[0] + 1)
                    if not (first and u < 2):
                        pe.wait_ge(exp_ready, g - 1)
                    lhsT = q[:, hd, row * P:(row + 1) * P]
                    products(nc, score[u % 2][:, :], [(lhsT, kh[:, hd // HPG, :]), (lhsT, kl[:, hd // HPG, :])]
                             ).then_inc(scored, 1)
                out_u = u - OUT_LAG
                if not (first and out_u < 0) and not (drain and out_u >= 0):
                    hd, t = out_u // T, out_u % T
                    if t == 0:
                        pe.wait_ge(lo_ready, (b * HEADS + hd + 1) * T)
                        if hd % HEADS == 0:
                            pe.wait_ge(side_free, side_use(b, "v")[0] + 1)
                        if not (first and hd < 2):
                            pe.wait_ge(sum_ready, b * HEADS + hd - 1)
                    lhsT = v[:, p if out_u >= 0 else 1 - p, t, hd % HEADS // HPG, :]
                    nc.tensor.matmul(output[hd % 2][:, :], lhsT, pth[:, hd % 2, t, :], start=(t == 0), stop=False)
                    mm = nc.tensor.matmul(output[hd % 2][:, :], lhsT, ptl[:, hd % 2, t, :], start=False,
                                            stop=(t == T - 1))
                    if t == T - 1:
                        mm.then_inc(out_ready, 1)
                turn_u = u - TURN_LAG
                if not (first and turn_u < 0) and not (drain and turn_u >= 0):
                    pe.wait_ge(prob_ready, g - TURN_LAG + 1)
                    if not (first and turn_u < 2):
                        pe.wait_ge(lo_ready, g - TURN_LAG - 1)
                    for k in range(T):
                        cols = slice(k * P, (k + 1) * P)
                        mm = nc.tensor.transpose(turned[turn_u % 2][:, cols], prob[:, turn_u % 4, cols],
                                                   s.identity[:, :])
                    mm.then_inc(turn_ready, 1)
                if u in Q_AT and not drain:
                    q_of(b, Q_AT[u])
                if u in WO_AT and not first:
                    t = WO_AT[u]
                    if drain:
                        wo_of(b - 1, (B - 1) * SIDE + SIDE_OF["h0"] + t, t % 2, t)
                    else:
                        wo_of(b - 1, *side_use(b, f"wo{t}"), t)
                if u in H_AT and not last and not drain:
                    turn_h(b + 1, *side_use(b, f"h{H_AT[u]}"), H_AT[u])

            def body(b, p, first, last):
                pe.wait_ge(side_free, b * SIDE + (T if first else 0))
                k_of(b)
                q_of(b, 0)
                v_of(b)
                for u in range(UNITS):
                    step(b, p, u, first, last, False)

            over_batches(pe, body)
            for u in range(15):
                step(B, 0, u, False, True, True)


INNER_PAIRS = IT + T // 2


def turn_bank(p, t):
    return (p * INNER_PAIRS + t // 2) % 2 * 2 + t % 2


def pair_at(p, i):
    return (p * INNER_PAIRS + T // 2 + i) % 2 * 2


def gated_ffn(nc, s, gate_t, up_t, down_t, gate_s, up_s, down_s, x_in, out):
    with ExitStack() as ctx:
        def sb(name, shape, dt=F32):
            return ctx.enter_context(nc.sbuf_tensor("f_" + name, shape, dt))

        def sem(name):
            return s.stack.enter_context(nc.semaphore("f1_" + name))

        def bank(name):
            return ctx.enter_context(nc.psum_tensor("f_" + name, [P, N], F32))

        wh, wl = sb("wh", [P, IT, 3, N], F32R), sb("wl", [P, IT, 3, N], F32R)
        inner_scale = sb("inner_scale", [P, 2, IT])
        down_scale = sb("down_scale", [P, N])
        x = sb("x", [P, 2, T, N])
        xn = sb("xn", [P, T, N])
        xth, xtl = sb("xth", [P, T, N], F32R), sb("xtl", [P, T, N], F32R)
        silu = sb("silu", [P, 2, N])
        hidden = sb("hidden", [P, 2, N])
        hh, hl = sb("hh", [P, 2, N], F32R), sb("hl", [P, 2, N], F32R)
        y = sb("y", [P, T, N])
        bn, mv = sb("bn", [P, T, 6]), sb("mv", [P, T, 2])
        ve, rs, shift = sb("ve", [P, T]), sb("rs", [P, T]), sb("shift", [P, T])
        obn, omv = sb("obn", [P, T, 6]), sb("omv", [P, T, 2])
        ove, ors, oshift = sb("ove", [P, T]), sb("ors", [P, T]), sb("oshift", [P, T])
        inner = [bank(f"inner{i}") for i in range(4)]
        down = [bank(f"down{i}") for i in range(T)]
        raw = [y[:, 0:3, :], x[:, 1, 0:3, :]]

        raw_loaded = [sem("raw_loaded0"), sem("raw_loaded1")]
        scale_loaded, wh_ready, wl_ready = sem("scale_loaded"), sem("wh_ready"), sem("wl_ready")
        x_loaded, stored = [sem("x_loaded0"), sem("x_loaded1")], sem("stored")
        own_bn, stats, pool_step, scales = sem("own_bn"), sem("stats"), sem("pool_step"), sem("scales")
        xn_ready, turn_ready, th_ready, tl_ready = sem("xn_ready"), sem("turn_ready"), sem("th_ready"), sem("tl_ready")
        gate_ready, up_ready, silu_ready, hidden_ready = (
            sem("gate_ready"), sem("up_ready"), sem("silu_ready"), sem("hidden_ready"))
        hh_ready, hl_ready, down_used = sem("hh_ready"), sem("hl_ready"), sem("down_used")
        y_ready, own_obn, ostats, opool, oscales = (
            sem("y_ready"), sem("own_obn"), sem("ostats"), sem("opool"), sem("oscales"))
        normed, added = sem("normed"), sem("added")

        block = ctx.enter_context(nc.Block())

        def is_first(b):
            return isinstance(b, int) and b == 0

        @block.sync
        def _(sp):
            sp.dma_start(x[:, 0, :, :], rows_of(x_in, 0)).then_inc(x_loaded[0], 16)
            for dst, src in ((inner_scale[:, 0, :], gate_s), (inner_scale[:, 1, :], up_s),
                             (down_scale[:, :], down_s.partition_broadcast(P))):
                sp.dma_start(dst, src).then_inc(scale_loaded, 16)
            for i in range(IT):
                if i >= 2:
                    sp.wait_ge(wl_ready, i - 1)
                for j, src in enumerate((gate_t, up_t, down_t)):
                    sp.dma_start(raw[i % 2][:, j, :], src[i, :, :]).then_inc(raw_loaded[i % 2], 16)
            sp.wait_ge(wl_ready, IT)

            def store(b, p):
                sp.wait_ge(added, (b + 2) * T)
                sp.dma_start(rows_of(out, b), x[:, p, :, :]).then_inc(stored, 16)

            def body(b, p, first, last):
                if not first:
                    store(b - 1, 1 - p)
                if not last:
                    if not first:
                        sp.wait_ge(stored, b * 16)
                    sp.dma_start(x[:, 1 - p, :, :], rows_of(x_in, b + 1)).then_inc(x_loaded[1 - p], 16)

            over_batches(sp, body)
            store(B - 1, (B - 1) % 2)
            sp.wait_ge(stored, B * 16)

        @block.gpsimd
        def _(pool):
            def scales_of(b):
                if not is_first(b):
                    pool.wait_ge(xn_ready, b * T)
                wait_alone(pool, s, stats, b + 1)
                row_scales(nc, s, pool, mv, ve[:, :], rs[:, :], shift[:, :], s.minus_half[:, :],
                           pool_step, b * 2).then_inc(scales, 1)

            def lo_of_hidden(b, i, at):
                pool.wait_ge(hh_ready, b * IT + i + 1)
                nc.gpsimd.tensor_tensor(hl[:, at, :], hidden[:, at, :], hh[:, at, :].bitcast(F32),
                                        ALU.subtract).then_inc(hl_ready, 1)

            def output_scales(b):
                wait_alone(pool, s, ostats, b + 1)
                row_scales(nc, s, pool, omv, ove[:, :], ors[:, :], oshift[:, :], s.minus_half[:, :],
                           opool, b * 2).then_inc(oscales, 1)

            def add(b, p, t):
                pool.wait_ge(normed, b * T + t + 1)
                nc.gpsimd.tensor_tensor(x[:, p, t, :], x[:, p, t, :], y[:, t, :], ALU.add).then_inc(added, 1)

            pool.sem_inc(added, T)
            scales_of(0)

            def body(b, p, first, last):
                for i in range(IT):
                    if not first:
                        if i == 1:
                            output_scales(b - 1)
                        if 2 <= i < 2 + T:
                            add(b - 1, 1 - p, i - 2)
                    if i == 9 and not first and not last:
                        scales_of(b + 1)
                    lo_of_hidden(b, i, (i + p) % 2)
                if first:
                    scales_of(b + 1)

            over_batches(pool, body)
            output_scales(B - 1)
            for t in range(T):
                add(B - 1, (B - 1) % 2, t)

        @block.scalar
        def _(act):
            def normalised(b, p):
                act.wait_ge(scales, b + 1)
                if not is_first(b):
                    act.wait_ge(turn_ready, b * T)
                for t in range(T):
                    nc.scalar.activation(xn[:, t, :], x[:, p, t, :], ACT.Identity, bias=shift[:, t:t + 1],
                                         scale=rs[:, t:t + 1]).then_inc(xn_ready, 1)

            def hi_of_xt(b, t, bank_of):
                if t == 0 and not is_first(b):
                    act.wait_ge(up_ready, b * IT)
                act.wait_ge(turn_ready, b * T + t + 1)
                nc.scalar.copy(xth[:, :, t * P:(t + 1) * P],
                               blocks_of(inner[bank_of(t)][:, :])).then_inc(th_ready, 1)

            def silu_of(b, p, i, first):
                act.wait_ge(gate_ready, b * IT + i + 1)
                if not (first and i < 2):
                    act.wait_ge(hidden_ready, b * IT + i - 1)
                at = (i + p) % 2
                nc.scalar.activation(silu[:, at, :], inner[pair_at(p, i)][:, :], ACT.Silu,
                                     scale=inner_scale[:, 0, i:i + 1]).then_inc(silu_ready, 1)

            def norm(b, t):
                if t == 0:
                    act.wait_ge(oscales, b + 1)
                nc.scalar.activation(y[:, t, :], y[:, t, :], ACT.Identity, bias=oshift[:, t:t + 1],
                                     scale=ors[:, t:t + 1]).then_inc(normed, 1)

            normalised(0, 0)
            for t in range(T):
                hi_of_xt(0, t, lambda t: turn_bank(0, t))
            act.wait_ge(scale_loaded, 48)

            def body(b, p, first, last):
                for i in range(IT):
                    if first:
                        act.wait_ge(raw_loaded[i % 2], (i // 2 + 1) * 48)
                        nc.scalar.copy(wh[:, i, :, :], raw[i % 2]).then_inc(wh_ready, 1)
                    silu_of(b, p, i, first)
                    if 2 <= i < 2 + T and not first:
                        norm(b - 1, i - 2)
                if not last:
                    normalised(b + 1, 1 - p)
                    for t in range(T):
                        hi_of_xt(b + 1, t, lambda t: turn_bank(1 - p, t))

            over_batches(act, body)
            for t in range(T):
                norm(B - 1, t)

        @block.vector
        def _(dve):
            def stats_of(b, p):
                dve.wait_ge(x_loaded[p], (b - p) * 8 + 16)
                if not is_first(b):
                    dve.wait_ge(stats, b)
                for t in range(T):
                    last = nc.vector.bn_stats(bn[:, t, :], x[:, p, t, :])
                last.then_inc(own_bn, 1)
                if not is_first(b):
                    dve.wait_ge(scales, b)
                wait_alone(dve, s, own_bn, b + 1)
                for t in range(T):
                    last = nc.vector.bn_aggr(mv[:, t, :], bn[:, t, :])
                last.then_inc(stats, 1)

            def lo_of_xt(b, t, at):
                dve.wait_ge(th_ready, b * T + t + 1)
                cols = slice(t * P, (t + 1) * P)
                nc.vector.tensor_tensor(xtl[:, :, cols], blocks_of(inner[at][:, :]),
                                        xth[:, :, cols].bitcast(F32), ALU.subtract).then_inc(tl_ready, 1)

            def hidden_of(b, p, i, first):
                dve.wait_ge(up_ready, b * IT + i + 1)
                dve.wait_ge(silu_ready, b * IT + i + 1)
                if not (first and i < 2):
                    dve.wait_ge(hl_ready, b * IT + i - 1)
                at = (i + p) % 2
                nc.vector.scalar_tensor_tensor(out=hidden[:, at, :], in0=inner[pair_at(p, i) + 1][:, :],
                                               scalar=inner_scale[:, 1, i:i + 1], in1=silu[:, at, :],
                                               op0=ALU.mult, op1=ALU.mult).then_inc(hidden_ready, 1)
                if not (first and i < 2):
                    dve.wait_ge(down_used, b * IT + i - 1)
                dve.wait_ge(hidden_ready, b * IT + i + 1)
                nc.vector.tensor_copy(hh[:, at, :], hidden[:, at, :]).then_inc(hh_ready, 1)

            def y_of(b, t):
                dve.wait_ge(down_used, (b + 1) * IT)
                dve.wait_ge(added, b * T + t + 1)
                nc.vector.tensor_tensor(y[:, t, :], down[t][:, :], down_scale[:, :], ALU.mult).then_inc(y_ready, 1)

            def output_stats(b):
                for t in range(T):
                    dve.wait_ge(y_ready, b * T + t + 1)
                    last = nc.vector.bn_stats(obn[:, t, :], y[:, t, :])
                last.then_inc(own_obn, 1)
                wait_alone(dve, s, own_obn, b + 1)
                for t in range(T):
                    last = nc.vector.bn_aggr(omv[:, t, :], obn[:, t, :])
                last.then_inc(ostats, 1)

            stats_of(0, 0)
            for t in range(T):
                lo_of_xt(0, t, turn_bank(0, t))
            dve.wait_ge(scale_loaded, 48)

            def body(b, p, first, last):
                for i in range(IT):
                    if first:
                        dve.wait_ge(wh_ready, i + 1)
                        nc.vector.tensor_tensor(wl[:, i, :, :], raw[i % 2], wh[:, i, :, :].bitcast(F32),
                                                ALU.subtract).then_inc(wl_ready, 1)
                    if i == 0 and not first:
                        for t in range(T):
                            y_of(b - 1, t)
                    hidden_of(b, p, i, first)
                    if i == 0 and not first:
                        output_stats(b - 1)
                    if i == (IT - 1 if first else 8) and not last:
                        stats_of(b + 1, 1 - p)
                if not last:
                    for t in range(T):
                        lo_of_xt(b + 1, t, turn_bank(1 - p, t))

            over_batches(dve, body)
            for t in range(T):
                y_of(B - 1, t)
            output_stats(B - 1)

        @block.tensor
        def _(pe):
            def turn(b, p, t):
                pe.wait_ge(xn_ready, b * T + t + 1)
                if not is_first(b):
                    pe.wait_ge(hidden_ready, b * IT - 1 + t // 2)
                for k in range(T):
                    cols = slice(k * P, (k + 1) * P)
                    last = nc.tensor.transpose(inner[turn_bank(p, t)][:, cols], xn[:, t, cols], s.identity[:, :])
                last.then_inc(turn_ready, 1)

            def inner_of(b, p, i, first):
                if first:
                    pe.wait_ge(wl_ready, i + 1)
                if i == 0:
                    pe.wait_ge(tl_ready, (b + 1) * T)
                if i >= 2:
                    pe.wait_ge(hidden_ready, b * IT + i - 1)
                for j, done in ((0, gate_ready), (1, up_ready)):
                    pairs = []
                    for k in range(T):
                        cols = slice(k * P, (k + 1) * P)
                        pairs += [(wh[:, i, j, cols], xth[:, k, :]), (wl[:, i, j, cols], xth[:, k, :]),
                                  (wh[:, i, j, cols], xtl[:, k, :])]
                    products(nc, inner[pair_at(p, i) + j][:, :], pairs).then_inc(done, 1)

            def down_of(b, p, i, first):
                pe.wait_ge(hl_ready, b * IT + i + 1)
                if i == 0 and not first:
                    pe.wait_ge(y_ready, b * T)
                at = (i + p) % 2
                for t in range(T):
                    cols = slice(t * P, (t + 1) * P)
                    for n, (l, r) in enumerate(((hh, wh), (hl, wh), (hh, wl))):
                        last = nc.tensor.matmul(down[t][:, :], l[:, at, cols], r[:, i, 2, :],
                                                start=(i == 0 and n == 0), stop=(i == IT - 1 and n == 2))
                last.then_inc(down_used, 1)

            for t in range(T):
                turn(0, 0, t)

            def body(b, p, first, last):
                for i in range(IT):
                    inner_of(b, p, i, first)
                    if i > 0:
                        down_of(b, p, i - 1, first)
                if not last:
                    for t in range(T):
                        turn(b + 1, 1 - p, t)
                down_of(b, p, IT - 1, first)

            over_batches(pe, body)


def four_blocks(nc, x_in, factors, bias, norm_scale, split_scale, wq_t, wk_t, wv_t, wo_t,
                gate_t, up_t, down_t, gate_s, up_s, down_s, out):
    x_mixed = nc.dram_tensor("x_mixed", [B, N, N], F32).ap()
    x_attended = nc.dram_tensor("x_attended", [B, N, N], F32).ap()

    with ExitStack() as stack:
        s = Shared()
        s.stack = stack
        prepare(nc, s)
        with ExitStack() as resident:
            s.x = resident.enter_context(nc.sbuf_tensor("x_resident", [P, B * T, N], F32))
            s.factor_sum = resident.enter_context(nc.sbuf_tensor("factor_sum", [P, T, N], F32))
            column_attention(nc, s, x_in, factors)
            linear_map(nc, s, bias, x_mixed)
        grouped_attention(nc, s, norm_scale, split_scale, wq_t, wk_t, wv_t, wo_t, x_mixed, x_attended)
        gated_ffn(nc, s, gate_t, up_t, down_t, gate_s, up_s, down_s, x_attended, out)


def kernel(L0_attn_x, L0_ffn_factors, L0_ffn_bias, L1_attn_norm_scale, L1_attn_split_scale,
           L1_attn_Wq, L1_attn_Wk, L1_attn_Wv, L1_attn_Wo,
           L1_ffn_gate_w, L1_ffn_up_w, L1_ffn_down_w, L1_ffn_gate_s, L1_ffn_up_s, L1_ffn_down_s):
    import numpy as np
    import concourse.bacc as bacc
    from concourse.bass_utils import run_bass_kernel_spmd

    def per_partition(v):
        return v.reshape(-1, P).T

    def inner_tiles(w):
        return w.reshape(IT, P, T, P).transpose(0, 3, 2, 1).reshape(IT, P, N)

    arrays = {
        "x": L0_attn_x, "factors": L0_ffn_factors, "bias": L0_ffn_bias,
        "norm_scale": per_partition(L1_attn_norm_scale), "split_scale": per_partition(L1_attn_split_scale),
        "wq_t": L1_attn_Wq.T, "wk_t": L1_attn_Wk.T, "wv_t": L1_attn_Wv.T, "wo_t": L1_attn_Wo.T,
        "gate_t": inner_tiles(L1_ffn_gate_w), "up_t": inner_tiles(L1_ffn_up_w),
        "down_t": L1_ffn_down_w.T.reshape(IT, P, N),
        "gate_s": per_partition(L1_ffn_gate_s), "up_s": per_partition(L1_ffn_up_s), "down_s": L1_ffn_down_s,
    }
    arrays = {name: np.ascontiguousarray(a) for name, a in arrays.items()}
    nc = bacc.Bacc("TRN2", target_bir_lowering=False, num_devices=1)
    args = [nc.dram_tensor(name, a.shape, F32, kind="ExternalInput").ap() for name, a in arrays.items()]
    out = nc.dram_tensor("out", (B, N, N), F32, kind="ExternalOutput")
    four_blocks(nc, *args, out.ap())
    result = run_bass_kernel_spmd(nc, [arrays], core_ids=[0])
    return result.results[0]["out"]
```

```python
from contextlib import ExitStack

import concourse.bass as bass
from concourse import mybir

P = 128
B = 8
N = 512
T = N // P
HEADS = 8
GROUPS = 2
DH = 64
HPG = HEADS // GROUPS
INTER = 1408
IT = INTER // P
RANK = 8
EPS = 1e-5
EPS_RMS = 1e-8

F32 = mybir.dt.float32
F32R = mybir.dt.float32r
I32 = mybir.dt.int32
ALU = mybir.AluOpType
ACT = mybir.ActivationFunctionType
AX = mybir.AxisListType.X


def tile_of(t, i):
    if isinstance(i, int):
        return t[:, i, :]
    return t[:, bass.ds(i, 1), :].rearrange("p a n -> p (a n)")


def rows_of(dram, b):
    if isinstance(b, int):
        return dram[b, :, :].rearrange("(t p) n -> p t n", p=P)
    return dram[bass.ds(b, 1), :, :].rearrange("a (t p) n -> p (a t) n", p=P)


def blocks_of(row):
    return row.rearrange("p (t c) -> p t c", t=T)


def products(nc, out, pairs):
    for n, (lhsT, rhs) in enumerate(pairs):
        last = nc.tensor.matmul(out, lhsT, rhs, start=(n == 0), stop=(n == len(pairs) - 1))
    return last


def wait_alone(eng, s, sem, value):
    eng.wait_ge(sem, value)
    if not isinstance(value, int):
        eng.sem_inc(s.waits_passed, 1)


def over_batches(eng, body):
    body(0, 0, True, False)
    with eng.Fori(0, (B - 2) // 2) as i:
        body(i * 2 + 1, 1, False, False)
        body(i * 2 + 2, 0, False, False)
    body(B - 1, 1, False, True)


def over_batches_two_behind(eng, body):
    body(0, 0, 0, False)
    body(1, 1, 1, False)
    with eng.Fori(0, (B - 4) // 2) as i:
        body(i * 2 + 2, 0, 2, False)
        body(i * 2 + 3, 1, 2, False)
    body(B - 2, 0, 2, False)
    body(B - 1, 1, 2, True)


class Shared:
    pass


def row_scales(nc, s, pool, mv, ve, rs, shift, exponent, step, at):
    nc.gpsimd.tensor_scalar(ve, mv[:, :, 1], EPS, None, ALU.add)
    nc.gpsimd.tensor_scalar(shift, mv[:, :, 0], -1.0, None, ALU.mult).then_inc(step, 1)
    pool.wait_ge(step, at + 1)
    nc.gpsimd.tensor_tensor(rs, ve, exponent, ALU.pow).then_inc(step, 1)
    pool.wait_ge(step, at + 2)
    return nc.gpsimd.tensor_tensor(shift, shift, rs, ALU.mult)


def column_attention(nc, s, x_in, factors):
    with ExitStack() as ctx:
        def sb(name, shape, dt=F32):
            return ctx.enter_context(nc.sbuf_tensor(name, shape, dt))

        def sem(name):
            return s.stack.enter_context(nc.semaphore("a0_" + name))

        xn = sb("xn", [P, 2, T, N])
        xh = sb("xh", [P, 2, T, N], F32R)
        xl = sb("xl", [P, 2, T, N], F32R)
        xth = sb("xth", [P, 2, T, N], F32R)
        xtl = sb("xtl", [P, 2, T, N], F32R)
        pth = sb("pth", [P, 2, T, N], F32R)
        ptl = sb("ptl", [P, 2, T, N], F32R)
        prob = sb("prob", [P, T, N])
        normed = sb("normed", [P, 2, N])
        factor = sb("factor", [P, T, N])
        bn = sb("bn", [P, T, 6])
        mv = sb("mv", [P, T, 2])
        ve = sb("ve", [P, T])
        rs = sb("rs", [P, T])
        shift = sb("shift", [P, T])
        obn = sb("obn", [P, T, 6])
        omv = sb("omv", [P, T, 2])
        ove = sb("ove", [P, T])
        ors = sb("ors", [P, T])
        oshift = sb("oshift", [P, T])
        neg_max = sb("neg_max", [P, 2 * T])
        row_sum = sb("row_sum", [P, 2 * T])
        inv_sum = sb("inv_sum", [P, 2 * T])

        score = [ctx.enter_context(nc.psum_tensor(f"score{i}", [P, N], F32)) for i in range(2)]
        turned = [ctx.enter_context(nc.psum_tensor(f"turned{i}", [P, N], F32)) for i in range(2)]
        context = [ctx.enter_context(nc.psum_tensor(f"context{i}", [P, N], F32)) for i in range(T)]

        x_loaded = [sem("x_loaded0"), sem("x_loaded1")]
        factor_loaded, factor_used = sem("factor_loaded"), sem("factor_used")
        own_bn, stats = sem("own_bn"), sem("stats")
        pool_step, scales = sem("pool_step"), sem("scales")
        xn_ready, xh_ready, xl_ready = sem("xn_ready"), sem("xh_ready"), sem("xl_ready")
        scored, max_ready, exp_ready = sem("scored"), sem("max_ready"), sem("exp_ready")
        inv_ready, prob_ready = sem("inv_ready"), sem("prob_ready")
        turn_ready, hi_ready, lo_ready = sem("turn_ready"), sem("hi_ready"), sem("lo_ready")
        ctx_ready, own_obn, ostats, opool, oscales = (
            sem("ctx_ready"), sem("own_obn"), sem("ostats"), sem("opool"), sem("oscales"))
        ctx_normed, added = sem("ctx_normed"), sem("added")

        block = ctx.enter_context(nc.Block())

        @block.sync
        def _(sp):
            def load_x(b, p):
                dst = s.x[:, b * T:(b + 1) * T, :] if isinstance(b, int) else s.x[:, bass.ds(b * T, T), :]
                sp.dma_start(dst, rows_of(x_in, b)).then_inc(x_loaded[p], 16)

            load_x(0, 0)

            def load(b, p, first, last):
                if not last:
                    sp.wait_ge(x_loaded[p], (b - p) * 8 + 16)
                    load_x(b + 1, 1 - p)
                if first:
                    sp.dma_start(s.factor_sum[:, :, :], rows_of(factors, b)).then_inc(factor_loaded, 16)
                else:
                    sp.wait_ge(factor_loaded, b * 16)
                    sp.wait_ge(factor_used, b)
                    sp.dma_start(factor[:, :, :], rows_of(factors, b)).then_inc(factor_loaded, 16)

            over_batches(sp, load)

        @block.gpsimd
        def _(pool):
            pool.sem_inc(added, 2)

            def scales_of(b):
                wait_alone(pool, s, stats, b + 1)
                row_scales(nc, s, pool, mv, ve[:, :], rs[:, :], shift[:, :], s.minus_half[:, :],
                           pool_step, b * 2).then_inc(scales, 1)

            def lo_of(b, p, t):
                pool.wait_ge(xh_ready, b * T + t + 1)
                nc.gpsimd.tensor_tensor(xl[:, p, t, :], xn[:, p, t, :], xh[:, p, t, :].bitcast(F32),
                                        ALU.subtract).then_inc(xl_ready, 1)

            def normalise(b, p, t):
                wait_alone(pool, s, inv_ready, b * T + t + 1)
                nc.gpsimd.tensor_scalar(prob[:, t, :], prob[:, t, :], inv_sum[:, p * T + t:p * T + t + 1],
                                        1.0, ALU.mult, ALU.mult).then_inc(prob_ready, 1)

            def output_scales(b):
                wait_alone(pool, s, ostats, b + 1)
                row_scales(nc, s, pool, omv, ove[:, :], ors[:, :], oshift[:, :], s.minus_half[:, :],
                           opool, b * 2).then_inc(oscales, 1)

            def add(b, t):
                pool.wait_ge(ctx_normed, b * T + t + 1 + T)
                x = tile_of(s.x, b * T + t)
                nc.gpsimd.tensor_tensor(x, x, normed[:, t % 2, :], ALU.add).then_inc(added, 1)

            scales_of(0)
            for t in range(T):
                lo_of(0, 0, t)

            def body(b, p, before, last):
                if before == 2:
                    output_scales(b - 2)
                for t in range(T):
                    normalise(b, p, t)
                    if t == 0 and not last:
                        scales_of(b + 1)
                    if before == 2:
                        add(b - 2, t)
                if not last:
                    for t in range(T):
                        lo_of(b + 1, 1 - p, t)

            over_batches_two_behind(pool, body)
            for b in (B - 2, B - 1):
                output_scales(b)
                for t in range(T):
                    add(b, t)

        @block.scalar
        def _(act):
            act.sem_inc(ctx_normed, T)

            def exp(b, p, t):
                act.wait_ge(max_ready, b * T + t + 1)
                if not (isinstance(b, int) and b == 0):
                    act.wait_ge(turn_ready, b * 8 - 4 + t + 1 )
                nc.scalar.activation(prob[:, t, :], score[t % 2][:, :], ACT.Exp,
                                     bias=neg_max[:, p * T + t:p * T + t + 1], scale=1.0,
                                     accum_out=row_sum[:, p * T + t:p * T + t + 1]).then_inc(exp_ready, 1)

            def hi_of(b, p, g, first):
                act.wait_ge(turn_ready, b * 8 + g + 1)
                if not first and g % T == 0:
                    act.wait_ge(ctx_ready, b * T)
                dst = (xth if g < T else pth)[:, p, :, (g % T) * P:(g % T + 1) * P]
                nc.scalar.copy(dst, blocks_of(turned[g % 2][:, :])).then_inc(hi_ready, 1)

            def norm(b, t):
                if t == 0:
                    act.wait_ge(oscales, b + 1)
                act.wait_ge(added, b * T + t + 1)
                nc.scalar.activation(normed[:, t % 2, :], context[t][:, :], ACT.Identity,
                                     bias=oshift[:, t:t + 1], scale=ors[:, t:t + 1]).then_inc(ctx_normed, 1)

            def body(b, p, before, last):
                for t in range(T):
                    exp(b, p, t)
                    hi_of(b, p, t, before == 0)
                    if before == 2:
                        norm(b - 2, t)
                for g in range(T, 2 * T):
                    hi_of(b, p, g, before == 0)

            over_batches_two_behind(act, body)
            for b in (B - 2, B - 1):
                for t in range(T):
                    norm(b, t)

        @block.vector
        def _(dve):
            def stats_of(b, p):
                n = b // 2 if isinstance(b, int) else None
                dve.wait_ge(x_loaded[p], (b - p) * 8 + 16)
                for t in range(T):
                    last = nc.vector.bn_stats(bn[:, t, :], tile_of(s.x, b * T + t))
                last.then_inc(own_bn, 1)
                wait_alone(dve, s, own_bn, b + 1)
                for t in range(T):
                    last = nc.vector.bn_aggr(mv[:, t, :], bn[:, t, :])
                last.then_inc(stats, 1)

            def normalised(b, p, tiles):
                if tiles[0] == 0:
                    dve.wait_ge(scales, b + 1)
                for t in tiles:
                    nc.vector.tensor_scalar(xn[:, p, t, :], tile_of(s.x, b * T + t), mv[:, t, 0:1],
                                            rs[:, t:t + 1], ALU.subtract, ALU.mult).then_inc(xn_ready, 1)

            def hi_of_xn(b, p):
                for t in range(T):
                    dve.wait_ge(xn_ready, b * T + t + 1)
                    nc.vector.tensor_copy(xh[:, p, t, :], xn[:, p, t, :]).then_inc(xh_ready, 1)

            def maximum(b, p, t):
                dve.wait_ge(scored, b * T + t + 1)
                nc.vector.reduce_max(neg_max[:, p * T + t:p * T + t + 1], score[t % 2][:, :], AX,
                                     negate=True).then_inc(max_ready, 1)

            def inverse(b, p, t):
                dve.wait_ge(exp_ready, b * T + t + 1)
                nc.vector.reciprocal(inv_sum[:, p * T + t:p * T + t + 1],
                                     row_sum[:, p * T + t:p * T + t + 1]).then_inc(inv_ready, 1)

            def lo_of(b, p, g):
                dve.wait_ge(hi_ready, b * 8 + g + 1)
                at = slice((g % T) * P, (g % T + 1) * P)
                hi, lo = ((xth, xtl) if g < T else (pth, ptl))
                nc.vector.tensor_tensor(lo[:, p, :, at], blocks_of(turned[g % 2][:, :]),
                                        hi[:, p, :, at].bitcast(F32), ALU.subtract).then_inc(lo_ready, 1)

            def output_stats(b, t):
                dve.wait_ge(ctx_ready, (b + 1) * T + t + 1)
                last = nc.vector.bn_stats(obn[:, t, :], context[t][:, :])
                if t == T - 1:
                    last.then_inc(own_obn, 1)
                    wait_alone(dve, s, own_obn, b + 1)
                    for t in range(T):
                        last = nc.vector.bn_aggr(omv[:, t, :], obn[:, t, :])
                    last.then_inc(ostats, 1)

            stats_of(0, 0)
            normalised(0, 0, range(T))
            hi_of_xn(0, 0)

            def body(b, p, first, last):
                for t in range(T):
                    maximum(b, p, t)
                    lo_of(b, p, t)
                    inverse(b, p, t)
                    if t == 0 and not last:
                        stats_of(b + 1, 1 - p)
                    if t == 1 and first:
                        dve.wait_ge(factor_loaded, 16)
                        dve.sem_inc(factor_used, 1)
                    if t == 1 and not first:
                        dve.wait_ge(factor_loaded, b * 16 + 16)
                        dve.wait_ge(factor_used, b)
                        nc.vector.tensor_tensor(s.factor_sum[:, :, :], s.factor_sum[:, :, :], factor[:, :, :],
                                                ALU.add).then_inc(factor_used, 1)
                    if t >= 2 and not last:
                        normalised(b + 1, 1 - p, (0, 1) if t == 2 else (2, 3))
                if not last:
                    hi_of_xn(b + 1, 1 - p)
                for t in range(T):
                    if not first:
                        output_stats(b - 1, t)
                    lo_of(b, p, T + t)

            over_batches(dve, body)
            for t in range(T):
                output_stats(B - 1, t)

        @block.tensor
        def _(pe):
            def scores(b, p, t, first):
                if t == 0:
                    pe.wait_ge(xh_ready, (b + 1) * T)
                    pe.wait_ge(xl_ready, (b + 1) * T)
                if not (first and t < 2):
                    pe.wait_ge(exp_ready, b * T + t - 1)
                at = slice(t * P, (t + 1) * P)
                products(nc, score[t % 2][:, :],
                         [(l[:, p, k, at], r[:, p, k, :])
                          for k in range(T) for l, r in ((xh, xh), (xl, xh), (xh, xl))]).then_inc(scored, 1)

            def turn(b, p, g, first):
                if g < T:
                    pe.wait_ge(xn_ready, b * T + g + 1)
                else:
                    pe.wait_ge(prob_ready, b * T + g - T + 1)
                if not (first and g < 2):
                    pe.wait_ge(lo_ready, b * 8 + g - 1)
                for k in range(T):
                    at = slice(k * P, (k + 1) * P)
                    src = xn[:, p, g, at] if g < T else prob[:, g - T, at]
                    last = nc.tensor.transpose(turned[g % 2][:, at], src, s.identity[:, :])
                last.then_inc(turn_ready, 1)

            def contexts(b, p, t):
                if t == 0:
                    pe.wait_ge(lo_ready, (b + 1) * 8)
                pe.wait_ge(ctx_normed, b * T + t + 1)
                at = slice(t * P, (t + 1) * P)
                products(nc, context[t][:, :],
                         [(l[:, p, k, at], r[:, p, k, :])
                          for k in range(T) for l, r in ((xth, pth), (xtl, pth), (xth, ptl))]).then_inc(ctx_ready, 1)

            pe.sem_inc(ctx_ready, T)

            def body(b, p, first, last):
                for t in range(T):
                    scores(b, p, t, first)
                    turn(b, p, t, first)
                for t in range(T):
                    if not first:
                        contexts(b - 1, 1 - p, t)
                    turn(b, p, T + t, first)

            over_batches(pe, body)
            for t in range(T):
                contexts(B - 1, (B - 1) % 2, t)


def linear_map(nc, s, bias, x_out):
    with ExitStack() as ctx:
        def sb(name, shape, dt=F32):
            return ctx.enter_context(nc.sbuf_tensor(name, shape, dt))

        def sem(name):
            return s.stack.enter_context(nc.semaphore("f0_" + name))

        mh = sb("mh", [P, T, N], F32R)
        ml = sb("ml", [P, T, N], F32R)
        bias_rows = sb("bias_rows", [P, N])
        xn = sb("xn2", [P, 2, T, N])
        xth = sb("xth2", [P, 2, T, N], F32R)
        xtl = sb("xtl2", [P, 2, T, N], F32R)
        mixed = sb("mixed", [P, T, N])
        normed = sb("normed2", [P, 2, N])
        bn = sb("bn2", [P, T, 6])
        mv = sb("mv2", [P, T, 2])
        ve = sb("ve2", [P, T])
        rs = sb("rs2", [P, T])
        shift = sb("shift2", [P, T])
        obn = sb("obn2", [P, T, 6])
        omv = sb("omv2", [P, T, 2])
        ove = sb("ove2", [P, T])
        ors = sb("ors2", [P, T])
        oshift = sb("oshift2", [P, T])
        turned = [ctx.enter_context(nc.psum_tensor(f"turned2_{i}", [P, N], F32)) for i in range(2)]
        mix = [ctx.enter_context(nc.psum_tensor(f"mix{i}", [P, N], F32)) for i in range(T)]

        bias_loaded, weights = sem("bias_loaded"), sem("weights")
        own_bn, stats = sem("own_bn"), sem("stats")
        pool_step, scales = sem("pool_step"), sem("scales")
        xn_ready, turn_ready, hi_ready, lo_ready = (
            sem("xn_ready"), sem("turn_ready"), sem("hi_ready"), sem("lo_ready"))
        mix_ready, mixed_ready, own_obn, ostats, opool, oscales = (
            sem("mix_ready"), sem("mixed_ready"), sem("own_obn"), sem("ostats"), sem("opool"), sem("oscales"))
        normed_ready, added = sem("normed_ready"), sem("added")
        stored = sem("stored")

        block = ctx.enter_context(nc.Block())

        @block.sync
        def _(sp):
            sp.dma_start(bias_rows[:, :], bias.partition_broadcast(P)).then_inc(bias_loaded, 16)

            def store(b, p, first, last):
                sp.wait_ge(added, (b + 1) * T + 2)
                src = s.x[:, b * T:(b + 1) * T, :] if isinstance(b, int) else s.x[:, bass.ds(b * T, T), :]
                sp.dma_start(rows_of(x_out, b), src).then_inc(stored, 16)

            over_batches(sp, store)
            sp.wait_ge(stored, B * 16)

        @block.gpsimd
        def _(pool):
            pool.sem_inc(added, 2)

            def scales_of(b):
                if not (isinstance(b, int) and b == 0):
                    pool.wait_ge(xn_ready, b * T)
                wait_alone(pool, s, stats, b + 1)
                row_scales(nc, s, pool, mv, ve[:, :], rs[:, :], shift[:, :], s.minus_half[:, :],
                           pool_step, b * 2).then_inc(scales, 1)

            def output_scales(b):
                wait_alone(pool, s, ostats, b + 1)
                row_scales(nc, s, pool, omv, ove[:, :], ors[:, :], oshift[:, :], s.minus_half[:, :],
                           opool, b * 2).then_inc(oscales, 1)

            def add(b, t):
                pool.wait_ge(normed_ready, b * T + t + 1 + T)
                x = tile_of(s.x, b * T + t)
                nc.gpsimd.tensor_tensor(x, x, normed[:, t % 2, :], ALU.add).then_inc(added, 1)

            scales_of(0)

            def body(b, p, before, last):
                if before == 2:
                    output_scales(b - 2)
                    add(b - 2, 0)
                    add(b - 2, 1)
                if not last:
                    scales_of(b + 1)
                if before == 2:
                    add(b - 2, 2)
                    add(b - 2, 3)

            over_batches_two_behind(pool, body)
            for b in (B - 2, B - 1):
                output_scales(b)
                for t in range(T):
                    add(b, t)

        @block.scalar
        def _(act):
            act.sem_inc(normed_ready, T)

            def normalised(b, p):
                act.wait_ge(scales, b + 1)
                if not (isinstance(b, int) and b < 2):
                    act.wait_ge(turn_ready, (b - 1) * T)
                for t in range(T):
                    nc.scalar.activation(xn[:, p, t, :], tile_of(s.x, b * T + t), ACT.Identity,
                                         bias=shift[:, t:t + 1], scale=rs[:, t:t + 1]).then_inc(xn_ready, 1)

            def hi_of(b, p, t, first):
                act.wait_ge(turn_ready, b * T + t + 1)
                if not first and t == 0:
                    act.wait_ge(mix_ready, b * T)
                nc.scalar.copy(xth[:, p, :, t * P:(t + 1) * P],
                               blocks_of(turned[t % 2][:, :])).then_inc(hi_ready, 1)

            def norm(b, t):
                if t == 0:
                    act.wait_ge(oscales, b + 1)
                act.wait_ge(added, b * T + t + 1)
                nc.scalar.activation(normed[:, t % 2, :], mixed[:, t, :], ACT.Identity,
                                     bias=oshift[:, t:t + 1], scale=ors[:, t:t + 1]).then_inc(normed_ready, 1)

            nc.scalar.copy(mh[:, :, :], s.factor_sum[:, :, :]).then_inc(weights, 1)
            normalised(0, 0)

            def body(b, p, before, last):
                for t in range(T):
                    hi_of(b, p, t, before == 0)
                    if before == 2:
                        norm(b - 2, t)
                if not last:
                    normalised(b + 1, 1 - p)

            over_batches_two_behind(act, body)
            for b in (B - 2, B - 1):
                for t in range(T):
                    norm(b, t)

        @block.vector
        def _(dve):
            def tile_stats(b, t):
                if t == 0 and not (isinstance(b, int) and b == 0):
                    dve.wait_ge(stats, b)
                tile = nc.vector.bn_stats(bn[:, t, :], tile_of(s.x, b * T + t))
                if t == T - 1:
                    tile.then_inc(own_bn, 1)

            def stats_of(b):
                if not (isinstance(b, int) and b == 0):
                    dve.wait_ge(scales, b)
                wait_alone(dve, s, own_bn, b + 1)
                for t in range(T):
                    last = nc.vector.bn_aggr(mv[:, t, :], bn[:, t, :])
                last.then_inc(stats, 1)

            def lo_of(b, p, t):
                dve.wait_ge(hi_ready, b * T + t + 1)
                at = slice(t * P, (t + 1) * P)
                nc.vector.tensor_tensor(xtl[:, p, :, at], blocks_of(turned[t % 2][:, :]),
                                        xth[:, p, :, at].bitcast(F32), ALU.subtract).then_inc(lo_ready, 1)

            def mixed_of(b, t):
                if t == 0:
                    dve.wait_ge(bias_loaded, 16)
                dve.wait_ge(mix_ready, (b + 1) * T + t + 1)
                dve.wait_ge(normed_ready, b * T + t + 1)
                nc.vector.scalar_tensor_tensor(out=mixed[:, t, :], in0=mix[t][:, :], scalar=RANK ** -0.5,
                                               in1=bias_rows[:, :], op0=ALU.mult, op1=ALU.add).then_inc(mixed_ready, 1)

            def tile_output_stats(b, t):
                dve.wait_ge(mixed_ready, b * T + t + 1 + T)
                tile = nc.vector.bn_stats(obn[:, t, :], mixed[:, t, :])
                if t == T - 1:
                    tile.then_inc(own_obn, 1)

            def output_stats(b):
                wait_alone(dve, s, own_obn, b + 1)
                for t in range(T):
                    last = nc.vector.bn_aggr(omv[:, t, :], obn[:, t, :])
                last.then_inc(ostats, 1)

            dve.sem_inc(mixed_ready, T)
            for t in range(T):
                tile_stats(0, t)
            stats_of(0)
            dve.wait_ge(weights, 1)
            nc.vector.tensor_tensor(ml[:, :, :], s.factor_sum[:, :, :], mh[:, :, :].bitcast(F32),
                                    ALU.subtract).then_inc(weights, 1)

            def body(b, p, first, last):
                for t in range(T):
                    lo_of(b, p, t)
                    if t < 2 and not last:
                        tile_stats(b + 1, 2 * t)
                        tile_stats(b + 1, 2 * t + 1)
                        if t == 1:
                            stats_of(b + 1)
                    if not first:
                        mixed_of(b - 1, t)
                        tile_output_stats(b - 1, t)
                if not first:
                    output_stats(b - 1)

            over_batches(dve, body)
            for t in range(T):
                mixed_of(B - 1, t)
                tile_output_stats(B - 1, t)
            output_stats(B - 1)

        @block.tensor
        def _(pe):
            def turn(b, p, t, first):
                pe.wait_ge(xn_ready, b * T + t + 1)
                if not (first and t < 2):
                    pe.wait_ge(lo_ready, b * T + t - 1)
                for k in range(T):
                    at = slice(k * P, (k + 1) * P)
                    last = nc.tensor.transpose(turned[t % 2][:, at], xn[:, p, t, at], s.identity[:, :])
                last.then_inc(turn_ready, 1)

            def mixes(b, p, t):
                if t == 0:
                    pe.wait_ge(weights, 2)
                    pe.wait_ge(lo_ready, (b + 1) * T)
                pe.wait_ge(mixed_ready, b * T + t + 1)
                at = slice(t * P, (t + 1) * P)
                products(nc, mix[t][:, :],
                         [(l[:, p, k, at], r[:, k, :])
                          for k in range(T) for l, r in ((xth, mh), (xtl, mh), (xth, ml))]).then_inc(mix_ready, 1)

            pe.sem_inc(mix_ready, T)

            def body(b, p, first, last):
                for t in range(T):
                    turn(b, p, t, first)
                    if not first:
                        mixes(b - 1, 1 - p, t)

            over_batches(pe, body)
            for t in range(T):
                mixes(B - 1, (B - 1) % 2, t)


def prepare(nc, s):
    s.identity = s.stack.enter_context(nc.sbuf_tensor("identity", [P, P], F32))
    s.minus_half = s.stack.enter_context(nc.sbuf_tensor("minus_half", [P, T], F32))
    s.minus_one = s.stack.enter_context(nc.sbuf_tensor("minus_one", [P, T], F32))
    s.eps_rms = s.stack.enter_context(nc.sbuf_tensor("eps_rms", [P, T], F32))
    s.plus_half = s.stack.enter_context(nc.sbuf_tensor("plus_half", [P, T], F32))
    s.waits_passed = s.stack.enter_context(nc.semaphore("waits_passed"))
    zeroed = s.stack.enter_context(nc.semaphore("identity_zeroed"))
    with nc.Block() as block:
        @block.gpsimd
        def _(pool):
            nc.gpsimd.memset(s.minus_half[:, :], -0.5)
            nc.gpsimd.memset(s.plus_half[:, :], 0.5)
            nc.gpsimd.memset(s.minus_one[:, :], -1.0)
            nc.gpsimd.memset(s.eps_rms[:, :], EPS_RMS)
            nc.gpsimd.memset(s.identity[:, :], 0.0).then_inc(zeroed, 1)
            pool.wait_ge(zeroed, 1)
            nc.gpsimd.affine_select(out=s.identity[:, :], in_=s.identity[:, :], compare_op=ALU.not_equal,
                                    fill=1.0, base=0, pattern=[[-1, P]], channel_multiplier=1)


HALF = (slice(0, DH), slice(DH, P))
UNITS = HEADS * T
TURN_LAG = 4
OUT_LAG = 9
SUM_LAG = OUT_LAG + 2

NAMES = ["q1", "q2", "q3", "h0", "h1", "wo0", "wo1", "h2", "h3", "wo2", "wo3", "k", "v", "q0"]
SPLIT = [name for name in NAMES if name[0] != "w"]


def side_schedule():
    shares, end = [], {}
    waiting = [(name, {"h": 1, "v": 3 * T * T}.get(name[0], 3 * T)) for name in NAMES]
    at = 0
    for u in range(UNITS):
        shares.append([])
        room = SHARE_BESIDE_OUT if (u - OUT_LAG) % T < 2 else SHARE
        while waiting and room > 0:
            name, count = waiting[0]
            cost = {"h": 2, "v": 0.5}.get(name[0], 1)
            i = NAMES.index(name)
            before = [end[n] + (2 if n[0] == "w" else 3) for n in NAMES[i - 2:i - 1] if n in end]
            before += {"wo0": [CONVERT[-1] - UNITS + 2], "k": [end.get("h3", 0) + 3], "h0": [H[0] + 1], "h1": [H[1] + 1]}.get(name, [])
            if at == 0 and before and max(before) > u:
                break
            step = min(count - at, max(1, int(room / cost)))
            shares[u].append((name, at, at + step, at + step == count))
            room -= step * cost
            at += step
            if at == count:
                end[name] = u
                waiting.pop(0)
                at = 0
    assert not waiting
    return shares, end


STATS = (0, 1, 2, 2)
SCALES = (3, 4, 5)
H = (6, 7, 10, 11)
SHARE, SHARE_BESIDE_OUT = 8, 4
CONVERT = (20, 24, 32, 40)
SHARES, END = side_schedule()
AHEAD = sum(name[0] in "hkv" or name == "q0" for name in NAMES)
WO = [END[f"wo{t}"] for t in range(T)]


RESIDUAL = [at - 1 for at in WO]
NORM = [WO[-1] + 4 + t for t in range(T)]
ADD = [at + 1 for at in NORM]


def side_at(name):
    return (AHEAD + SPLIT.index(name)) % 2 if name in SPLIT else (AHEAD + NAMES.index(name) + T) % 2


def side_use(b, name):
    if isinstance(b, int) and b <= 0:
        return AHEAD + b * len(SPLIT) + SPLIT.index(name)
    j = NAMES.index(name)
    if isinstance(b, int) and b >= B - 1 and name[0] == "w":
        missing = [n for n in NAMES[:j] if n[0] != "w" and (b == B or n[0] != "q")]
        j -= len(missing) + (AHEAD if b == B else 0)
    return b * len(NAMES) + (AHEAD - T + j)


def side_split(b, name):
    return b * len(SPLIT) + (AHEAD + SPLIT.index(name) + 1)


def side_works(u, first, last, drain):
    return [w for w in SHARES[u] if side_runs(w[0], first, last, drain)]


def side_done(u, first, last, drain, lag):
    return [name for name in NAMES if END[name] + lag == u and side_runs(name, first, last, drain)]


def side_runs(name, first, last, drain):
    if name[0] == "w":
        return not first
    return not drain and (not last or name in ("q1", "q2", "q3"))


def grouped_attention(nc, s, norm_scale, split_scale, wq_t, wk_t, wv_t, wo_t, x_in, x_out):
    with ExitStack() as ctx:
        def sb(name, shape, dt=F32):
            return ctx.enter_context(nc.sbuf_tensor("g_" + name, shape, dt))

        def sem(name):
            return s.stack.enter_context(nc.semaphore("a1_" + name))

        def bank(name):
            return ctx.enter_context(nc.psum_tensor("g_" + name, [P, N], F32))

        KV = GROUPS * DH
        wqh, wql = sb("wqh", [P, T, N], F32R), sb("wql", [P, T, N], F32R)
        wkh, wkl = sb("wkh", [P, T, KV], F32R), sb("wkl", [P, T, KV], F32R)
        wvh, wvl = sb("wvh", [P, T, KV], F32R), sb("wvl", [P, T, KV], F32R)
        woh, wol = sb("woh", [P, T, N], F32R), sb("wol", [P, T, N], F32R)
        feature = sb("feature", [P, 3, T])
        x = sb("x", [P, 2, T, N])
        res = sb("res", [P, T, N])
        h = sb("h", [P, 2, N])
        hth, htl = sb("hth", [P, T, N], F32R), sb("htl", [P, T, N], F32R)
        q = sb("q", [P, HEADS, N], F32R)
        kh, kl = sb("kh", [P, 2, GROUPS, N], F32R), sb("kl", [P, 2, GROUPS, N], F32R)
        v = sb("v", [P, 2, T, GROUPS, 2 * DH], F32R)
        prob = sb("prob", [P, T, N])
        pth, ptl = sb("pth", [P, 2, T, N], F32R), sb("ptl", [P, 2, T, N], F32R)
        v_lo_part = sb("v_lo_part", [DH, 2, N])
        out_sum = sb("out_sum", [P, T, N])
        oh, ol = sb("oh", [P, T, N], F32R), sb("ol", [P, T, N], F32R)
        xn = sb("xn", [P, 2, N])
        total = sb("total", [P, T, N])
        bn, mv = sb("bn", [P, T, 6]), sb("mv", [P, T, 2])
        ve, rs, shift = sb("ve", [P, T]), sb("rs", [P, T]), sb("shift", [P, T])
        kept = sb("kept", [P, 2, 2, T])
        root, rms, inv_rms = sb("root", [P, T]), sb("rms", [P, T]), sb("inv_rms", [P, T])
        hs, hshift = sb("hs", [P, T]), sb("hshift", [P, T])
        obn, omv = sb("obn", [P, T, 6]), sb("omv", [P, T, 2])
        ove, ors, oshift = sb("ove", [P, T]), sb("ors", [P, T]), sb("oshift", [P, T])
        neg_max, row_sum, inv_sum = sb("neg_max", [P, 4]), sb("row_sum", [P, 4]), sb("inv_sum", [P, 4])

        score = [bank("score0"), bank("score1")]
        turned = [bank("turned0"), bank("turned1")]
        output = [bank("output0"), bank("output1")]
        side = [bank("side0"), bank("side1")]

        w_loaded, scaled, w_ready = sem("w_loaded"), sem("scaled"), sem("w_ready")
        scaled_step = sem("scaled_step")
        x_loaded = [sem("x_loaded0"), sem("x_loaded1")]
        res_loaded, stored = sem("res_loaded"), sem("stored")
        own_bn, stats, pool_step, scales = sem("own_bn"), sem("stats"), sem("pool_step"), sem("scales")
        h_ready, kept_ready = sem("h_ready"), sem("kept_ready")
        side_ready, side_hi, side_free = sem("side_ready"), sem("side_hi"), sem("side_free")
        scored, max_ready, exp_ready = sem("scored"), sem("max_ready"), sem("exp_ready")
        inv_ready, prob_ready = sem("inv_ready"), sem("prob_ready")
        turn_ready, hi_ready, lo_ready = sem("turn_ready"), sem("hi_ready"), sem("lo_ready")
        out_ready, part_ready, sum_ready = sem("out_ready"), sem("part_ready"), sem("sum_ready")
        oh_ready, ol_ready = sem("oh_ready"), sem("ol_ready")
        xn_ready, total_ready = sem("xn_ready"), sem("total_ready")
        ostats, opool, oscales = sem("ostats"), sem("opool"), sem("oscales")
        normed_ready, added = sem("normed_ready"), sem("added")

        block = ctx.enter_context(nc.Block())

        def is_first(b):
            return isinstance(b, int) and b == 0

        @block.sync
        def _(sp):
            sp.dma_start(x[:, 0, :, :], rows_of(x_in, 0)).then_inc(x_loaded[0], 16)
            for dst, src in ((prob[:, :, :], wq_t.rearrange("(k p) n -> p k n", p=P)),
                             (total[:, :, :], wo_t.rearrange("(k p) n -> p k n", p=P)),
                             (out_sum[:, 0, :].rearrange("p (k n) -> p k n", k=T), wk_t.rearrange("(k p) n -> p k n", p=P)),
                             (out_sum[:, 1, :].rearrange("p (k n) -> p k n", k=T), wv_t.rearrange("(k p) n -> p k n", p=P)),
                             (feature[:, 0, :], norm_scale), (feature[:, 1, :], split_scale)):
                sp.dma_start(dst, src).then_inc(w_loaded, 16)

            def store(b):
                sp.wait_ge(added, (b + 2) * T)
                sp.dma_start(rows_of(x_out, b), res[:, :, :]).then_inc(stored, 16)

            def body(b, p, first, last):
                if not last:
                    if not first:
                        sp.wait_ge(h_ready, b * T)
                        sp.wait_ge(x_loaded[1 - p], (b + 1 - (1 - p)) * 8)
                    sp.dma_start(x[:, 1 - p, :, :], rows_of(x_in, b + 1)).then_inc(x_loaded[1 - p], 16)
                if not first:
                    sp.wait_ge(stored, b * 16)
                    sp.dma_start(res[:, :, :], rows_of(x_in, b - 1)).then_inc(res_loaded, 16)
                    store(b - 1)

            sp.sem_inc(stored, 16)
            over_batches(sp, body)
            sp.wait_ge(stored, B * 16)
            sp.dma_start(res[:, :, :], rows_of(x_in, B - 1)).then_inc(res_loaded, 16)
            store(B - 1)
            sp.wait_ge(stored, B * 16 + 16)

        @block.gpsimd
        def _(pool):
            pool.sem_inc(added, T)
            pool.sem_inc(ol_ready, T)

            def scales_of(b, p, part):
                at = b * 7
                if part == 0:
                    if not is_first(b):
                        pool.wait_ge(h_ready, b * T)
                        pool.wait_ge(kept_ready, b)
                        if not isinstance(b, int):
                            pool.sem_inc(s.waits_passed, 1)
                    wait_alone(pool, s, stats, b + 1)
                    row_scales(nc, s, pool, mv, ve[:, :], rs[:, :], shift[:, :], s.minus_half[:, :],
                               pool_step, at)
                elif part == 1:
                    nc.gpsimd.tensor_tensor(root[:, :], mv[:, :, 1], s.plus_half[:, :],
                                            ALU.pow).then_inc(pool_step, 1)
                    pool.wait_ge(pool_step, at + 3)
                    nc.gpsimd.tensor_tensor(rms[:, :], root[:, :], rs[:, :], ALU.mult).then_inc(pool_step, 1)
                    pool.wait_ge(pool_step, at + 4)
                    nc.gpsimd.tensor_tensor(rms[:, :], rms[:, :], s.eps_rms[:, :], ALU.add).then_inc(pool_step, 1)
                else:
                    pool.wait_ge(pool_step, at + 5)
                    nc.gpsimd.tensor_tensor(inv_rms[:, :], rms[:, :], s.minus_one[:, :],
                                            ALU.pow).then_inc(pool_step, 1)
                    pool.wait_ge(pool_step, at + 6)
                    nc.gpsimd.tensor_tensor(hs[:, :], rs[:, :], inv_rms[:, :], ALU.mult).then_inc(pool_step, 1)
                    nc.gpsimd.tensor_tensor(hshift[:, :], shift[:, :], inv_rms[:, :],
                                            ALU.mult).then_inc(scales, 1)

            def keep_scales(b, p):
                if not isinstance(b, int) or b > 1:
                    pool.wait_ge(xn_ready, (b - 1) * T)
                wait_alone(pool, s, scales, b + 1)
                nc.gpsimd.tensor_copy(kept[:, p, 0, :], rs[:, :])
                nc.gpsimd.tensor_copy(kept[:, p, 1, :], shift[:, :]).then_inc(kept_ready, 1)

            def normalise(g, u):
                wait_alone(pool, s, inv_ready, g + 1)
                at = u % 4
                nc.gpsimd.tensor_scalar(prob[:, at, :], prob[:, at, :], inv_sum[:, at:at + 1],
                                        1.0, ALU.mult, ALU.mult).then_inc(prob_ready, 1)

            def lo_of_output(b, m):
                pool.wait_ge(oh_ready, b * T + m + 1)
                nc.gpsimd.tensor_tensor(ol[:, m, :], out_sum[:, m, :], oh[:, m, :].bitcast(F32),
                                        ALU.subtract).then_inc(ol_ready, 1)

            def residual(b, p, t):
                if t == 0:
                    pool.wait_ge(res_loaded, b * 16 + 16)
                pool.wait_ge(total_ready, b * T + t + 1)
                wait_alone(pool, s, kept_ready, b + 1)
                nc.gpsimd.tensor_scalar(xn[:, t % 2, :], res[:, t, :], kept[:, p, 0, t:t + 1],
                                        kept[:, p, 1, t:t + 1], ALU.mult, ALU.add).then_inc(xn_ready, 1)

            def output_scales(b):
                wait_alone(pool, s, ostats, b + 1)
                row_scales(nc, s, pool, omv, ove[:, :], ors[:, :], oshift[:, :], s.minus_half[:, :],
                           opool, b * 2).then_inc(oscales, 1)

            def add(b, t):
                pool.wait_ge(normed_ready, b * T + t + 1)
                nc.gpsimd.tensor_tensor(res[:, t, :], res[:, t, :], total[:, t, :],
                                        ALU.add).then_inc(added, 1)

            for part in range(3):
                scales_of(0, 0, part)
            keep_scales(0, 0)

            def step(b, p, u, first, last, drain):
                if u > 0 or not first:
                    if not drain or u == 0:
                        normalise(b * UNITS + u - 1, u + 3)
                for m, at in enumerate(CONVERT):
                    if at + 1 == u and not drain:
                        lo_of_output(b, m)
                    if at + 1 - UNITS == u and not first:
                        lo_of_output(b - 1, m)
                if u in RESIDUAL and not first:
                    residual(b - 1, 1 - p, RESIDUAL.index(u))
                if u == WO[-1] + 2 and not first:
                    output_scales(b - 1)
                if u in ADD and not first:
                    add(b - 1, ADD.index(u))
                if not last and not drain:
                    if u in SCALES:
                        scales_of(b + 1, 1 - p, SCALES.index(u))
                    if u == WO[-1] + 1:
                        keep_scales(b + 1, 1 - p)

            def body(b, p, first, last):
                for u in range(UNITS):
                    step(b, p, u, first, last, False)

            over_batches(pool, body)
            for u in range(ADD[-1] + 1):
                step(B, 0, u, False, True, True)

        @block.scalar
        def _(act):
            def h_of(b, p, t):
                if t == 0:
                    act.wait_ge(scales, b + 1)
                nc.scalar.activation(h[:, t % 2, :], x[:, p, t, :], ACT.Identity, bias=hshift[:, t:t + 1],
                                     scale=hs[:, t:t + 1]).then_inc(h_ready, 1)

            def hi_of(b, p, name):
                act.wait_ge(side_ready, side_use(b, name) + 1)
                src = side[side_at(name)]
                if name[0] == "h":
                    t = int(name[1])
                    last = nc.scalar.copy(hth[:, :, t * P:(t + 1) * P], blocks_of(src[:, :]))
                elif name[0] == "q":
                    m = int(name[1])
                    for e, half in enumerate(HALF):
                        last = nc.scalar.copy(q[half, 2 * m + e, :], src[half, :])
                elif name == "k":
                    for g in range(GROUPS):
                        for half in HALF:
                            last = nc.scalar.copy(kh[half, 1 - p, g, :], src[HALF[g], :])
                else:
                    last = nc.scalar.copy(v[:, 1 - p, :, :, 0:DH],
                                          src[:, :].rearrange("p (t g d) -> p t g d", t=T, g=GROUPS))
                last.then_inc(side_hi, 1)

            def exp(g, u, first):
                act.wait_ge(max_ready, g + 1)
                if not (first and u < 4):
                    act.wait_ge(turn_ready, g - 3)
                at = u % 4
                nc.scalar.activation(prob[:, at, :], score[u % 2][:, :], ACT.Exp, bias=neg_max[:, at:at + 1],
                                     scale=1.0, accum_out=row_sum[:, at:at + 1]).then_inc(exp_ready, 1)

            def v_lo_of(head, hd):
                act.wait_ge(out_ready, head + 1)
                nc.scalar.copy(v_lo_part[:, hd % 2, :], output[hd % 2][HALF[1], :]).then_inc(part_ready, 1)

            def norm(b, t):
                if t == 0:
                    act.wait_ge(oscales, b + 1)
                nc.scalar.activation(total[:, t, :], total[:, t, :], ACT.Identity,
                                     bias=oshift[:, t:t + 1], scale=ors[:, t:t + 1]).then_inc(normed_ready, 1)

            h_of(0, 0, 0)
            h_of(0, 0, 1)
            for t in range(T):
                hi_of(-1, 1, f"h{t}")
                if t < 2:
                    h_of(0, 0, t + 2)
            act.wait_ge(scaled, 1)
            nc.scalar.copy(wkh[:, :, :], out_sum[:, 0, :].rearrange("p (k n) -> p k n", k=T))
            nc.scalar.copy(wvh[:, :, :], out_sum[:, 1, :].rearrange("p (k n) -> p k n", k=T))
            nc.scalar.copy(wqh[:, :, :], prob[:, :, :])
            nc.scalar.copy(woh[:, :, :], total[:, :, :]).then_inc(w_ready, 1)
            for name in ("k", "v", "q0"):
                hi_of(-1, 1, name)

            def step(b, p, u, first, last, drain):
                g = b * UNITS + u
                turn_u = u - TURN_LAG
                if not (first and turn_u < 0) and not (drain and turn_u >= 0):
                    if turn_u % T == 0 and not (first and turn_u < 2 * T):
                        act.wait_ge(out_ready, b * HEADS + turn_u // T - 1)
                    act.wait_ge(turn_ready, g - TURN_LAG + 1)
                    at = turn_u % T
                    nc.scalar.copy(pth[:, (turn_u // T) % 2, :, at * P:(at + 1) * P],
                                   blocks_of(turned[turn_u % 2][:, :])).then_inc(hi_ready, 1)
                if not drain:
                    exp(g, u, first)
                done = u - OUT_LAG - 1
                if done % T == 0 and not (first and done < 0) and not (drain and done >= 0):
                    v_lo_of(b * HEADS + done // T, done // T)
                for name in side_done(u, first, last, drain, 1):
                    if name in SPLIT:
                        hi_of(b, p, name)
                if u in NORM and not first:
                    norm(b - 1, NORM.index(u))
                if u in H and not last and not drain:
                    h_of(b + 1, 1 - p, H.index(u))

            def body(b, p, first, last):
                for u in range(UNITS):
                    step(b, p, u, first, last, False)

            over_batches(act, body)
            for u in range(NORM[-1] + 1):
                step(B, 0, u, False, True, True)

        @block.vector
        def _(dve):
            def stats_of(b, p, t):
                if t == 0:
                    dve.wait_ge(x_loaded[p], (b - p) * 8 + 16)
                    if not is_first(b):
                        dve.wait_ge(stats, b)
                last = nc.vector.bn_stats(bn[:, t, :], x[:, p, t, :])
                if t == T - 1:
                    last.then_inc(own_bn, 1)
                    if not is_first(b):
                        dve.wait_ge(scales, b)
                    wait_alone(dve, s, own_bn, b + 1)
                    for t in range(T):
                        last = nc.vector.bn_aggr(mv[:, t, :], bn[:, t, :])
                    last.then_inc(stats, 1)

            def lo_of(b, p, name):
                dve.wait_ge(side_hi, side_split(b, name))
                src = side[side_at(name)]
                if name[0] == "h":
                    cols = slice(int(name[1]) * P, (int(name[1]) + 1) * P)
                    last = nc.vector.tensor_tensor(htl[:, :, cols], blocks_of(src[:, :]),
                                                   hth[:, :, cols].bitcast(F32), ALU.subtract)
                elif name[0] == "q":
                    m = int(name[1])
                    for e, half in enumerate(HALF):
                        last = nc.vector.tensor_tensor(q[HALF[1 - e], 2 * m + e, :], src[half, :],
                                                       q[half, 2 * m + e, :].bitcast(F32), ALU.subtract)
                elif name == "k":
                    for g in range(GROUPS):
                        for half in HALF:
                            last = nc.vector.tensor_tensor(kl[half, 1 - p, g, :], src[HALF[g], :],
                                                           kh[HALF[g], 1 - p, g, :].bitcast(F32), ALU.subtract)
                else:
                    last = nc.vector.tensor_tensor(v[:, 1 - p, :, :, DH:],
                                                   src[:, :].rearrange("p (t g d) -> p t g d", t=T, g=GROUPS),
                                                   v[:, 1 - p, :, :, 0:DH].bitcast(F32), ALU.subtract)
                last.then_inc(side_free, 1)

            def total_of(b, use, t):
                dve.wait_ge(side_ready, use + 1)
                dve.wait_ge(xn_ready, b * T + t + 1)
                dve.wait_ge(added, b * T + t + 1)
                nc.vector.tensor_tensor(total[:, t, :], side[side_at(f"wo{t}")][:, :], xn[:, t % 2, :],
                                        ALU.add).then_inc(total_ready, 1)
                dve.wait_ge(total_ready, b * T + t + 1 + 2)
                nc.vector.bn_stats(obn[:, t, :], total[:, t, :]).then_inc(side_free, 1)
                if t == T - 1:
                    wait_alone(dve, s, side_free, use + 1)
                    for t in range(T):
                        last = nc.vector.bn_aggr(omv[:, t, :], obn[:, t, :])
                    last.then_inc(ostats, 1)

            def sum_of(b, hd):
                dve.wait_ge(part_ready, b * HEADS + hd + 1)
                m = hd // 2
                if hd % 2 == 0 and not (is_first(b) and hd >= 0):
                    dve.wait_ge(ol_ready, b * T + m + 1)
                nc.vector.tensor_tensor(out_sum[HALF[hd % 2], m % T, :], output[hd % 2][HALF[0], :],
                                        v_lo_part[:, hd % 2, :], ALU.add).then_inc(sum_ready, 1)

            def hi_of_output(b, m):
                dve.wait_ge(sum_ready, b * HEADS + 2 * m + 2)
                nc.vector.tensor_copy(oh[:, m, :], out_sum[:, m, :]).then_inc(oh_ready, 1)

            dve.sem_inc(total_ready, 2)
            for t in range(T):
                stats_of(0, 0, t)
            dve.wait_ge(w_loaded, 6 * 16)
            nc.vector.tensor_tensor(feature[:, 2, :], feature[:, 0, :], feature[:, 1, :],
                                    ALU.mult).then_inc(scaled_step, 1)
            dve.wait_ge(scaled_step, 1)
            raw_k = out_sum[:, 0, :].rearrange("p (k n) -> p k n", k=T)
            raw_v = out_sum[:, 1, :].rearrange("p (k n) -> p k n", k=T)
            for k in range(T):
                nc.vector.tensor_scalar(prob[:, k, :], prob[:, k, :], feature[:, 2, k:k + 1], DH ** -0.5,
                                        ALU.mult, ALU.mult)
                for w in (raw_k, raw_v):
                    last = nc.vector.tensor_scalar(w[:, k, :], w[:, k, :], feature[:, 2, k:k + 1], None, ALU.mult)
            last.then_inc(scaled, 1)
            for t in range(T):
                lo_of(-1, 1, f"h{t}")
            dve.wait_ge(w_ready, 1)
            nc.vector.tensor_tensor(wkl[:, :, :], raw_k, wkh[:, :, :].bitcast(F32), ALU.subtract)
            nc.vector.tensor_tensor(wvl[:, :, :], raw_v, wvh[:, :, :].bitcast(F32), ALU.subtract)
            nc.vector.tensor_tensor(wql[:, :, :], prob[:, :, :], wqh[:, :, :].bitcast(F32), ALU.subtract)
            nc.vector.tensor_tensor(wol[:, :, :], total[:, :, :], woh[:, :, :].bitcast(F32),
                                    ALU.subtract).then_inc(w_ready, 1)
            for name in ("k", "v", "q0"):
                lo_of(-1, 1, name)

            def step(b, p, u, first, last, drain):
                g = b * UNITS + u
                if not drain:
                    dve.wait_ge(scored, g + 1)
                    at = u % 4
                    nc.vector.reduce_max(neg_max[:, at:at + 1], score[u % 2][:, :], AX,
                                         negate=True).then_inc(max_ready, 1)
                if (u > 0 or not first) and (not drain or u == 0):
                    at = (u - 1) % 4
                    dve.wait_ge(exp_ready, g)
                    nc.vector.reciprocal(inv_sum[:, at:at + 1], row_sum[:, at:at + 1]).then_inc(inv_ready, 1)
                for name in side_done(u, first, last, drain, 2):
                    if name in SPLIT:
                        lo_of(b, p, name)
                turn_u = u - TURN_LAG
                if not (first and turn_u < 0) and not (drain and turn_u >= 0):
                    dve.wait_ge(hi_ready, g - TURN_LAG + 1)
                    cols = slice(turn_u % T * P, (turn_u % T + 1) * P)
                    at = (turn_u // T) % 2
                    nc.vector.tensor_tensor(ptl[:, at, :, cols], blocks_of(turned[turn_u % 2][:, :]),
                                            pth[:, at, :, cols].bitcast(F32), ALU.subtract).then_inc(lo_ready, 1)
                for name in side_done(u, first, last, drain, 1):
                    if name not in SPLIT:
                        total_of(b - 1, side_use(b, name), int(name[2]))
                done = u - SUM_LAG
                if done % T == 0 and not (first and done < 0) and not (drain and done >= 0):
                    hd = done // T
                    sum_of(b, hd)
                for m, at in enumerate(CONVERT):
                    if at == u and not drain:
                        hi_of_output(b, m)
                    if at - UNITS == u and not first:
                        hi_of_output(b - 1, m)
                for t, at in enumerate(STATS):
                    if at == u and not last and not drain:
                        stats_of(b + 1, 1 - p, t)

            def body(b, p, first, last):
                for u in range(UNITS):
                    step(b, p, u, first, last, False)

            over_batches(dve, body)
            for u in range(WO[-1] + 2):
                step(B, 0, u, False, True, True)

        @block.tensor
        def _(pe):
            def side_bank(use):
                if not (isinstance(use, int) and use < 2):
                    pe.wait_ge(side_free, use - 1)

            def turn_h(b, use, t):
                side_bank(use)
                pe.wait_ge(h_ready, b * T + t + 1)
                for k in range(T):
                    cols = slice(k * P, (k + 1) * P)
                    last = nc.tensor.transpose(side[side_at(f"h{t}")][:, cols], h[:, t % 2, cols], s.identity[:, :])
                last.then_inc(side_ready, 1)

            def split(lh, ll, rh, rl):
                return ((lh, rh), (ll, rh), (lh, rl))

            def side_share(b, name, start, end, done):
                use, out = side_use(b, name), side[side_at(name)]
                if name[0] == "h":
                    return turn_h(b + 1, use, int(name[1]))
                if start == 0:
                    side_bank(use)
                if name == "k" and start == 0:
                    pe.wait_ge(side_free, side_use(b, "h3") + 1)
                if name == "wo0" and start == 0:
                    pe.wait_ge(ol_ready, (b + 1) * T)
                for m in range(start, end):
                    k, n, bank_cols = m // 3 % T, m % 3, slice(0, N)
                    if name == "v":
                        cols = bank_cols = slice(m // (3 * T) * P, (m // (3 * T) + 1) * P)
                        pairs = split(hth[:, k, cols], htl[:, k, cols], wvh[:, k, :], wvl[:, k, :])
                    elif name == "k":
                        pairs = split(wkh[:, k, :], wkl[:, k, :], hth[:, k, :], htl[:, k, :])
                    else:
                        cols = slice(int(name[-1]) * P, (int(name[-1]) + 1) * P)
                        pairs = (split(wqh[:, k, cols], wql[:, k, cols], hth[:, k, :], htl[:, k, :])
                                 if name[0] == "q" else
                                 split(oh[:, k, cols], ol[:, k, cols], woh[:, k, :], wol[:, k, :]))
                    last = nc.tensor.matmul(out[:, bank_cols], *pairs[n], start=(k == 0 and n == 0),
                                            stop=(k == T - 1 and n == 2))
                if done:
                    last.then_inc(side_ready, 1)

            for t in range(T):
                turn_h(0, t, t)
            pe.wait_ge(w_ready, 2)
            for name, count in (("k", 3 * T), ("v", 3 * T * T), ("q0", 3 * T)):
                side_share(-1, name, 0, count, True)

            def step(b, p, u, first, last, drain):
                g = b * UNITS + u
                turn_u = u - TURN_LAG
                if not (first and turn_u < 0) and not (drain and turn_u >= 0):
                    pe.wait_ge(prob_ready, g - TURN_LAG + 1)
                    if not (first and turn_u < 2):
                        pe.wait_ge(lo_ready, g - TURN_LAG - 1)
                    for k in range(T):
                        cols = slice(k * P, (k + 1) * P)
                        mm = nc.tensor.transpose(turned[turn_u % 2][:, cols], prob[:, turn_u % 4, cols],
                                                 s.identity[:, :])
                    mm.then_inc(turn_ready, 1)
                if not drain:
                    hd, row = u // T, u % T
                    if u == 0:
                        pe.wait_ge(side_free, side_use(b, "q1"))
                    elif u % (2 * T) == 0:
                        pe.wait_ge(side_free, side_use(b, f"q{u // (2 * T)}") + 1)
                    if not (first and u < 2):
                        pe.wait_ge(exp_ready, g - 1)
                    lhsT = q[:, hd, row * P:(row + 1) * P]
                    products(nc, score[u % 2][:, :], [(lhsT, kh[:, p, hd // HPG, :]), (lhsT, kl[:, p, hd // HPG, :])]
                             ).then_inc(scored, 1)
                out_u = u - OUT_LAG
                if out_u % T < 2 and not (first and out_u < 0) and not (drain and out_u >= 0):
                    hd = out_u // T
                    if out_u % T == 0:
                        pe.wait_ge(lo_ready, (b * HEADS + hd + 1) * T)
                        if not (first and hd < 2):
                            pe.wait_ge(sum_ready, b * HEADS + hd - 1)
                    for t in (out_u % T * 2, out_u % T * 2 + 1):
                        lhsT = v[:, p if out_u >= 0 else 1 - p, t, hd % HEADS // HPG, :]
                        nc.tensor.matmul(output[hd % 2][:, :], lhsT, pth[:, hd % 2, t, :],
                                         start=(t == 0), stop=False)
                        mm = nc.tensor.matmul(output[hd % 2][:, :], lhsT, ptl[:, hd % 2, t, :], start=False,
                                              stop=(t == T - 1))
                    if t == T - 1:
                        mm.then_inc(out_ready, 1)
                for name, start, end, done in side_works(u, first, last, drain):
                    side_share(b, name, start, end, done)

            def body(b, p, first, last):
                for u in range(UNITS):
                    step(b, p, u, first, last, False)

            over_batches(pe, body)
            for u in range(WO[-1] + 1):
                step(B, 0, u, False, True, True)


INNER_PAIRS = IT + T // 2


def turn_bank(p, t):
    return (p * INNER_PAIRS + t // 2) % 2 * 2 + t % 2


def pair_at(p, i):
    return (p * INNER_PAIRS + T // 2 + i) % 2 * 2


def gated_ffn(nc, s, gate_t, up_t, down_t, gate_s, up_s, down_s, x_in, out):
    with ExitStack() as ctx:
        def sb(name, shape, dt=F32):
            return ctx.enter_context(nc.sbuf_tensor("f_" + name, shape, dt))

        def sem(name):
            return s.stack.enter_context(nc.semaphore("f1_" + name))

        def bank(name):
            return ctx.enter_context(nc.psum_tensor("f_" + name, [P, N], F32))

        wh, wl = sb("wh", [P, IT, 3, N], F32R), sb("wl", [P, IT, 3, N], F32R)
        inner_scale = sb("inner_scale", [P, 2, IT])
        down_scale = sb("down_scale", [P, N])
        x = sb("x", [P, 2, T, N])
        xn = sb("xn", [P, T, N])
        xth, xtl = sb("xth", [P, T, N], F32R), sb("xtl", [P, T, N], F32R)
        silu = sb("silu", [P, 2, N])
        hidden = sb("hidden", [P, 2, N])
        hh, hl = sb("hh", [P, 2, N], F32R), sb("hl", [P, 2, N], F32R)
        y = sb("y", [P, T, N])
        lo_max, lo_column, lo_row = sb("lo_max", [P, IT]), sb("lo_column", [P, 1]), sb("lo_row", [1, P])
        lo_most, lo_counts = sb("lo_most", [1, 1]), sb("lo_counts", [1, 1], I32)
        bn, mv = sb("bn", [P, T, 6]), sb("mv", [P, T, 2])
        ve, rs, shift = sb("ve", [P, T]), sb("rs", [P, T]), sb("shift", [P, T])
        obn, omv = sb("obn", [P, T, 6]), sb("omv", [P, T, 2])
        ove, ors, oshift = sb("ove", [P, T]), sb("ors", [P, T]), sb("oshift", [P, T])
        inner = [bank(f"inner{i}") for i in range(4)]
        down = [bank(f"down{i}") for i in range(T)]
        raw = [y[:, 0:3, :], x[:, 1, 0:3, :]]

        raw_loaded = [sem("raw_loaded0"), sem("raw_loaded1")]
        scale_loaded, wh_ready, wl_ready = sem("scale_loaded"), sem("wh_ready"), sem("wl_ready")
        x_loaded, stored = [sem("x_loaded0"), sem("x_loaded1")], sem("stored")
        own_bn, stats, pool_step, scales = sem("own_bn"), sem("stats"), sem("pool_step"), sem("scales")
        xn_ready, turn_ready, th_ready, tl_ready = sem("xn_ready"), sem("turn_ready"), sem("th_ready"), sem("tl_ready")
        gate_ready, up_ready, silu_ready, hidden_ready = (
            sem("gate_ready"), sem("up_ready"), sem("silu_ready"), sem("hidden_ready"))
        hh_ready, hl_ready, down_used = sem("hh_ready"), sem("hl_ready"), sem("down_used")
        y_ready, own_obn, ostats, opool, oscales = (
            sem("y_ready"), sem("own_obn"), sem("ostats"), sem("opool"), sem("oscales"))
        normed, added = sem("normed"), sem("added")
        lo_step, lo_turned = sem("lo_step"), sem("lo_turned")

        block = ctx.enter_context(nc.Block())

        def is_first(b):
            return isinstance(b, int) and b == 0

        @block.sync
        def _(sp):
            sp.dma_start(x[:, 0, :, :], rows_of(x_in, 0)).then_inc(x_loaded[0], 16)
            for dst, src in ((inner_scale[:, 0, :], gate_s), (inner_scale[:, 1, :], up_s),
                             (down_scale[:, :], down_s.partition_broadcast(P))):
                sp.dma_start(dst, src).then_inc(scale_loaded, 16)
            for i in range(IT):
                if i >= 2:
                    sp.wait_ge(wl_ready, i - 1)
                for j, src in enumerate((gate_t, up_t, down_t)):
                    sp.dma_start(raw[i % 2][:, j, :], src[i, :, :]).then_inc(raw_loaded[i % 2], 16)
            sp.wait_ge(wl_ready, IT)
            sp.dma_start(x[:, 1, :, :], rows_of(x_in, 1)).then_inc(x_loaded[1], 16)
            sp.wait_ge(lo_step, 2)
            sp.dma_start(lo_row[:, :], lo_column[:, :]).then_inc(lo_turned, 16)

            def store(b, p):
                sp.wait_ge(added, (b + 2) * T)
                sp.dma_start(rows_of(out, b), x[:, p, :, :]).then_inc(stored, 16)

            def body(b, p, first, last):
                if not first:
                    store(b - 1, 1 - p)
                if not last and not first:
                    sp.wait_ge(stored, b * 16)
                    sp.dma_start(x[:, 1 - p, :, :], rows_of(x_in, b + 1)).then_inc(x_loaded[1 - p], 16)

            over_batches(sp, body)
            store(B - 1, (B - 1) % 2)
            sp.wait_ge(stored, B * 16)

        @block.gpsimd
        def _(pool):
            def scales_of(b):
                if not is_first(b):
                    pool.wait_ge(xn_ready, b * T)
                wait_alone(pool, s, stats, b + 1)
                row_scales(nc, s, pool, mv, ve[:, :], rs[:, :], shift[:, :], s.minus_half[:, :],
                           pool_step, b * 2).then_inc(scales, 1)

            def lo_of_hidden(b, i, at):
                pool.wait_ge(hh_ready, b * IT + i + 1)
                nc.gpsimd.tensor_tensor(hl[:, at, :], hidden[:, at, :], hh[:, at, :].bitcast(F32),
                                        ALU.subtract).then_inc(hl_ready, 1)

            def output_scales(b):
                wait_alone(pool, s, ostats, b + 1)
                row_scales(nc, s, pool, omv, ove[:, :], ors[:, :], oshift[:, :], s.minus_half[:, :],
                           opool, b * 2).then_inc(oscales, 1)

            def add(b, p, t):
                pool.wait_ge(normed, b * T + t + 1)
                nc.gpsimd.tensor_tensor(x[:, p, t, :], x[:, p, t, :], y[:, t, :], ALU.add).then_inc(added, 1)

            pool.sem_inc(added, T)
            scales_of(0)

            def body(b, p, first, last):
                for i in range(IT):
                    if not first:
                        if i == 1:
                            output_scales(b - 1)
                        if 2 <= i < 2 + T:
                            add(b - 1, 1 - p, i - 2)
                    if i == 9 and not first and not last:
                        scales_of(b + 1)
                    lo_of_hidden(b, i, (i + p) % 2)
                if first:
                    scales_of(b + 1)

            over_batches(pool, body)
            output_scales(B - 1)
            for t in range(T):
                add(B - 1, (B - 1) % 2, t)

        @block.scalar
        def _(act):
            def normalised(b, p):
                act.wait_ge(scales, b + 1)
                if not is_first(b):
                    act.wait_ge(turn_ready, b * T)
                for t in range(T):
                    nc.scalar.activation(xn[:, t, :], x[:, p, t, :], ACT.Identity, bias=shift[:, t:t + 1],
                                         scale=rs[:, t:t + 1]).then_inc(xn_ready, 1)

            def hi_of_xt(b, t, bank_of):
                if t == 0 and not is_first(b):
                    act.wait_ge(up_ready, b * IT)
                act.wait_ge(turn_ready, b * T + t + 1)
                nc.scalar.copy(xth[:, :, t * P:(t + 1) * P],
                               blocks_of(inner[bank_of(t)][:, :])).then_inc(th_ready, 1)

            def silu_of(b, p, i, first):
                act.wait_ge(gate_ready, b * IT + i + 1)
                if not (first and i < 2):
                    act.wait_ge(hidden_ready, b * IT + i - 1)
                at = (i + p) % 2
                nc.scalar.activation(silu[:, at, :], inner[pair_at(p, i)][:, :], ACT.Silu,
                                     scale=inner_scale[:, 0, i:i + 1]).then_inc(silu_ready, 1)

            def norm(b, t):
                if t == 0:
                    act.wait_ge(oscales, b + 1)
                nc.scalar.activation(y[:, t, :], y[:, t, :], ACT.Identity, bias=oshift[:, t:t + 1],
                                     scale=ors[:, t:t + 1]).then_inc(normed, 1)

            normalised(0, 0)
            for t in range(T):
                hi_of_xt(0, t, lambda t: turn_bank(0, t))
            act.wait_ge(scale_loaded, 48)

            def body(b, p, first, last):
                for i in range(IT):
                    if first:
                        act.wait_ge(raw_loaded[i % 2], (i // 2 + 1) * 48)
                        nc.scalar.copy(wh[:, i, :, :], raw[i % 2]).then_inc(wh_ready, 1)
                    silu_of(b, p, i, first)
                    if 2 <= i < 2 + T and not first:
                        norm(b - 1, i - 2)
                if not last:
                    normalised(b + 1, 1 - p)
                    for t in range(T):
                        hi_of_xt(b + 1, t, lambda t: turn_bank(1 - p, t))

            over_batches(act, body)
            for t in range(T):
                norm(B - 1, t)

        @block.vector
        def _(dve):
            def stats_of(b, p):
                dve.wait_ge(x_loaded[p], (b - p) * 8 + 16)
                if not is_first(b):
                    dve.wait_ge(stats, b)
                for t in range(T):
                    last = nc.vector.bn_stats(bn[:, t, :], x[:, p, t, :])
                last.then_inc(own_bn, 1)
                if not is_first(b):
                    dve.wait_ge(scales, b)
                wait_alone(dve, s, own_bn, b + 1)
                for t in range(T):
                    last = nc.vector.bn_aggr(mv[:, t, :], bn[:, t, :])
                last.then_inc(stats, 1)

            def lo_of_xt(b, t, at):
                dve.wait_ge(th_ready, b * T + t + 1)
                cols = slice(t * P, (t + 1) * P)
                nc.vector.tensor_tensor(xtl[:, :, cols], blocks_of(inner[at][:, :]),
                                        xth[:, :, cols].bitcast(F32), ALU.subtract).then_inc(tl_ready, 1)

            def hidden_of(b, p, i, first):
                dve.wait_ge(up_ready, b * IT + i + 1)
                dve.wait_ge(silu_ready, b * IT + i + 1)
                if not (first and i < 2):
                    dve.wait_ge(hl_ready, b * IT + i - 1)
                at = (i + p) % 2
                nc.vector.scalar_tensor_tensor(out=hidden[:, at, :], in0=inner[pair_at(p, i) + 1][:, :],
                                               scalar=inner_scale[:, 1, i:i + 1], in1=silu[:, at, :],
                                               op0=ALU.mult, op1=ALU.mult).then_inc(hidden_ready, 1)
                if not (first and i < 2):
                    dve.wait_ge(down_used, b * IT + i - 1)
                dve.wait_ge(hidden_ready, b * IT + i + 1)
                nc.vector.tensor_copy(hh[:, at, :], hidden[:, at, :]).then_inc(hh_ready, 1)

            def y_of(b, t):
                dve.wait_ge(down_used, (b + 1) * IT)
                dve.wait_ge(added, b * T + t + 1)
                nc.vector.tensor_tensor(y[:, t, :], down[t][:, :], down_scale[:, :], ALU.mult).then_inc(y_ready, 1)

            def output_stats(b):
                for t in range(T):
                    dve.wait_ge(y_ready, b * T + t + 1)
                    last = nc.vector.bn_stats(obn[:, t, :], y[:, t, :])
                last.then_inc(own_obn, 1)
                wait_alone(dve, s, own_obn, b + 1)
                for t in range(T):
                    last = nc.vector.bn_aggr(omv[:, t, :], obn[:, t, :])
                last.then_inc(ostats, 1)

            stats_of(0, 0)
            for t in range(T):
                lo_of_xt(0, t, turn_bank(0, t))
            dve.wait_ge(scale_loaded, 48)

            def body(b, p, first, last):
                for i in range(IT):
                    if first:
                        dve.wait_ge(wh_ready, i + 1)
                        nc.vector.tensor_tensor(wl[:, i, :, :], raw[i % 2], wh[:, i, :, :].bitcast(F32),
                                                ALU.subtract).then_inc(wl_ready, 1)
                        dve.wait_ge(wl_ready, i + 1)
                        largest = nc.vector.tensor_reduce(lo_max[:, i:i + 1], wl[:, i, :, :].bitcast(F32),
                                                          mybir.AxisListType.XY, ALU.max,
                                                          apply_absolute_value=True)
                        if i == IT - 1:
                            largest.then_inc(lo_step, 1)
                            dve.wait_ge(lo_step, 1)
                            nc.vector.reduce_max(lo_column[:, :], lo_max[:, :], AX).then_inc(lo_step, 1)
                    if i == 0 and not first:
                        for t in range(T):
                            y_of(b - 1, t)
                    hidden_of(b, p, i, first)
                    if i == 0 and not first:
                        output_stats(b - 1)
                    if i == (IT - 1 if first else 8) and not last:
                        stats_of(b + 1, 1 - p)
                if not last:
                    for t in range(T):
                        lo_of_xt(b + 1, t, turn_bank(1 - p, t))
                if first:
                    dve.wait_ge(lo_turned, 16)
                    nc.vector.reduce_max(lo_most[:, :], lo_row[:, :], AX).then_inc(lo_step, 1)
                    dve.wait_ge(lo_step, 3)
                    nc.vector.tensor_scalar(lo_counts[:, :], lo_most[:, :], 0.0, None,
                                            ALU.is_gt).then_inc(lo_step, 1)

            over_batches(dve, body)
            for t in range(T):
                y_of(B - 1, t)
            output_stats(B - 1)

        @block.tensor
        def _(pe):
            def turn(b, p, t):
                pe.wait_ge(xn_ready, b * T + t + 1)
                if not is_first(b):
                    pe.wait_ge(hidden_ready, b * IT - 1 + t // 2)
                for k in range(T):
                    cols = slice(k * P, (k + 1) * P)
                    last = nc.tensor.transpose(inner[turn_bank(p, t)][:, cols], xn[:, t, cols], s.identity[:, :])
                last.then_inc(turn_ready, 1)

            def inner_of(b, p, i, first, with_lo):
                if first:
                    pe.wait_ge(wl_ready, i + 1)
                if i == 0:
                    pe.wait_ge(tl_ready, (b + 1) * T)
                if i >= 2:
                    pe.wait_ge(hidden_ready, b * IT + i - 1)
                for j, done in ((0, gate_ready), (1, up_ready)):
                    pairs = []
                    for k in range(T):
                        cols = slice(k * P, (k + 1) * P)
                        pairs += [(wh[:, i, j, cols], xth[:, k, :]), (wh[:, i, j, cols], xtl[:, k, :])]
                        if with_lo:
                            pairs.append((wl[:, i, j, cols], xth[:, k, :]))
                    products(nc, inner[pair_at(p, i) + j][:, :], pairs).then_inc(done, 1)

            def down_of(b, p, i, first, with_lo):
                pe.wait_ge(hl_ready, b * IT + i + 1)
                if i == 0 and not first:
                    pe.wait_ge(y_ready, b * T)
                at = (i + p) % 2
                for t in range(T):
                    cols = slice(t * P, (t + 1) * P)
                    halves = ((hh, wh), (hl, wh), (hh, wl)) if with_lo else ((hh, wh), (hl, wh))
                    for n, (l, r) in enumerate(halves):
                        last = nc.tensor.matmul(down[t][:, :], l[:, at, cols], r[:, i, 2, :],
                                                start=(i == 0 and n == 0),
                                                stop=(i == IT - 1 and n == len(halves) - 1))
                last.then_inc(down_used, 1)

            for t in range(T):
                turn(0, 0, t)

            def batch(b, p, first, last, with_lo):
                for i in range(IT):
                    inner_of(b, p, i, first, with_lo)
                    if i > 0:
                        down_of(b, p, i - 1, first, with_lo)
                if not last:
                    for t in range(T):
                        turn(b + 1, 1 - p, t)
                down_of(b, p, IT - 1, first, with_lo)

            def batches_after_first(with_lo):
                with pe.Fori(0, (B - 2) // 2) as i:
                    batch(i * 2 + 1, 1, False, False, with_lo)
                    batch(i * 2 + 2, 0, False, False, with_lo)
                batch(B - 1, 1, False, True, with_lo)

            batch(0, 0, True, False, True)
            pe.wait_ge(lo_step, 4)
            lo_count = pe.value_load(lo_counts[0:1, 0:1], min_val=0, max_val=1)
            with pe.If(lo_count > 0):
                batches_after_first(True)
            with pe.Else():
                batches_after_first(False)


def four_blocks(nc, x_in, factors, bias, norm_scale, split_scale, wq_t, wk_t, wv_t, wo_t,
                gate_t, up_t, down_t, gate_s, up_s, down_s, out):
    x_mixed = nc.dram_tensor("x_mixed", [B, N, N], F32).ap()
    x_attended = nc.dram_tensor("x_attended", [B, N, N], F32).ap()

    with ExitStack() as stack:
        s = Shared()
        s.stack = stack
        prepare(nc, s)
        with ExitStack() as resident:
            s.x = resident.enter_context(nc.sbuf_tensor("x_resident", [P, B * T, N], F32))
            s.factor_sum = resident.enter_context(nc.sbuf_tensor("factor_sum", [P, T, N], F32))
            column_attention(nc, s, x_in, factors)
            linear_map(nc, s, bias, x_mixed)
        grouped_attention(nc, s, norm_scale, split_scale, wq_t, wk_t, wv_t, wo_t, x_mixed, x_attended)
        gated_ffn(nc, s, gate_t, up_t, down_t, gate_s, up_s, down_s, x_attended, out)


def kernel(L0_attn_x, L0_ffn_factors, L0_ffn_bias, L1_attn_norm_scale, L1_attn_split_scale,
           L1_attn_Wq, L1_attn_Wk, L1_attn_Wv, L1_attn_Wo,
           L1_ffn_gate_w, L1_ffn_up_w, L1_ffn_down_w, L1_ffn_gate_s, L1_ffn_up_s, L1_ffn_down_s):
    import numpy as np
    import concourse.bacc as bacc
    from concourse.bass_utils import run_bass_kernel_spmd

    def per_partition(v):
        return v.reshape(-1, P).T

    def inner_tiles(w):
        return w.reshape(IT, P, T, P).transpose(0, 3, 2, 1).reshape(IT, P, N)

    arrays = {
        "x": L0_attn_x, "factors": L0_ffn_factors, "bias": L0_ffn_bias,
        "norm_scale": per_partition(L1_attn_norm_scale), "split_scale": per_partition(L1_attn_split_scale),
        "wq_t": L1_attn_Wq.T, "wk_t": L1_attn_Wk.T, "wv_t": L1_attn_Wv.T, "wo_t": L1_attn_Wo.T,
        "gate_t": inner_tiles(L1_ffn_gate_w), "up_t": inner_tiles(L1_ffn_up_w),
        "down_t": L1_ffn_down_w.T.reshape(IT, P, N),
        "gate_s": per_partition(L1_ffn_gate_s), "up_s": per_partition(L1_ffn_up_s), "down_s": L1_ffn_down_s,
    }
    arrays = {name: np.ascontiguousarray(a) for name, a in arrays.items()}
    nc = bacc.Bacc("TRN2", target_bir_lowering=False, num_devices=1)
    args = [nc.dram_tensor(name, a.shape, F32, kind="ExternalInput").ap() for name, a in arrays.items()]
    out = nc.dram_tensor("out", (B, N, N), F32, kind="ExternalOutput")
    four_blocks(nc, *args, out.ap())
    result = run_bass_kernel_spmd(nc, [arrays], core_ids=[0])
    return result.results[0]["out"]
```

```python
from contextlib import ExitStack

import concourse.bass as bass
from concourse import mybir

P = 128
B = 8
N = 512
T = N // P
HEADS = 8
GROUPS = 2
DH = 64
HPG = HEADS // GROUPS
INTER = 1408
IT = INTER // P
RANK = 8
EPS = 1e-5
EPS_RMS = 1e-8

F32 = mybir.dt.float32
F32R = mybir.dt.float32r
I32 = mybir.dt.int32
ALU = mybir.AluOpType
ACT = mybir.ActivationFunctionType
AX = mybir.AxisListType.X


def tile_of(t, i):
    if isinstance(i, int):
        return t[:, i, :]
    return t[:, bass.ds(i, 1), :].rearrange("p a n -> p (a n)")


def rows_of(dram, b):
    if isinstance(b, int):
        return dram[b, :, :].rearrange("(t p) n -> p t n", p=P)
    return dram[bass.ds(b, 1), :, :].rearrange("a (t p) n -> p (a t) n", p=P)


def blocks_of(row):
    return row.rearrange("p (t c) -> p t c", t=T)


def products(nc, out, pairs):
    for n, (lhsT, rhs) in enumerate(pairs):
        last = nc.tensor.matmul(out, lhsT, rhs, start=(n == 0), stop=(n == len(pairs) - 1))
    return last


def wait_alone(eng, s, sem, value):
    eng.wait_ge(sem, value)
    if not isinstance(value, int):
        eng.sem_inc(s.waits_passed, 1)


def over_batches(eng, body):
    body(0, 0, True, False)
    with eng.Fori(0, (B - 2) // 2) as i:
        body(i * 2 + 1, 1, False, False)
        body(i * 2 + 2, 0, False, False)
    body(B - 1, 1, False, True)


def over_batches_two_behind(eng, body):
    body(0, 0, 0, False)
    body(1, 1, 1, False)
    with eng.Fori(0, (B - 4) // 2) as i:
        body(i * 2 + 2, 0, 2, False)
        body(i * 2 + 3, 1, 2, False)
    body(B - 2, 0, 2, False)
    body(B - 1, 1, 2, True)


class Shared:
    pass


def row_scales(nc, s, pool, mv, ve, rs, shift, exponent, step, at):
    nc.gpsimd.tensor_scalar(ve, mv[:, :, 1], EPS, None, ALU.add)
    nc.gpsimd.tensor_scalar(shift, mv[:, :, 0], -1.0, None, ALU.mult).then_inc(step, 1)
    pool.wait_ge(step, at + 1)
    nc.gpsimd.tensor_tensor(rs, ve, exponent, ALU.pow).then_inc(step, 1)
    pool.wait_ge(step, at + 2)
    return nc.gpsimd.tensor_tensor(shift, shift, rs, ALU.mult)


class FirstNorm:

    def __init__(self, nc, s, stack, name):
        def sb(what, shape):
            return stack.enter_context(nc.sbuf_tensor(f"{name}_{what}", shape, F32, side="right"))

        def sem(what):
            return s.stack.enter_context(nc.semaphore(f"{name}_{what}"))

        self.bn, self.mv = sb("bn", [P, T, 6]), sb("mv", [P, T, 2])
        self.ve, self.rs, self.shift = sb("ve", [P, T]), sb("rs", [P, T]), sb("shift", [P, T])
        self.own_bn, self.stats = sem("own_bn"), sem("stats")
        self.pool_step, self.scales = sem("pool_step"), sem("scales")

    def statistics(self, nc, dve, tiles):
        for t in range(T):
            last = nc.vector.bn_stats(self.bn[:, t, :], tiles[t])
        last.then_inc(self.own_bn, 1)
        dve.wait_ge(self.own_bn, 1)
        for t in range(T):
            last = nc.vector.bn_aggr(self.mv[:, t, :], self.bn[:, t, :])
        last.then_inc(self.stats, 1)

    def row_scales(self, nc, s, pool):
        pool.wait_ge(self.stats, 1)
        row_scales(nc, s, pool, self.mv, self.ve[:, :], self.rs[:, :], self.shift[:, :],
                   s.minus_half[:, :], self.pool_step, 0).then_inc(self.scales, 1)


def column_attention(nc, s, x_in, factors, following):
    with ExitStack() as ctx:
        def sb(name, shape, dt=F32):
            return ctx.enter_context(nc.sbuf_tensor(name, shape, dt))

        def sem(name):
            return s.stack.enter_context(nc.semaphore("a0_" + name))

        xn = sb("xn", [P, 2, T, N])
        xh = sb("xh", [P, 2, T, N], F32R)
        xl = sb("xl", [P, 2, T, N], F32R)
        xth = sb("xth", [P, 2, T, N], F32R)
        xtl = sb("xtl", [P, 2, T, N], F32R)
        pth = sb("pth", [P, 2, T, N], F32R)
        ptl = sb("ptl", [P, 2, T, N], F32R)
        prob = sb("prob", [P, T, N])
        normed = sb("normed", [P, 2, N])
        factor = sb("factor", [P, T, N])
        bn = sb("bn", [P, T, 6])
        mv = sb("mv", [P, T, 2])
        ve = sb("ve", [P, T])
        rs = sb("rs", [P, T])
        shift = sb("shift", [P, T])
        obn = sb("obn", [P, T, 6])
        omv = sb("omv", [P, T, 2])
        ove = sb("ove", [P, T])
        ors = sb("ors", [P, T])
        oshift = sb("oshift", [P, T])
        neg_max = sb("neg_max", [P, 2 * T])
        row_sum = sb("row_sum", [P, 2 * T])
        inv_sum = sb("inv_sum", [P, 2 * T])

        score = [ctx.enter_context(nc.psum_tensor(f"score{i}", [P, N], F32)) for i in range(2)]
        turned = [ctx.enter_context(nc.psum_tensor(f"turned{i}", [P, N], F32)) for i in range(2)]
        context = [ctx.enter_context(nc.psum_tensor(f"context{i}", [P, N], F32)) for i in range(T)]

        x_loaded = [sem("x_loaded0"), sem("x_loaded1")]
        factor_loaded, factor_used = sem("factor_loaded"), sem("factor_used")
        own_bn, stats = sem("own_bn"), sem("stats")
        pool_step, scales = sem("pool_step"), sem("scales")
        xn_ready, xh_ready, xl_ready = sem("xn_ready"), sem("xh_ready"), sem("xl_ready")
        first_lo = sem("first_lo")
        scored, max_ready, exp_ready = sem("scored"), sem("max_ready"), sem("exp_ready")
        inv_ready, prob_ready = sem("inv_ready"), sem("prob_ready")
        turn_ready, hi_ready, lo_ready = sem("turn_ready"), sem("hi_ready"), sem("lo_ready")
        ctx_ready, own_obn, ostats, opool, oscales = (
            sem("ctx_ready"), sem("own_obn"), sem("ostats"), sem("opool"), sem("oscales"))
        ctx_normed, added = sem("ctx_normed"), sem("added")
        last_added = sem("last_added")

        block = ctx.enter_context(nc.Block())

        @block.sync
        def _(sp):
            def load_x(b, p):
                dst = s.x[:, b * T:(b + 1) * T, :] if isinstance(b, int) else s.x[:, bass.ds(b * T, T), :]
                sp.dma_start(dst, rows_of(x_in, b)).then_inc(x_loaded[p], 16)

            load_x(0, 0)

            def load(b, p, first, last):
                if not last:
                    sp.wait_ge(x_loaded[p], (b - p) * 8 + 16)
                    load_x(b + 1, 1 - p)
                if first:
                    sp.dma_start(s.factor_sum[:, :, :], rows_of(factors, b)).then_inc(factor_loaded, 16)
                else:
                    sp.wait_ge(factor_loaded, b * 16)
                    sp.wait_ge(factor_used, b)
                    sp.dma_start(factor[:, :, :], rows_of(factors, b)).then_inc(factor_loaded, 16)

            over_batches(sp, load)

        @block.gpsimd
        def _(pool):
            pool.sem_inc(added, 2)

            def scales_of(b):
                wait_alone(pool, s, stats, b + 1)
                row_scales(nc, s, pool, mv, ve[:, :], rs[:, :], shift[:, :], s.minus_half[:, :],
                           pool_step, b * 2).then_inc(scales, 1)

            def lo_of(b, p, t):
                pool.wait_ge(xh_ready, b * T + t + 1)
                nc.gpsimd.tensor_tensor(xl[:, p, t, :], xn[:, p, t, :], xh[:, p, t, :].bitcast(F32),
                                        ALU.subtract).then_inc(xl_ready, 1)

            def normalise(b, p, t):
                wait_alone(pool, s, inv_ready, b * T + t + 1)
                nc.gpsimd.tensor_scalar(prob[:, t, :], prob[:, t, :], inv_sum[:, p * T + t:p * T + t + 1],
                                        1.0, ALU.mult, ALU.mult).then_inc(prob_ready, 1)

            def output_scales(b):
                wait_alone(pool, s, ostats, b + 1)
                row_scales(nc, s, pool, omv, ove[:, :], ors[:, :], oshift[:, :], s.minus_half[:, :],
                           opool, b * 2).then_inc(oscales, 1)

            def add(b, t):
                pool.wait_ge(ctx_normed, b * T + t + 1 + T)
                x = tile_of(s.x, b * T + t)
                nc.gpsimd.tensor_tensor(x, x, normed[:, t % 2, :], ALU.add).then_inc(added, 1)

            scales_of(0)
            for t in range(T // 2):
                lo_of(0, 0, t)
            pool.sem_inc(xl_ready, T // 2)

            def body(b, p, before, last):
                if before == 2:
                    output_scales(b - 2)
                for t in range(T):
                    normalise(b, p, t)
                    if t == 0 and not last:
                        scales_of(b + 1)
                    if before == 2:
                        add(b - 2, t)
                if not last:
                    for t in range(T):
                        lo_of(b + 1, 1 - p, t)

            over_batches_two_behind(pool, body)
            output_scales(B - 2)
            for t in range(T):
                add(B - 2, t)
            following.row_scales(nc, s, pool)
            output_scales(B - 1)

        @block.scalar
        def _(act):
            act.sem_inc(ctx_normed, T)

            def exp(b, p, t):
                act.wait_ge(max_ready, b * T + t + 1)
                if not (isinstance(b, int) and b == 0):
                    act.wait_ge(turn_ready, b * 8 - 4 + t + 1 )
                nc.scalar.activation(prob[:, t, :], score[t % 2][:, :], ACT.Exp,
                                     bias=neg_max[:, p * T + t:p * T + t + 1], scale=1.0,
                                     accum_out=row_sum[:, p * T + t:p * T + t + 1]).then_inc(exp_ready, 1)

            def hi_of(b, p, g, first):
                act.wait_ge(turn_ready, b * 8 + g + 1)
                if not first and g % T == 0:
                    act.wait_ge(ctx_ready, b * T)
                dst = (xth if g < T else pth)[:, p, :, (g % T) * P:(g % T + 1) * P]
                nc.scalar.copy(dst, blocks_of(turned[g % 2][:, :])).then_inc(hi_ready, 1)

            def norm(b, t):
                if t == 0:
                    act.wait_ge(oscales, b + 1)
                if isinstance(b, int) and b == B - 1 and t >= 2:
                    act.wait_ge(last_added, t - 1)
                else:
                    act.wait_ge(added, b * T + t + 1)
                nc.scalar.activation(normed[:, t % 2, :], context[t][:, :], ACT.Identity,
                                     bias=oshift[:, t:t + 1], scale=ors[:, t:t + 1]).then_inc(ctx_normed, 1)

            def body(b, p, before, last):
                for t in range(T):
                    hi_of(b, p, t, before == 0)
                    exp(b, p, t)
                    if before == 2:
                        norm(b - 2, t)
                for g in range(T, 2 * T):
                    hi_of(b, p, g, before == 0)

            over_batches_two_behind(act, body)
            for b in (B - 2, B - 1):
                for t in range(T):
                    norm(b, t)

        @block.vector
        def _(dve):
            def stats_of(b, p):
                dve.wait_ge(x_loaded[p], (b - p) * 8 + 16)
                for t in range(T):
                    last = nc.vector.bn_stats(bn[:, t, :], tile_of(s.x, b * T + t))
                last.then_inc(own_bn, 1)
                wait_alone(dve, s, own_bn, b + 1)
                for t in range(T):
                    last = nc.vector.bn_aggr(mv[:, t, :], bn[:, t, :])
                last.then_inc(stats, 1)

            def normalised(b, p, tiles):
                if tiles[0] == 0:
                    dve.wait_ge(scales, b + 1)
                for t in tiles:
                    nc.vector.tensor_scalar(xn[:, p, t, :], tile_of(s.x, b * T + t), mv[:, t, 0:1],
                                            rs[:, t:t + 1], ALU.subtract, ALU.mult).then_inc(xn_ready, 1)

            def hi_of_xn(b, p):
                for t in range(T):
                    dve.wait_ge(xn_ready, b * T + t + 1)
                    nc.vector.tensor_copy(xh[:, p, t, :], xn[:, p, t, :]).then_inc(xh_ready, 1)

            def maximum(b, p, t):
                dve.wait_ge(scored, b * T + t + 1)
                nc.vector.reduce_max(neg_max[:, p * T + t:p * T + t + 1], score[t % 2][:, :], AX,
                                     negate=True).then_inc(max_ready, 1)

            def inverse(b, p, t):
                dve.wait_ge(exp_ready, b * T + t + 1)
                nc.vector.reciprocal(inv_sum[:, p * T + t:p * T + t + 1],
                                     row_sum[:, p * T + t:p * T + t + 1]).then_inc(inv_ready, 1)

            def lo_of(b, p, g):
                dve.wait_ge(hi_ready, b * 8 + g + 1)
                at = slice((g % T) * P, (g % T + 1) * P)
                hi, lo = ((xth, xtl) if g < T else (pth, ptl))
                nc.vector.tensor_tensor(lo[:, p, :, at], blocks_of(turned[g % 2][:, :]),
                                        hi[:, p, :, at].bitcast(F32), ALU.subtract).then_inc(lo_ready, 1)

            def output_stats(b, t):
                dve.wait_ge(ctx_ready, (b + 1) * T + t + 1)
                last = nc.vector.bn_stats(obn[:, t, :], context[t][:, :])
                if t == T - 1:
                    last.then_inc(own_obn, 1)
                    wait_alone(dve, s, own_obn, b + 1)
                    for t in range(T):
                        last = nc.vector.bn_aggr(omv[:, t, :], obn[:, t, :])
                    last.then_inc(ostats, 1)

            stats_of(0, 0)
            normalised(0, 0, range(T))
            hi_of_xn(0, 0)
            for t in range(T // 2, T):
                dve.wait_ge(xh_ready, t + 1)
                nc.vector.tensor_tensor(xl[:, 0, t, :], xn[:, 0, t, :], xh[:, 0, t, :].bitcast(F32),
                                        ALU.subtract).then_inc(first_lo, 1)

            def body(b, p, first, last):
                for t in range(T):
                    maximum(b, p, t)
                    lo_of(b, p, t)
                    if t == 0 and not last:
                        stats_of(b + 1, 1 - p)
                    if t == 1 and first:
                        dve.wait_ge(factor_loaded, 16)
                        dve.sem_inc(factor_used, 1)
                    if t == 1 and not first:
                        dve.wait_ge(factor_loaded, b * 16 + 16)
                        dve.wait_ge(factor_used, b)
                        nc.vector.tensor_tensor(s.factor_sum[:, :, :], s.factor_sum[:, :, :], factor[:, :, :],
                                                ALU.add).then_inc(factor_used, 1)
                    if t >= 2 and not last:
                        normalised(b + 1, 1 - p, (0, 1) if t == 2 else (2, 3))
                    inverse(b, p, t)
                if not last:
                    hi_of_xn(b + 1, 1 - p)
                for t in range(T):
                    if not first:
                        output_stats(b - 1, t)
                    lo_of(b, p, T + t)

            over_batches(dve, body)
            dve.wait_ge(added, T + 2)
            following.statistics(nc, dve, [s.x[:, t, :] for t in range(T)])
            for t in range(T):
                output_stats(B - 1, t)
            for t in range(T):
                dve.wait_ge(ctx_normed, B * T + t + 1)
                x = tile_of(s.x, (B - 1) * T + t)
                nc.vector.tensor_tensor(x, x, normed[:, t % 2, :], ALU.add).then_inc(last_added, 1)

        @block.tensor
        def _(pe):
            def scores(b, p, t, first):
                if t == 0:
                    pe.wait_ge(xh_ready, (b + 1) * T)
                    pe.wait_ge(xl_ready, (b + 1) * T)
                    if first:
                        pe.wait_ge(first_lo, T // 2)
                if not (first and t < 2):
                    pe.wait_ge(exp_ready, b * T + t - 1)
                at = slice(t * P, (t + 1) * P)
                products(nc, score[t % 2][:, :],
                         [(l[:, p, k, at], r[:, p, k, :])
                          for k in range(T) for l, r in ((xh, xh), (xl, xh), (xh, xl))]).then_inc(scored, 1)

            def turn(b, p, g, first):
                if g < T:
                    pe.wait_ge(xn_ready, b * T + g + 1)
                else:
                    pe.wait_ge(prob_ready, b * T + g - T + 1)
                if not (first and g < 2):
                    pe.wait_ge(lo_ready, b * 8 + g - 1)
                for k in range(T):
                    at = slice(k * P, (k + 1) * P)
                    src = xn[:, p, g, at] if g < T else prob[:, g - T, at]
                    last = nc.tensor.transpose(turned[g % 2][:, at], src, s.identity[:, :])
                last.then_inc(turn_ready, 1)

            def contexts(b, p, t):
                if t == 0:
                    pe.wait_ge(lo_ready, (b + 1) * 8)
                pe.wait_ge(ctx_normed, b * T + t + 1)
                at = slice(t * P, (t + 1) * P)
                products(nc, context[t][:, :],
                         [(l[:, p, k, at], r[:, p, k, :])
                          for k in range(T) for l, r in ((xth, pth), (xtl, pth), (xth, ptl))]).then_inc(ctx_ready, 1)

            pe.sem_inc(ctx_ready, T)

            def body(b, p, first, last):
                for t in range(T):
                    scores(b, p, t, first)
                    turn(b, p, t, first)
                for t in range(T):
                    if not first:
                        contexts(b - 1, 1 - p, t)
                    turn(b, p, T + t, first)

            over_batches(pe, body)
            for t in range(T):
                contexts(B - 1, (B - 1) % 2, t)


def linear_map(nc, s, bias, x_out, fetch, norm_in, following):
    with ExitStack() as ctx:
        def sb(name, shape, dt=F32):
            return ctx.enter_context(nc.sbuf_tensor(name, shape, dt))

        def sem(name):
            return s.stack.enter_context(nc.semaphore("f0_" + name))

        mh = sb("mh", [P, T, N], F32R)
        ml = sb("ml", [P, T, N], F32R)
        bias_rows = sb("bias_rows", [P, N])
        xn = sb("xn2", [P, 2, T, N])
        xth = sb("xth2", [P, 2, T, N], F32R)
        xtl = sb("xtl2", [P, 2, T, N], F32R)
        mixed = sb("mixed", [P, T, N])
        normed = sb("normed2", [P, 2, N])
        bn, mv, ve, rs, shift = norm_in.bn, norm_in.mv, norm_in.ve, norm_in.rs, norm_in.shift
        obn = sb("obn2", [P, T, 6])
        omv = sb("omv2", [P, T, 2])
        ove = sb("ove2", [P, T])
        ors = sb("ors2", [P, T])
        oshift = sb("oshift2", [P, T])
        turned = [ctx.enter_context(nc.psum_tensor(f"turned2_{i}", [P, N], F32)) for i in range(2)]
        mix = [ctx.enter_context(nc.psum_tensor(f"mix{i}", [P, N], F32)) for i in range(T)]

        bias_loaded, weights = sem("bias_loaded"), sem("weights")
        own_bn, stats, pool_step, scales = norm_in.own_bn, norm_in.stats, norm_in.pool_step, norm_in.scales
        xn_ready, turn_ready, hi_ready, lo_ready = (
            sem("xn_ready"), sem("turn_ready"), sem("hi_ready"), sem("lo_ready"))
        mix_ready, mixed_ready, own_obn, ostats, opool, oscales = (
            sem("mix_ready"), sem("mixed_ready"), sem("own_obn"), sem("ostats"), sem("opool"), sem("oscales"))
        normed_ready, added = sem("normed_ready"), sem("added")
        last_added = sem("last_added")
        first_stored, stored, last_stored = sem("first_stored"), sem("stored"), sem("last_stored")
        s.mixed_stored = last_stored

        block = ctx.enter_context(nc.Block())

        @block.sync
        def _(sp):
            sp.dma_start(bias_rows[:, :], bias.partition_broadcast(P)).then_inc(bias_loaded, 16)
            fetch(sp, "start")

            def store(b, p, first, last):
                if last:
                    sp.wait_ge(first_stored, 16)
                    fetch(sp, "stored")
                    sp.wait_ge(last_added, T)
                else:
                    sp.wait_ge(added, (b + 1) * T + 2)
                src = s.x[:, b * T:(b + 1) * T, :] if isinstance(b, int) else s.x[:, bass.ds(b * T, T), :]
                sp.dma_start(rows_of(x_out, b), src).then_inc(
                    first_stored if first else last_stored if last else stored, 16)

            over_batches(sp, store)
            sp.wait_ge(stored, (B - 2) * 16)

        @block.gpsimd
        def _(pool):
            pool.sem_inc(added, 2)

            def scales_of(b):
                if not (isinstance(b, int) and b == 0):
                    pool.wait_ge(xn_ready, b * T)
                wait_alone(pool, s, stats, b + 1)
                row_scales(nc, s, pool, mv, ve[:, :], rs[:, :], shift[:, :], s.minus_half[:, :],
                           pool_step, b * 2).then_inc(scales, 1)

            def output_scales(b):
                wait_alone(pool, s, ostats, b + 1)
                row_scales(nc, s, pool, omv, ove[:, :], ors[:, :], oshift[:, :], s.minus_half[:, :],
                           opool, b * 2).then_inc(oscales, 1)

            def add(b, t):
                pool.wait_ge(normed_ready, b * T + t + 1 + T)
                x = tile_of(s.x, b * T + t)
                nc.gpsimd.tensor_tensor(x, x, normed[:, t % 2, :], ALU.add).then_inc(added, 1)

            def body(b, p, before, last):
                if before == 2:
                    output_scales(b - 2)
                    add(b - 2, 0)
                    add(b - 2, 1)
                if not last:
                    scales_of(b + 1)
                if before == 2:
                    add(b - 2, 2)
                    add(b - 2, 3)

            over_batches_two_behind(pool, body)
            output_scales(B - 2)
            for t in range(T):
                add(B - 2, t)
            output_scales(B - 1)

        @block.scalar
        def _(act):
            act.sem_inc(normed_ready, T)

            def normalised(b, p):
                act.wait_ge(scales, b + 1)
                if not (isinstance(b, int) and b < 2):
                    act.wait_ge(turn_ready, (b - 1) * T)
                for t in range(T):
                    nc.scalar.activation(xn[:, p, t, :], tile_of(s.x, b * T + t), ACT.Identity,
                                         bias=shift[:, t:t + 1], scale=rs[:, t:t + 1]).then_inc(xn_ready, 1)

            def hi_of(b, p, t, first):
                act.wait_ge(turn_ready, b * T + t + 1)
                if not first and t == 0:
                    act.wait_ge(mix_ready, b * T)
                nc.scalar.copy(xth[:, p, :, t * P:(t + 1) * P],
                               blocks_of(turned[t % 2][:, :])).then_inc(hi_ready, 1)

            def norm(b, t):
                if t == 0:
                    act.wait_ge(oscales, b + 1)
                if isinstance(b, int) and b == B - 1 and t >= 2:
                    act.wait_ge(last_added, t - 1)
                else:
                    act.wait_ge(added, b * T + t + 1)
                nc.scalar.activation(normed[:, t % 2, :], mixed[:, t, :], ACT.Identity,
                                     bias=oshift[:, t:t + 1], scale=ors[:, t:t + 1]).then_inc(normed_ready, 1)

            normalised(0, 0)

            def body(b, p, before, last):
                for t in range(T):
                    hi_of(b, p, t, before == 0)
                    if before == 2:
                        norm(b - 2, t)
                if before == 0:
                    nc.scalar.copy(mh[:, :, :], s.factor_sum[:, :, :]).then_inc(weights, 1)
                if not last:
                    normalised(b + 1, 1 - p)

            over_batches_two_behind(act, body)
            for b in (B - 2, B - 1):
                for t in range(T):
                    norm(b, t)

        @block.vector
        def _(dve):
            def tile_stats(b, t):
                if t == 0 and not (isinstance(b, int) and b == 0):
                    dve.wait_ge(stats, b)
                tile = nc.vector.bn_stats(bn[:, t, :], tile_of(s.x, b * T + t))
                if t == T - 1:
                    tile.then_inc(own_bn, 1)

            def stats_of(b):
                if not (isinstance(b, int) and b == 0):
                    dve.wait_ge(scales, b)
                wait_alone(dve, s, own_bn, b + 1)
                for t in range(T):
                    last = nc.vector.bn_aggr(mv[:, t, :], bn[:, t, :])
                last.then_inc(stats, 1)

            def lo_of(b, p, t):
                dve.wait_ge(hi_ready, b * T + t + 1)
                at = slice(t * P, (t + 1) * P)
                nc.vector.tensor_tensor(xtl[:, p, :, at], blocks_of(turned[t % 2][:, :]),
                                        xth[:, p, :, at].bitcast(F32), ALU.subtract).then_inc(lo_ready, 1)

            def mixed_of(b, t):
                if t == 0:
                    dve.wait_ge(bias_loaded, 16)
                dve.wait_ge(mix_ready, (b + 1) * T + t + 1)
                dve.wait_ge(normed_ready, b * T + t + 1)
                nc.vector.scalar_tensor_tensor(out=mixed[:, t, :], in0=mix[t][:, :], scalar=RANK ** -0.5,
                                               in1=bias_rows[:, :], op0=ALU.mult, op1=ALU.add).then_inc(mixed_ready, 1)

            def tile_output_stats(b, t):
                dve.wait_ge(mixed_ready, b * T + t + 1 + T)
                tile = nc.vector.bn_stats(obn[:, t, :], mixed[:, t, :])
                if t == T - 1:
                    tile.then_inc(own_obn, 1)

            def output_stats(b):
                wait_alone(dve, s, own_obn, b + 1)
                for t in range(T):
                    last = nc.vector.bn_aggr(omv[:, t, :], obn[:, t, :])
                last.then_inc(ostats, 1)

            dve.sem_inc(mixed_ready, T)

            def body(b, p, first, last):
                for t in range(T):
                    lo_of(b, p, t)
                    if t < 2 and not last:
                        tile_stats(b + 1, 2 * t)
                        tile_stats(b + 1, 2 * t + 1)
                        if t == 1:
                            stats_of(b + 1)
                    if not first:
                        mixed_of(b - 1, t)
                        tile_output_stats(b - 1, t)
                if first:
                    dve.wait_ge(weights, 1)
                    nc.vector.tensor_tensor(ml[:, :, :], s.factor_sum[:, :, :], mh[:, :, :].bitcast(F32),
                                            ALU.subtract).then_inc(weights, 1)
                if not first:
                    output_stats(b - 1)

            over_batches(dve, body)
            dve.wait_ge(added, T + 2)
            following.statistics(nc, dve, [s.x[:, t, :] for t in range(T)])
            for t in range(T):
                mixed_of(B - 1, t)
                tile_output_stats(B - 1, t)
            output_stats(B - 1)
            for t in range(T):
                dve.wait_ge(normed_ready, B * T + t + 1)
                x = tile_of(s.x, (B - 1) * T + t)
                nc.vector.tensor_tensor(x, x, normed[:, t % 2, :], ALU.add).then_inc(last_added, 1)

        @block.tensor
        def _(pe):
            def turn(b, p, t, first):
                pe.wait_ge(xn_ready, b * T + t + 1)
                if not (first and t < 2):
                    pe.wait_ge(lo_ready, b * T + t - 1)
                for k in range(T):
                    at = slice(k * P, (k + 1) * P)
                    last = nc.tensor.transpose(turned[t % 2][:, at], xn[:, p, t, at], s.identity[:, :])
                last.then_inc(turn_ready, 1)

            def mixes(b, p, t):
                if t == 0:
                    pe.wait_ge(weights, 2)
                    pe.wait_ge(lo_ready, (b + 1) * T)
                pe.wait_ge(mixed_ready, b * T + t + 1)
                at = slice(t * P, (t + 1) * P)
                products(nc, mix[t][:, :],
                         [(l[:, p, k, at], r[:, k, :])
                          for k in range(T) for l, r in ((xth, mh), (xtl, mh), (xth, ml))]).then_inc(mix_ready, 1)

            pe.sem_inc(mix_ready, T)

            def body(b, p, first, last):
                for t in range(T):
                    turn(b, p, t, first)
                    if not first:
                        mixes(b - 1, 1 - p, t)

            over_batches(pe, body)
            for t in range(T):
                mixes(B - 1, (B - 1) % 2, t)


def prepare(nc, s):
    s.identity = s.stack.enter_context(nc.sbuf_tensor("identity", [P, P], F32))
    s.minus_half = s.stack.enter_context(nc.sbuf_tensor("minus_half", [P, T], F32))
    s.minus_one = s.stack.enter_context(nc.sbuf_tensor("minus_one", [P, T], F32))
    s.eps_rms = s.stack.enter_context(nc.sbuf_tensor("eps_rms", [P, T], F32))
    s.waits_passed = s.stack.enter_context(nc.semaphore("waits_passed"))
    zeroed = s.stack.enter_context(nc.semaphore("identity_zeroed"))
    with nc.Block() as block:
        @block.gpsimd
        def _(pool):
            nc.gpsimd.memset(s.minus_half[:, :], -0.5)
            nc.gpsimd.memset(s.minus_one[:, :], -1.0)
            nc.gpsimd.memset(s.eps_rms[:, :], EPS_RMS)
            nc.gpsimd.memset(s.identity[:, :], 0.0).then_inc(zeroed, 1)
            pool.wait_ge(zeroed, 1)
            nc.gpsimd.affine_select(out=s.identity[:, :], in_=s.identity[:, :], compare_op=ALU.not_equal,
                                    fill=1.0, base=0, pattern=[[-1, P]], channel_multiplier=1)


HALF = (slice(0, DH), slice(DH, P))
UNITS = HEADS * T
TURN_LAG = 4
OUT_LAG = 9
SUM_LAG = OUT_LAG + 2

NAMES = ["q1", "q2", "q3", "h0", "h1", "wo0", "wo1", "h2", "h3", "wo2", "wo3", "k", "v", "q0"]
SPLIT = [name for name in NAMES if name[0] != "w"]


STATS = (0, 1, 2, 2)
SCALES = (3, 4)
H = (5, 6, 10, 11)
CONVERT = (20, 24, 32, 39)
SHARE, SHARE_BESIDE_OUT = 8, 4


def side_schedule():
    shares, end = [], {}
    waiting = [(name, {"h": 1, "v": 3 * T * T}.get(name[0], 3 * T)) for name in NAMES]
    at = 0
    for u in range(UNITS):
        shares.append([])
        room = SHARE_BESIDE_OUT if (u - OUT_LAG) % T < 2 else SHARE
        while waiting and room > 0:
            name, count = waiting[0]
            cost = {"h": 2, "v": 0.5}.get(name[0], 1)
            i = NAMES.index(name)
            earliest = [end[n] + (2 if n[0] == "w" else 3) for n in NAMES[i - 2:i - 1] if n in end]
            earliest += {"wo0": [CONVERT[-1] - UNITS + 2], "k": [end.get("h3", 0) + 3],
                         "h0": [H[0] + 2], "h1": [H[1] + 2]}.get(name, [])
            if at == 0 and earliest and max(earliest) > u:
                break
            step = min(count - at, max(1, int(room / cost)))
            shares[u].append((name, at, at + step, at + step == count))
            room -= step * cost
            at += step
            if at == count:
                end[name] = u
                waiting.pop(0)
                at = 0
    assert not waiting
    return shares, end


SHARES, END = side_schedule()
AHEAD = sum(name[0] in "hkv" or name == "q0" for name in NAMES)
WO = [END[f"wo{t}"] for t in range(T)]
RESIDUAL = [at - 1 for at in WO]
NORM = [WO[-1] + 4 + t for t in range(T)]
ADD = [at + 1 for at in NORM]


def side_at(name):
    return (AHEAD + SPLIT.index(name)) % 2 if name in SPLIT else (AHEAD + NAMES.index(name) + T) % 2


def side_use(b, name):
    if isinstance(b, int) and b <= 0:
        return AHEAD + b * len(SPLIT) + SPLIT.index(name)
    j = NAMES.index(name)
    if isinstance(b, int) and b >= B - 1 and name[0] == "w":
        missing = [n for n in NAMES[:j] if n[0] != "w" and (b == B or n[0] != "q")]
        j -= len(missing) + (AHEAD if b == B else 0)
    return b * len(NAMES) + (AHEAD - T + j)


def side_split(b, name):
    return b * len(SPLIT) + (AHEAD + SPLIT.index(name) + 1)


def side_works(u, first, last, drain):
    return [w for w in SHARES[u] if side_runs(w[0], first, last, drain)]


def side_done(u, first, last, drain, lag):
    return [name for name in NAMES if END[name] + lag == u and side_runs(name, first, last, drain)]


def side_runs(name, first, last, drain):
    if name[0] == "w":
        return not first
    return not drain and (not last or name in ("q1", "q2", "q3"))


def attention_fetch(nc, s, stack, norm_scale, split_scale, wq_t, wk_t, wv_t, wo_t, x_in):
    def sb(name, shape):
        return stack.enter_context(nc.sbuf_tensor("g_" + name, shape, F32, side="right"))

    s.prob = sb("prob", [P, T, N])
    s.total = sb("total", [P, T, N])
    s.out_sum = sb("out_sum", [P, T, N])
    s.feature = sb("feature", [P, 3, T])
    s.w_loaded = s.stack.enter_context(nc.semaphore("a1_w_loaded"))
    s.x_first_loaded = s.stack.enter_context(nc.semaphore("a1_x_first_loaded"))

    def fetch(sp, when):
        if when == "start":
            for dst, src in ((s.prob[:, :, :], wq_t), (s.total[:, :, :], wo_t),
                             (blocks_of(s.out_sum[:, 0, :]), wk_t), (blocks_of(s.out_sum[:, 1, :]), wv_t)):
                sp.dma_start(dst, src.rearrange("(k p) n -> p k n", p=P)).then_inc(s.w_loaded, 16)
            for dst, src in ((s.feature[:, 0, :], norm_scale), (s.feature[:, 1, :], split_scale)):
                sp.dma_start(dst, src).then_inc(s.w_loaded, 16)
        else:
            sp.dma_start(s.x_pair[:, 0, :, :], rows_of(x_in, 0)).then_inc(s.x_first_loaded, 16)

    return fetch


def grouped_attention(nc, s, x_in, x_out, fetch, norm_in, following):
    with ExitStack() as ctx:
        def sb(name, shape, dt=F32):
            return ctx.enter_context(nc.sbuf_tensor("g_" + name, shape, dt))

        def sem(name):
            return s.stack.enter_context(nc.semaphore("a1_" + name))

        def bank(name):
            return ctx.enter_context(nc.psum_tensor("g_" + name, [P, N], F32))

        KV = GROUPS * DH
        wqh, wql = sb("wqh", [P, T, N], F32R), sb("wql", [P, T, N], F32R)
        wkh, wkl = sb("wkh", [P, T, KV], F32R), sb("wkl", [P, T, KV], F32R)
        wvh, wvl = sb("wvh", [P, T, KV], F32R), sb("wvl", [P, T, KV], F32R)
        woh, wol = sb("woh", [P, T, N], F32R), sb("wol", [P, T, N], F32R)
        x, prob, total, out_sum, feature = s.x_pair, s.prob, s.total, s.out_sum, s.feature
        hth, htl = sb("hth", [P, T, N], F32R), sb("htl", [P, T, N], F32R)
        res = sb("res", [P, T, N])
        h = sb("h", [P, 2, N])
        q = sb("q", [P, HEADS, N], F32R)
        kh, kl = sb("kh", [P, 2, GROUPS, N], F32R), sb("kl", [P, 2, GROUPS, N], F32R)
        v = sb("v", [P, 2, T, GROUPS, 2 * DH], F32R)
        pth, ptl = sb("pth", [P, 2, T, N], F32R), sb("ptl", [P, 2, T, N], F32R)
        v_lo_part = sb("v_lo_part", [DH, 2, N])
        oh, ol = sb("oh", [P, T, N], F32R), sb("ol", [P, T, N], F32R)
        xn = sb("xn", [P, 2, N])
        bn, mv = norm_in.bn, norm_in.mv
        var, power, exponents = sb("var", [P, 2, T]), sb("power", [P, 2, T]), sb("exponents", [P, 2, T])
        shift = sb("shift", [P, T])
        kept = sb("kept", [P, 2, 2, T])
        rms, inv_rms = sb("rms", [P, T]), sb("inv_rms", [P, T])
        hs, hshift = sb("hs", [P, T]), sb("hshift", [P, T])
        obn, omv = sb("obn", [P, T, 6]), sb("omv", [P, T, 2])
        ove, ors, oshift = sb("ove", [P, T]), sb("ors", [P, T]), sb("oshift", [P, T])
        neg_max, row_sum, inv_sum = sb("neg_max", [P, 4]), sb("row_sum", [P, 4]), sb("inv_sum", [P, 4])

        score = [bank("score0"), bank("score1")]
        turned = [bank("turned0"), bank("turned1")]
        output = [bank("output0"), bank("output1")]
        side = [bank("side0"), bank("side1")]

        scaled, w_hi, w_lo = sem("scaled"), sem("w_hi"), sem("w_lo")
        scaled_step = sem("scaled_step")
        x_loaded = [s.x_first_loaded, sem("x_loaded1")]
        res_loaded, stored = sem("res_loaded"), sem("stored")
        s.attended_stored = stored
        own_bn, stats, pool_step, scales = norm_in.own_bn, norm_in.stats, sem("pool_step"), sem("scales")
        h_ready, kept_ready, exponents_set = sem("h_ready"), sem("kept_ready"), sem("exponents_set")
        side_ready, side_hi, side_free = sem("side_ready"), sem("side_hi"), sem("side_free")
        scored, max_ready, exp_ready = sem("scored"), sem("max_ready"), sem("exp_ready")
        inv_ready, prob_ready = sem("inv_ready"), sem("prob_ready")
        turn_ready, hi_ready, lo_ready = sem("turn_ready"), sem("hi_ready"), sem("lo_ready")
        out_ready, part_ready, sum_ready = sem("out_ready"), sem("part_ready"), sem("sum_ready")
        oh_ready, ol_ready, k_repeated = sem("oh_ready"), sem("ol_ready"), sem("k_repeated")
        xn_ready, total_ready = sem("xn_ready"), sem("total_ready")
        ostats, opool, oscales = sem("ostats"), sem("opool"), sem("oscales")
        normed_ready, added = sem("normed_ready"), sem("added")
        last_added = sem("last_added")

        block = ctx.enter_context(nc.Block())

        def is_first(b):
            return isinstance(b, int) and b == 0

        @block.sync
        def _(sp):
            def store(b):
                if isinstance(b, int) and b == B - 1:
                    sp.wait_ge(last_added, T)
                else:
                    sp.wait_ge(added, (b + 2) * T)
                sp.dma_start(rows_of(x_out, b), res[:, :, :]).then_inc(stored, 16)

            def body(b, p, first, last):
                if not last:
                    if not first:
                        sp.wait_ge(h_ready, b * T)
                        sp.wait_ge(x_loaded[1 - p], (b + 1 - (1 - p)) * 8)
                    sp.dma_start(x[:, 1 - p, :, :], rows_of(x_in, b + 1)).then_inc(x_loaded[1 - p], 16)
                if not first:
                    sp.wait_ge(stored, b * 16)
                    sp.dma_start(res[:, :, :], rows_of(x_in, b - 1)).then_inc(res_loaded, 16)
                    if last:
                        sp.wait_ge(h_ready, B * T)
                        fetch(sp)
                    store(b - 1)

            sp.sem_inc(stored, 16)
            sp.wait_ge(s.mixed_stored, 16)
            over_batches(sp, body)
            sp.wait_ge(stored, B * 16)
            sp.dma_start(res[:, :, :], rows_of(x_in, B - 1)).then_inc(res_loaded, 16)
            store(B - 1)

        @block.gpsimd
        def _(pool):
            pool.sem_inc(added, T)
            pool.sem_inc(ol_ready, T)

            def scales_of(b, p, part):
                at = b * 6
                if part == 0:
                    if not is_first(b):
                        pool.wait_ge(h_ready, b * T)
                        pool.wait_ge(kept_ready, b)
                        if not isinstance(b, int):
                            pool.sem_inc(s.waits_passed, 1)
                    wait_alone(pool, s, stats, b + 1)
                    nc.gpsimd.tensor_scalar(var[:, 0, :], mv[:, :, 1], EPS, None, ALU.add)
                    nc.gpsimd.tensor_copy(var[:, 1, :], mv[:, :, 1])
                    nc.gpsimd.tensor_scalar(shift[:, :], mv[:, :, 0], -1.0, None, ALU.mult).then_inc(pool_step, 1)
                    pool.wait_ge(pool_step, at + 1)
                    nc.gpsimd.tensor_tensor(power[:, :, :], var[:, :, :], exponents[:, :, :],
                                            ALU.pow).then_inc(pool_step, 1)
                    pool.wait_ge(pool_step, at + 2)
                    nc.gpsimd.tensor_tensor(shift[:, :], shift[:, :], power[:, 0, :], ALU.mult)
                elif part == 1:
                    nc.gpsimd.tensor_tensor(rms[:, :], power[:, 1, :], power[:, 0, :], ALU.mult).then_inc(pool_step, 1)
                    pool.wait_ge(pool_step, at + 3)
                    nc.gpsimd.tensor_tensor(rms[:, :], rms[:, :], s.eps_rms[:, :], ALU.add).then_inc(pool_step, 1)
                    pool.wait_ge(pool_step, at + 4)
                    nc.gpsimd.tensor_tensor(inv_rms[:, :], rms[:, :], s.minus_one[:, :],
                                            ALU.pow).then_inc(pool_step, 1)
                    pool.wait_ge(pool_step, at + 5)
                    nc.gpsimd.tensor_tensor(hs[:, :], power[:, 0, :], inv_rms[:, :], ALU.mult).then_inc(pool_step, 1)
                    nc.gpsimd.tensor_tensor(hshift[:, :], shift[:, :], inv_rms[:, :],
                                            ALU.mult).then_inc(scales, 1)

            def keep_scales(b, p):
                if not isinstance(b, int) or b > 1:
                    pool.wait_ge(xn_ready, (b - 1) * T)
                wait_alone(pool, s, scales, b + 1)
                nc.gpsimd.tensor_copy(kept[:, p, 0, :], power[:, 0, :])
                nc.gpsimd.tensor_copy(kept[:, p, 1, :], shift[:, :]).then_inc(kept_ready, 1)

            def normalise(g, u):
                wait_alone(pool, s, inv_ready, g + 1)
                at = u % 4
                nc.gpsimd.tensor_scalar(prob[:, at, :], prob[:, at, :], inv_sum[:, at:at + 1],
                                        1.0, ALU.mult, ALU.mult).then_inc(prob_ready, 1)

            def lo_of_output(b, m):
                pool.wait_ge(oh_ready, b * T + m + 1)
                nc.gpsimd.tensor_tensor(ol[:, m, :], out_sum[:, m, :], oh[:, m, :].bitcast(F32),
                                        ALU.subtract).then_inc(ol_ready, 1)

            def residual(b, p, t):
                if t == 0:
                    pool.wait_ge(res_loaded, b * 16 + 16)
                pool.wait_ge(total_ready, b * T + t + 1)
                wait_alone(pool, s, kept_ready, b + 1)
                nc.gpsimd.tensor_scalar(xn[:, t % 2, :], res[:, t, :], kept[:, p, 0, t:t + 1],
                                        kept[:, p, 1, t:t + 1], ALU.mult, ALU.add).then_inc(xn_ready, 1)

            def output_scales(b):
                wait_alone(pool, s, ostats, b + 1)
                row_scales(nc, s, pool, omv, ove[:, :], ors[:, :], oshift[:, :], s.minus_half[:, :],
                           opool, b * 2).then_inc(oscales, 1)

            def add(b, t):
                pool.wait_ge(normed_ready, b * T + t + 1)
                nc.gpsimd.tensor_tensor(res[:, t, :], res[:, t, :], total[:, t, :],
                                        ALU.add).then_inc(added, 1)

            nc.gpsimd.memset(exponents[:, 0, :], -0.5)
            nc.gpsimd.memset(exponents[:, 1, :], 0.5).then_inc(exponents_set, 1)
            pool.wait_ge(exponents_set, 1)
            for part in range(2):
                scales_of(0, 0, part)
            keep_scales(0, 0)
            pool.wait_ge(w_hi, 3)
            nc.gpsimd.tensor_tensor(wol[:, :, :], total[:, :, :], woh[:, :, :].bitcast(F32), ALU.subtract)

            def step(b, p, u, first, last, drain):
                if u > 0 or not first:
                    if not drain or u == 0:
                        normalise(b * UNITS + u - 1, u + 3)
                for m, at in enumerate(CONVERT):
                    if at + 1 == u and not drain:
                        lo_of_output(b, m)
                    if at + 1 - UNITS == u and not first:
                        lo_of_output(b - 1, m)
                if u in RESIDUAL and not first:
                    residual(b - 1, 1 - p, RESIDUAL.index(u))
                if u == WO[-1] + 2 and not first:
                    output_scales(b - 1)
                if u in ADD and not first:
                    add(b - 1, ADD.index(u))
                if not last and not drain:
                    if u in SCALES:
                        scales_of(b + 1, 1 - p, SCALES.index(u))
                    if u == WO[-1] + 1:
                        keep_scales(b + 1, 1 - p)

            def body(b, p, first, last):
                for u in range(UNITS):
                    step(b, p, u, first, last, False)

            over_batches(pool, body)
            for u in range(WO[-1] + 3):
                if u == WO[1]:
                    following.row_scales(nc, s, pool)
                step(B, 0, u, False, True, True)

        @block.scalar
        def _(act):
            def h_of(b, p, t):
                if t == 0:
                    act.wait_ge(scales, b + 1)
                nc.scalar.activation(h[:, t % 2, :], x[:, p, t, :], ACT.Identity, bias=hshift[:, t:t + 1],
                                     scale=hs[:, t:t + 1]).then_inc(h_ready, 1)

            def hi_of(b, p, name):
                act.wait_ge(side_ready, side_use(b, name) + 1)
                src = side[side_at(name)]
                if name[0] == "h":
                    t = int(name[1])
                    last = nc.scalar.copy(hth[:, :, t * P:(t + 1) * P], blocks_of(src[:, :]))
                elif name[0] == "q":
                    m = int(name[1])
                    for e, half in enumerate(HALF):
                        last = nc.scalar.copy(q[half, 2 * m + e, :], src[half, :])
                elif name == "k":
                    for g in range(GROUPS):
                        for half in HALF:
                            last = nc.scalar.copy(kh[half, 1 - p, g, :], src[HALF[g], :])
                else:
                    last = nc.scalar.copy(v[:, 1 - p, :, :, 0:DH],
                                          src[:, :].rearrange("p (t g d) -> p t g d", t=T, g=GROUPS))
                last.then_inc(side_hi, 1)

            def repeat_k_lo(b, p):
                act.wait_ge(side_free, side_use(b, "k") + 1)
                for g in range(GROUPS):
                    last = nc.scalar.copy(kl[HALF[1 - g], 1 - p, g, :], kl[HALF[g], 1 - p, g, :].bitcast(F32))
                last.then_inc(k_repeated, 1)

            def exp(g, u, first):
                act.wait_ge(max_ready, g + 1)
                if not (first and u < 4):
                    act.wait_ge(turn_ready, g - 3)
                at = u % 4
                nc.scalar.activation(prob[:, at, :], score[u % 2][:, :], ACT.Exp, bias=neg_max[:, at:at + 1],
                                     scale=1.0, accum_out=row_sum[:, at:at + 1]).then_inc(exp_ready, 1)

            def v_lo_of(head, hd):
                act.wait_ge(out_ready, head + 1)
                nc.scalar.copy(v_lo_part[:, hd % 2, :], output[hd % 2][HALF[1], :]).then_inc(part_ready, 1)

            def norm(b, t):
                if t == 0:
                    act.wait_ge(oscales, b + 1)
                nc.scalar.activation(total[:, t, :], total[:, t, :], ACT.Identity,
                                     bias=oshift[:, t:t + 1], scale=ors[:, t:t + 1]).then_inc(normed_ready, 1)

            raw_k, raw_v = blocks_of(out_sum[:, 0, :]), blocks_of(out_sum[:, 1, :])
            act.wait_ge(scaled, 1)
            nc.scalar.copy(wkh[:, :, :], raw_k)
            nc.scalar.copy(wvh[:, :, :], raw_v).then_inc(w_hi, 1)
            act.wait_ge(x_loaded[0], 16)
            h_of(0, 0, 0)
            h_of(0, 0, 1)
            for t in range(T):
                hi_of(-1, 1, f"h{t}")
                if t < 2:
                    h_of(0, 0, t + 2)
            act.wait_ge(scaled, 2)
            nc.scalar.copy(wqh[:, :, :], prob[:, :, :]).then_inc(w_hi, 1)
            hi_of(-1, 1, "k")
            nc.scalar.copy(woh[:, :, :], total[:, :, :]).then_inc(w_hi, 1)
            hi_of(-1, 1, "v")
            hi_of(-1, 1, "q0")
            repeat_k_lo(-1, 1)

            def step(b, p, u, first, last, drain):
                g = b * UNITS + u
                turn_u = u - TURN_LAG
                if not (first and turn_u < 0) and not (drain and turn_u >= 0):
                    if turn_u % T == 0 and not (first and turn_u < 2 * T):
                        act.wait_ge(out_ready, b * HEADS + turn_u // T - 1)
                    act.wait_ge(turn_ready, g - TURN_LAG + 1)
                    at = turn_u % T
                    nc.scalar.copy(pth[:, (turn_u // T) % 2, :, at * P:(at + 1) * P],
                                   blocks_of(turned[turn_u % 2][:, :])).then_inc(hi_ready, 1)
                for name in side_done(u, first, last, drain, 1):
                    if name in SPLIT:
                        hi_of(b, p, name)
                if not drain:
                    exp(g, u, first)
                done = u - OUT_LAG - 1
                if done % T == 0 and not (first and done < 0) and not (drain and done >= 0):
                    v_lo_of(b * HEADS + done // T, done // T)
                if u == END["k"] + 4 and not last and not drain:
                    repeat_k_lo(b, p)
                if u in NORM and not first:
                    norm(b - 1, NORM.index(u))
                if u in H and not last and not drain:
                    h_of(b + 1, 1 - p, H.index(u))

            def body(b, p, first, last):
                for u in range(UNITS):
                    step(b, p, u, first, last, False)

            over_batches(act, body)
            for u in range(NORM[-1] + 1):
                step(B, 0, u, False, True, True)

        @block.vector
        def _(dve):
            def stats_of(b, p, t):
                if t == 0:
                    dve.wait_ge(x_loaded[p], (b - p) * 8 + 16)
                    if not is_first(b):
                        dve.wait_ge(stats, b)
                last = nc.vector.bn_stats(bn[:, t, :], x[:, p, t, :])
                if t == T - 1:
                    last.then_inc(own_bn, 1)
                    if not is_first(b):
                        dve.wait_ge(scales, b)
                    wait_alone(dve, s, own_bn, b + 1)
                    for t in range(T):
                        last = nc.vector.bn_aggr(mv[:, t, :], bn[:, t, :])
                    last.then_inc(stats, 1)

            def lo_of(b, p, name):
                dve.wait_ge(side_hi, side_split(b, name))
                src = side[side_at(name)]
                if name[0] == "h":
                    cols = slice(int(name[1]) * P, (int(name[1]) + 1) * P)
                    last = nc.vector.tensor_tensor(htl[:, :, cols], blocks_of(src[:, :]),
                                                   hth[:, :, cols].bitcast(F32), ALU.subtract)
                elif name[0] == "q":
                    m = int(name[1])
                    for e, half in enumerate(HALF):
                        last = nc.vector.tensor_tensor(q[HALF[1 - e], 2 * m + e, :], src[half, :],
                                                       q[half, 2 * m + e, :].bitcast(F32), ALU.subtract)
                elif name == "k":
                    for g in range(GROUPS):
                        last = nc.vector.tensor_tensor(kl[HALF[g], 1 - p, g, :], src[HALF[g], :],
                                                       kh[HALF[g], 1 - p, g, :].bitcast(F32), ALU.subtract)
                else:
                    last = nc.vector.tensor_tensor(v[:, 1 - p, :, :, DH:],
                                                   src[:, :].rearrange("p (t g d) -> p t g d", t=T, g=GROUPS),
                                                   v[:, 1 - p, :, :, 0:DH].bitcast(F32), ALU.subtract)
                last.then_inc(side_free, 1)

            def total_of(b, use, t):
                dve.wait_ge(side_ready, use + 1)
                dve.wait_ge(xn_ready, b * T + t + 1)
                dve.wait_ge(added, b * T + t + 1)
                nc.vector.tensor_tensor(total[:, t, :], side[side_at(f"wo{t}")][:, :], xn[:, t % 2, :],
                                        ALU.add).then_inc(total_ready, 1)
                dve.wait_ge(total_ready, b * T + t + 1 + 2)
                nc.vector.bn_stats(obn[:, t, :], total[:, t, :]).then_inc(side_free, 1)
                if t == T - 1:
                    wait_alone(dve, s, side_free, use + 1)
                    for t in range(T):
                        last = nc.vector.bn_aggr(omv[:, t, :], obn[:, t, :])
                    last.then_inc(ostats, 1)

            def sum_of(b, hd):
                dve.wait_ge(part_ready, b * HEADS + hd + 1)
                m = hd // 2
                if hd % 2 == 0 and not (is_first(b) and hd >= 0):
                    dve.wait_ge(ol_ready, b * T + m + 1)
                nc.vector.tensor_tensor(out_sum[HALF[hd % 2], m % T, :], output[hd % 2][HALF[0], :],
                                        v_lo_part[:, hd % 2, :], ALU.add).then_inc(sum_ready, 1)

            def hi_of_output(b, m):
                dve.wait_ge(sum_ready, b * HEADS + 2 * m + 2)
                nc.vector.tensor_copy(oh[:, m, :], out_sum[:, m, :]).then_inc(oh_ready, 1)

            dve.sem_inc(total_ready, 2)
            dve.wait_ge(s.w_loaded, 6 * 16)
            nc.vector.tensor_tensor(feature[:, 2, :], feature[:, 0, :], feature[:, 1, :],
                                    ALU.mult).then_inc(scaled_step, 1)
            dve.wait_ge(scaled_step, 1)
            raw_k, raw_v = blocks_of(out_sum[:, 0, :]), blocks_of(out_sum[:, 1, :])
            for k in range(T):
                for w in (raw_k, raw_v):
                    last = nc.vector.tensor_scalar(w[:, k, :], w[:, k, :], feature[:, 2, k:k + 1], None, ALU.mult)
            last.then_inc(scaled, 1)
            for k in range(T):
                last = nc.vector.tensor_scalar(prob[:, k, :], prob[:, k, :], feature[:, 2, k:k + 1], DH ** -0.5,
                                               ALU.mult, ALU.mult)
            last.then_inc(scaled, 1)
            dve.wait_ge(w_hi, 1)
            nc.vector.tensor_tensor(wkl[:, :, :], raw_k, wkh[:, :, :].bitcast(F32), ALU.subtract)
            nc.vector.tensor_tensor(wvl[:, :, :], raw_v, wvh[:, :, :].bitcast(F32), ALU.subtract).then_inc(w_lo, 1)
            for t in range(T):
                lo_of(-1, 1, f"h{t}")
            dve.wait_ge(w_hi, 2)
            nc.vector.tensor_tensor(wql[:, :, :], prob[:, :, :], wqh[:, :, :].bitcast(F32),
                                    ALU.subtract).then_inc(w_lo, 1)
            lo_of(-1, 1, "k")
            lo_of(-1, 1, "v")
            lo_of(-1, 1, "q0")

            def step(b, p, u, first, last, drain):
                g = b * UNITS + u
                if not drain:
                    dve.wait_ge(scored, g + 1)
                    at = u % 4
                    nc.vector.reduce_max(neg_max[:, at:at + 1], score[u % 2][:, :], AX,
                                         negate=True).then_inc(max_ready, 1)
                if (u > 0 or not first) and (not drain or u == 0):
                    at = (u - 1) % 4
                    dve.wait_ge(exp_ready, g)
                    nc.vector.reciprocal(inv_sum[:, at:at + 1], row_sum[:, at:at + 1]).then_inc(inv_ready, 1)
                for name in side_done(u, first, last, drain, 2):
                    if name in SPLIT:
                        lo_of(b, p, name)
                turn_u = u - TURN_LAG
                if not (first and turn_u < 0) and not (drain and turn_u >= 0):
                    dve.wait_ge(hi_ready, g - TURN_LAG + 1)
                    cols = slice(turn_u % T * P, (turn_u % T + 1) * P)
                    at = (turn_u // T) % 2
                    nc.vector.tensor_tensor(ptl[:, at, :, cols], blocks_of(turned[turn_u % 2][:, :]),
                                            pth[:, at, :, cols].bitcast(F32), ALU.subtract).then_inc(lo_ready, 1)
                for name in side_done(u, first, last, drain, 1):
                    if name not in SPLIT:
                        total_of(b - 1, side_use(b, name), int(name[2]))
                done = u - SUM_LAG
                if done % T == 0 and not (first and done < 0) and not (drain and done >= 0):
                    hd = done // T
                    sum_of(b, hd)
                for m, at in enumerate(CONVERT):
                    if at == u and not drain:
                        hi_of_output(b, m)
                    if at - UNITS == u and not first:
                        hi_of_output(b - 1, m)
                for t, at in enumerate(STATS):
                    if at == u and not last and not drain:
                        stats_of(b + 1, 1 - p, t)

            def body(b, p, first, last):
                for u in range(UNITS):
                    step(b, p, u, first, last, False)

            over_batches(dve, body)
            for u in range(WO[-1] + 2):
                if u == WO[0]:
                    dve.wait_ge(s.ffn_x_loaded, 16)
                    following.statistics(nc, dve, [x[:, 0, t, :] for t in range(T)])
                step(B, 0, u, False, True, True)
            for t in range(T):
                dve.wait_ge(normed_ready, (B - 1) * T + t + 1)
                nc.vector.tensor_tensor(res[:, t, :], res[:, t, :], total[:, t, :], ALU.add).then_inc(last_added, 1)

        @block.tensor
        def _(pe):
            def side_bank(use):
                if not (isinstance(use, int) and use < 2):
                    pe.wait_ge(side_free, use - 1)

            def turn_h(b, use, t):
                side_bank(use)
                pe.wait_ge(h_ready, b * T + t + 1)
                for k in range(T):
                    cols = slice(k * P, (k + 1) * P)
                    last = nc.tensor.transpose(side[side_at(f"h{t}")][:, cols], h[:, t % 2, cols], s.identity[:, :])
                last.then_inc(side_ready, 1)

            def split(lh, ll, rh, rl):
                return ((lh, rh), (ll, rh), (lh, rl))

            def side_share(b, name, start, end, done):
                use, out = side_use(b, name), side[side_at(name)]
                if name[0] == "h":
                    return turn_h(b + 1, use, int(name[1]))
                if start == 0:
                    side_bank(use)
                if name == "k" and start == 0:
                    pe.wait_ge(side_free, side_use(b, "h3") + 1)
                if name == "wo0" and start == 0:
                    pe.wait_ge(ol_ready, (b + 1) * T)
                for m in range(start, end):
                    k, n, bank_cols = m // 3 % T, m % 3, slice(0, N)
                    if name == "v":
                        cols = bank_cols = slice(m // (3 * T) * P, (m // (3 * T) + 1) * P)
                        pairs = split(hth[:, k, cols], htl[:, k, cols], wvh[:, k, :], wvl[:, k, :])
                    elif name == "k":
                        pairs = split(wkh[:, k, :], wkl[:, k, :], hth[:, k, :], htl[:, k, :])
                    else:
                        cols = slice(int(name[-1]) * P, (int(name[-1]) + 1) * P)
                        pairs = (split(wqh[:, k, cols], wql[:, k, cols], hth[:, k, :], htl[:, k, :])
                                 if name[0] == "q" else
                                 split(oh[:, k, cols], ol[:, k, cols], woh[:, k, :], wol[:, k, :]))
                    last = nc.tensor.matmul(out[:, bank_cols], *pairs[n], start=(k == 0 and n == 0),
                                            stop=(k == T - 1 and n == 2))
                if done:
                    last.then_inc(side_ready, 1)

            for t in range(T):
                turn_h(0, t, t)
            for name, count, group in (("k", 3 * T, 1), ("v", 3 * T * T, 1), ("q0", 3 * T, 2)):
                pe.wait_ge(w_lo, group)
                side_share(-1, name, 0, count, True)

            def step(b, p, u, first, last, drain):
                g = b * UNITS + u
                turn_u = u - TURN_LAG
                if not (first and turn_u < 0) and not (drain and turn_u >= 0):
                    pe.wait_ge(prob_ready, g - TURN_LAG + 1)
                    if not (first and turn_u < 2):
                        pe.wait_ge(lo_ready, g - TURN_LAG - 1)
                    for k in range(T):
                        cols = slice(k * P, (k + 1) * P)
                        mm = nc.tensor.transpose(turned[turn_u % 2][:, cols], prob[:, turn_u % 4, cols],
                                                 s.identity[:, :])
                    mm.then_inc(turn_ready, 1)
                if not drain:
                    hd, row = u // T, u % T
                    if u == 0:
                        pe.wait_ge(side_free, side_use(b, "q1"))
                        pe.wait_ge(k_repeated, b + 1)
                    elif u % (2 * T) == 0:
                        pe.wait_ge(side_free, side_use(b, f"q{u // (2 * T)}") + 1)
                    if not (first and u < 2):
                        pe.wait_ge(exp_ready, g - 1)
                    lhsT = q[:, hd, row * P:(row + 1) * P]
                    products(nc, score[u % 2][:, :], [(lhsT, kh[:, p, hd // HPG, :]), (lhsT, kl[:, p, hd // HPG, :])]
                             ).then_inc(scored, 1)
                out_u = u - OUT_LAG
                if out_u % T < 2 and not (first and out_u < 0) and not (drain and out_u >= 0):
                    hd = out_u // T
                    if out_u % T == 0:
                        pe.wait_ge(lo_ready, (b * HEADS + hd + 1) * T)
                        if not (first and hd < 2):
                            pe.wait_ge(sum_ready, b * HEADS + hd - 1)
                    for t in (out_u % T * 2, out_u % T * 2 + 1):
                        lhsT = v[:, p if out_u >= 0 else 1 - p, t, hd % HEADS // HPG, :]
                        nc.tensor.matmul(output[hd % 2][:, :], lhsT, pth[:, hd % 2, t, :],
                                         start=(t == 0), stop=False)
                        mm = nc.tensor.matmul(output[hd % 2][:, :], lhsT, ptl[:, hd % 2, t, :], start=False,
                                              stop=(t == T - 1))
                    if t == T - 1:
                        mm.then_inc(out_ready, 1)
                for name, start, end, done in side_works(u, first, last, drain):
                    side_share(b, name, start, end, done)

            def body(b, p, first, last):
                for u in range(UNITS):
                    step(b, p, u, first, last, False)

            over_batches(pe, body)
            for u in range(WO[-1] + 1):
                step(B, 0, u, False, True, True)


INNER_PAIRS = IT + T // 2


def turn_bank(p, t):
    return (p * INNER_PAIRS + t // 2) % 2 * 2 + t % 2


def pair_at(p, i):
    return (p * INNER_PAIRS + T // 2 + i) % 2 * 2


def ffn_fetch(nc, s, gate_t, up_t, down_t, x_in):
    s.ffn_x_loaded = s.stack.enter_context(nc.semaphore("f1_x_first_loaded"))
    s.ffn_raw_loaded = s.stack.enter_context(nc.semaphore("f1_raw_first_loaded"))

    def fetch(sp):
        sp.dma_start(s.x_pair[:, 0, :, :], rows_of(x_in, 0)).then_inc(s.ffn_x_loaded, 16)
        for j, src in enumerate((gate_t, up_t, down_t)):
            sp.dma_start(s.x_pair[:, 1, j, :], src[0, :, :]).then_inc(s.ffn_raw_loaded, 16)

    return fetch


def gated_ffn(nc, s, gate_t, up_t, down_t, gate_s, up_s, down_s, x_in, out, norm_in):
    with ExitStack() as ctx:
        def sb(name, shape, dt=F32):
            return ctx.enter_context(nc.sbuf_tensor("f_" + name, shape, dt))

        def sem(name):
            return s.stack.enter_context(nc.semaphore("f1_" + name))

        def bank(name):
            return ctx.enter_context(nc.psum_tensor("f_" + name, [P, N], F32))

        wh, wl = sb("wh", [P, IT, 3, N], F32R), sb("wl", [P, IT, 3, N], F32R)
        inner_scale = sb("inner_scale", [P, 2, IT])
        down_scale = sb("down_scale", [P, N])
        x = s.x_pair
        xn = sb("xn", [P, T, N])
        xth, xtl = sb("xth", [P, T, N], F32R), sb("xtl", [P, T, N], F32R)
        silu = sb("silu", [P, 2, N])
        hidden = sb("hidden", [P, 2, N])
        hh, hl = sb("hh", [P, 2, N], F32R), sb("hl", [P, 2, N], F32R)
        y = sb("y", [P, T, N])
        lo_max, lo_column, lo_row = sb("lo_max", [P, IT]), sb("lo_column", [P, 1]), sb("lo_row", [1, P])
        lo_most, lo_counts = sb("lo_most", [1, 1]), sb("lo_counts", [1, 1], I32)
        bn, mv, ve, rs, shift = norm_in.bn, norm_in.mv, norm_in.ve, norm_in.rs, norm_in.shift
        obn, omv = sb("obn", [P, T, 6]), sb("omv", [P, T, 2])
        ove, ors, oshift = sb("ove", [P, T]), sb("ors", [P, T]), sb("oshift", [P, T])
        inner = [bank(f"inner{i}") for i in range(4)]
        down = [bank(f"down{i}") for i in range(T)]
        raw = [x[:, 1, 0:3, :], y[:, 0:3, :]]

        raw_loaded = [s.ffn_raw_loaded, sem("raw_loaded1")]
        scale_loaded, wh_ready, wl_ready = sem("scale_loaded"), sem("wh_ready"), sem("wl_ready")
        x_loaded, stored = [s.ffn_x_loaded, sem("x_loaded1")], sem("stored")
        own_bn, stats, pool_step, scales = norm_in.own_bn, norm_in.stats, norm_in.pool_step, norm_in.scales
        xn_ready, turn_ready, th_ready, tl_ready = sem("xn_ready"), sem("turn_ready"), sem("th_ready"), sem("tl_ready")
        gate_ready, up_ready, silu_ready, hidden_ready = (
            sem("gate_ready"), sem("up_ready"), sem("silu_ready"), sem("hidden_ready"))
        hh_ready, hl_ready, down_used = sem("hh_ready"), sem("hl_ready"), sem("down_used")
        y_ready, own_obn, ostats, opool, oscales = (
            sem("y_ready"), sem("own_obn"), sem("ostats"), sem("opool"), sem("oscales"))
        normed, added = sem("normed"), sem("added")
        last_added = sem("last_added")
        lo_step, lo_turned = sem("lo_step"), sem("lo_turned")

        block = ctx.enter_context(nc.Block())

        def is_first(b):
            return isinstance(b, int) and b == 0

        @block.sync
        def _(sp):
            sp.wait_ge(s.attended_stored, (B + 1) * 16)
            for dst, src in ((inner_scale[:, 0, :], gate_s), (inner_scale[:, 1, :], up_s),
                             (down_scale[:, :], down_s.partition_broadcast(P))):
                sp.dma_start(dst, src).then_inc(scale_loaded, 16)
            for i in range(1, IT):
                if i >= 2:
                    sp.wait_ge(wl_ready, i - 1)
                for j, src in enumerate((gate_t, up_t, down_t)):
                    sp.dma_start(raw[i % 2][:, j, :], src[i, :, :]).then_inc(raw_loaded[i % 2], 16)
            sp.wait_ge(wl_ready, IT)
            sp.dma_start(x[:, 1, :, :], rows_of(x_in, 1)).then_inc(x_loaded[1], 16)
            sp.wait_ge(lo_step, 2)
            sp.dma_start(lo_row[:, :], lo_column[:, :]).then_inc(lo_turned, 16)

            def store(b, p):
                sp.wait_ge(added, (b + 2) * T)
                sp.dma_start(rows_of(out, b), x[:, p, :, :]).then_inc(stored, 16)

            def body(b, p, first, last):
                if not first:
                    store(b - 1, 1 - p)
                if not last and not first:
                    sp.wait_ge(stored, b * 16)
                    sp.dma_start(x[:, 1 - p, :, :], rows_of(x_in, b + 1)).then_inc(x_loaded[1 - p], 16)

            over_batches(sp, body)
            for t in range(T):
                sp.wait_ge(last_added, t + 1)
                sp.dma_start(out[B - 1, t * P:(t + 1) * P, :], x[:, (B - 1) % 2, t, :]).then_inc(stored, 16)
            sp.wait_ge(stored, (B - 1 + T) * 16)

        @block.gpsimd
        def _(pool):
            def scales_of(b):
                if not is_first(b):
                    pool.wait_ge(xn_ready, b * T)
                wait_alone(pool, s, stats, b + 1)
                row_scales(nc, s, pool, mv, ve[:, :], rs[:, :], shift[:, :], s.minus_half[:, :],
                           pool_step, b * 2).then_inc(scales, 1)

            def lo_of_hidden(b, i, at):
                pool.wait_ge(hh_ready, b * IT + i + 1)
                nc.gpsimd.tensor_tensor(hl[:, at, :], hidden[:, at, :], hh[:, at, :].bitcast(F32),
                                        ALU.subtract).then_inc(hl_ready, 1)

            def output_scales(b):
                wait_alone(pool, s, ostats, b + 1)
                row_scales(nc, s, pool, omv, ove[:, :], ors[:, :], oshift[:, :], s.minus_half[:, :],
                           opool, b * 2).then_inc(oscales, 1)

            def add(b, p, t):
                pool.wait_ge(normed, b * T + t + 1)
                nc.gpsimd.tensor_tensor(x[:, p, t, :], x[:, p, t, :], y[:, t, :], ALU.add).then_inc(added, 1)

            pool.sem_inc(added, T)
            def body(b, p, first, last):
                for i in range(IT):
                    if not first:
                        if i == 1:
                            output_scales(b - 1)
                        if 2 <= i < 2 + T:
                            add(b - 1, 1 - p, i - 2)
                    if i == 9 and not first and not last:
                        scales_of(b + 1)
                    lo_of_hidden(b, i, (i + p) % 2)
                if first:
                    scales_of(b + 1)

            over_batches(pool, body)
            output_scales(B - 1)

        @block.scalar
        def _(act):
            def normalised(b, p):
                act.wait_ge(scales, b + 1)
                if not is_first(b):
                    act.wait_ge(turn_ready, b * T)
                for t in range(T):
                    nc.scalar.activation(xn[:, t, :], x[:, p, t, :], ACT.Identity, bias=shift[:, t:t + 1],
                                         scale=rs[:, t:t + 1]).then_inc(xn_ready, 1)

            def hi_of_xt(b, t, bank_of):
                if t == 0 and not is_first(b):
                    act.wait_ge(up_ready, b * IT)
                act.wait_ge(turn_ready, b * T + t + 1)
                nc.scalar.copy(xth[:, :, t * P:(t + 1) * P],
                               blocks_of(inner[bank_of(t)][:, :])).then_inc(th_ready, 1)

            def silu_of(b, p, i, first):
                act.wait_ge(gate_ready, b * IT + i + 1)
                if not (first and i < 2):
                    act.wait_ge(hidden_ready, b * IT + i - 1)
                at = (i + p) % 2
                nc.scalar.activation(silu[:, at, :], inner[pair_at(p, i)][:, :], ACT.Silu,
                                     scale=inner_scale[:, 0, i:i + 1]).then_inc(silu_ready, 1)

            def norm(b, t):
                if t == 0:
                    act.wait_ge(oscales, b + 1)
                nc.scalar.activation(y[:, t, :], y[:, t, :], ACT.Identity, bias=oshift[:, t:t + 1],
                                     scale=ors[:, t:t + 1]).then_inc(normed, 1)

            normalised(0, 0)
            for t in range(T):
                hi_of_xt(0, t, lambda t: turn_bank(0, t))
            act.wait_ge(scale_loaded, 48)

            def body(b, p, first, last):
                for i in range(IT):
                    if first:
                        act.wait_ge(raw_loaded[i % 2], (i // 2 + 1) * 48)
                        nc.scalar.copy(wh[:, i, :, :], raw[i % 2]).then_inc(wh_ready, 1)
                    silu_of(b, p, i, first)
                    if 2 <= i < 2 + T and not first:
                        norm(b - 1, i - 2)
                if not last:
                    normalised(b + 1, 1 - p)
                    for t in range(T):
                        hi_of_xt(b + 1, t, lambda t: turn_bank(1 - p, t))

            over_batches(act, body)
            for t in range(T):
                norm(B - 1, t)

        @block.vector
        def _(dve):
            def stats_of(b, p):
                dve.wait_ge(x_loaded[p], (b - p) * 8 + 16)
                if not is_first(b):
                    dve.wait_ge(stats, b)
                for t in range(T):
                    last = nc.vector.bn_stats(bn[:, t, :], x[:, p, t, :])
                last.then_inc(own_bn, 1)
                if not is_first(b):
                    dve.wait_ge(scales, b)
                wait_alone(dve, s, own_bn, b + 1)
                for t in range(T):
                    last = nc.vector.bn_aggr(mv[:, t, :], bn[:, t, :])
                last.then_inc(stats, 1)

            def lo_of_xt(b, t, at):
                dve.wait_ge(th_ready, b * T + t + 1)
                cols = slice(t * P, (t + 1) * P)
                nc.vector.tensor_tensor(xtl[:, :, cols], blocks_of(inner[at][:, :]),
                                        xth[:, :, cols].bitcast(F32), ALU.subtract).then_inc(tl_ready, 1)

            def hidden_of(b, p, i, first):
                dve.wait_ge(up_ready, b * IT + i + 1)
                dve.wait_ge(silu_ready, b * IT + i + 1)
                if not (first and i < 2):
                    dve.wait_ge(hl_ready, b * IT + i - 1)
                at = (i + p) % 2
                nc.vector.scalar_tensor_tensor(out=hidden[:, at, :], in0=inner[pair_at(p, i) + 1][:, :],
                                               scalar=inner_scale[:, 1, i:i + 1], in1=silu[:, at, :],
                                               op0=ALU.mult, op1=ALU.mult).then_inc(hidden_ready, 1)
                if not (first and i < 2):
                    dve.wait_ge(down_used, b * IT + i - 1)
                dve.wait_ge(hidden_ready, b * IT + i + 1)
                nc.vector.tensor_copy(hh[:, at, :], hidden[:, at, :]).then_inc(hh_ready, 1)

            def y_of(b, t):
                dve.wait_ge(down_used, (b + 1) * IT)
                dve.wait_ge(added, b * T + t + 1)
                nc.vector.tensor_tensor(y[:, t, :], down[t][:, :], down_scale[:, :], ALU.mult).then_inc(y_ready, 1)

            def output_stats(b):
                for t in range(T):
                    dve.wait_ge(y_ready, b * T + t + 1)
                    last = nc.vector.bn_stats(obn[:, t, :], y[:, t, :])
                last.then_inc(own_obn, 1)
                wait_alone(dve, s, own_obn, b + 1)
                for t in range(T):
                    last = nc.vector.bn_aggr(omv[:, t, :], obn[:, t, :])
                last.then_inc(ostats, 1)

            for t in range(T):
                lo_of_xt(0, t, turn_bank(0, t))
            dve.wait_ge(scale_loaded, 48)

            def body(b, p, first, last):
                for i in range(IT):
                    if first:
                        dve.wait_ge(wh_ready, i + 1)
                        nc.vector.tensor_tensor(wl[:, i, :, :], raw[i % 2], wh[:, i, :, :].bitcast(F32),
                                                ALU.subtract).then_inc(wl_ready, 1)
                        dve.wait_ge(wl_ready, i + 1)
                        largest = nc.vector.tensor_reduce(lo_max[:, i:i + 1], wl[:, i, :, :].bitcast(F32),
                                                          mybir.AxisListType.XY, ALU.max,
                                                          apply_absolute_value=True)
                        if i == IT - 1:
                            largest.then_inc(lo_step, 1)
                            dve.wait_ge(lo_step, 1)
                            nc.vector.reduce_max(lo_column[:, :], lo_max[:, :], AX).then_inc(lo_step, 1)
                    if i == 0 and not first:
                        for t in range(T):
                            y_of(b - 1, t)
                    hidden_of(b, p, i, first)
                    if i == 0 and not first:
                        output_stats(b - 1)
                    if i == (IT - 1 if first else 8) and not last:
                        stats_of(b + 1, 1 - p)
                if not last:
                    for t in range(T):
                        lo_of_xt(b + 1, t, turn_bank(1 - p, t))
                if first:
                    dve.wait_ge(lo_turned, 16)
                    nc.vector.reduce_max(lo_most[:, :], lo_row[:, :], AX).then_inc(lo_step, 1)
                    dve.wait_ge(lo_step, 3)
                    nc.vector.tensor_scalar(lo_counts[:, :], lo_most[:, :], 0.0, None,
                                            ALU.is_gt).then_inc(lo_step, 1)

            over_batches(dve, body)
            for t in range(T):
                y_of(B - 1, t)
            output_stats(B - 1)
            for t in range(T):
                dve.wait_ge(normed, (B - 1) * T + t + 1)
                last_x = x[:, (B - 1) % 2, t, :]
                nc.vector.tensor_tensor(last_x, last_x, y[:, t, :], ALU.add).then_inc(last_added, 1)

        @block.tensor
        def _(pe):
            def turn(b, p, t):
                pe.wait_ge(xn_ready, b * T + t + 1)
                if not is_first(b):
                    pe.wait_ge(hidden_ready, b * IT - 1 + t // 2)
                for k in range(T):
                    cols = slice(k * P, (k + 1) * P)
                    last = nc.tensor.transpose(inner[turn_bank(p, t)][:, cols], xn[:, t, cols], s.identity[:, :])
                last.then_inc(turn_ready, 1)

            def inner_of(b, p, i, first, with_lo):
                if first:
                    pe.wait_ge(wl_ready, i + 1)
                if i == 0:
                    pe.wait_ge(tl_ready, (b + 1) * T)
                if i >= 2:
                    pe.wait_ge(hidden_ready, b * IT + i - 1)
                for j, done in ((0, gate_ready), (1, up_ready)):
                    pairs = []
                    for k in range(T):
                        cols = slice(k * P, (k + 1) * P)
                        pairs += [(wh[:, i, j, cols], xth[:, k, :]), (wh[:, i, j, cols], xtl[:, k, :])]
                        if with_lo:
                            pairs.append((wl[:, i, j, cols], xth[:, k, :]))
                    products(nc, inner[pair_at(p, i) + j][:, :], pairs).then_inc(done, 1)

            def down_of(b, p, i, first, with_lo):
                pe.wait_ge(hl_ready, b * IT + i + 1)
                if i == 0 and not first:
                    pe.wait_ge(y_ready, b * T)
                at = (i + p) % 2
                for t in range(T):
                    cols = slice(t * P, (t + 1) * P)
                    halves = ((hh, wh), (hl, wh), (hh, wl)) if with_lo else ((hh, wh), (hl, wh))
                    for n, (l, r) in enumerate(halves):
                        last = nc.tensor.matmul(down[t][:, :], l[:, at, cols], r[:, i, 2, :],
                                                start=(i == 0 and n == 0),
                                                stop=(i == IT - 1 and n == len(halves) - 1))
                last.then_inc(down_used, 1)

            for t in range(T):
                turn(0, 0, t)

            def batch(b, p, first, last, with_lo):
                for i in range(IT):
                    inner_of(b, p, i, first, with_lo)
                    if i > 0:
                        down_of(b, p, i - 1, first, with_lo)
                if not last:
                    for t in range(T):
                        turn(b + 1, 1 - p, t)
                down_of(b, p, IT - 1, first, with_lo)

            def batches_after_first(with_lo):
                with pe.Fori(0, (B - 2) // 2) as i:
                    batch(i * 2 + 1, 1, False, False, with_lo)
                    batch(i * 2 + 2, 0, False, False, with_lo)
                batch(B - 1, 1, False, True, with_lo)

            batch(0, 0, True, False, True)
            pe.wait_ge(lo_step, 4)
            lo_count = pe.value_load(lo_counts[0:1, 0:1], min_val=0, max_val=1)
            with pe.If(lo_count > 0):
                batches_after_first(True)
            with pe.Else():
                batches_after_first(False)


def four_blocks(nc, x_in, factors, bias, norm_scale, split_scale, wq_t, wk_t, wv_t, wo_t,
                gate_t, up_t, down_t, gate_s, up_s, down_s, out):
    x_mixed = nc.dram_tensor("x_mixed", [B, N, N], F32).ap()
    x_attended = nc.dram_tensor("x_attended", [B, N, N], F32).ap()

    with ExitStack() as stack:
        s = Shared()
        s.stack = stack
        prepare(nc, s)
        started = stack.enter_context(ExitStack())
        with ExitStack() as resident:
            s.x = resident.enter_context(nc.sbuf_tensor("x_resident", [P, B * T, N], F32))
            s.factor_sum = resident.enter_context(nc.sbuf_tensor("factor_sum", [P, T, N], F32))
            mix_norm = FirstNorm(nc, s, stack, "f0_norm")
            attention_norm = FirstNorm(nc, s, stack, "a1_norm")
            ffn_norm = FirstNorm(nc, s, stack, "f1_norm")
            column_attention(nc, s, x_in, factors, mix_norm)
            s.x_pair = stack.enter_context(nc.sbuf_tensor("x_pair", [P, 2, T, N], F32, side="right"))
            attention_start = attention_fetch(nc, s, started, norm_scale, split_scale, wq_t, wk_t, wv_t, wo_t, x_mixed)
            linear_map(nc, s, bias, x_mixed, attention_start, mix_norm, attention_norm)
        ffn_start = ffn_fetch(nc, s, gate_t, up_t, down_t, x_attended)
        grouped_attention(nc, s, x_mixed, x_attended, ffn_start, attention_norm, ffn_norm)
        started.close()
        gated_ffn(nc, s, gate_t, up_t, down_t, gate_s, up_s, down_s, x_attended, out, ffn_norm)


def kernel(L0_attn_x, L0_ffn_factors, L0_ffn_bias, L1_attn_norm_scale, L1_attn_split_scale,
           L1_attn_Wq, L1_attn_Wk, L1_attn_Wv, L1_attn_Wo,
           L1_ffn_gate_w, L1_ffn_up_w, L1_ffn_down_w, L1_ffn_gate_s, L1_ffn_up_s, L1_ffn_down_s):
    import numpy as np
    import concourse.bacc as bacc
    from concourse.bass_utils import run_bass_kernel_spmd

    def per_partition(v):
        return v.reshape(-1, P).T

    def inner_tiles(w):
        return w.reshape(IT, P, T, P).transpose(0, 3, 2, 1).reshape(IT, P, N)

    arrays = {
        "x": L0_attn_x, "factors": L0_ffn_factors, "bias": L0_ffn_bias,
        "norm_scale": per_partition(L1_attn_norm_scale), "split_scale": per_partition(L1_attn_split_scale),
        "wq_t": L1_attn_Wq.T, "wk_t": L1_attn_Wk.T, "wv_t": L1_attn_Wv.T, "wo_t": L1_attn_Wo.T,
        "gate_t": inner_tiles(L1_ffn_gate_w), "up_t": inner_tiles(L1_ffn_up_w),
        "down_t": L1_ffn_down_w.T.reshape(IT, P, N),
        "gate_s": per_partition(L1_ffn_gate_s), "up_s": per_partition(L1_ffn_up_s), "down_s": L1_ffn_down_s,
    }
    arrays = {name: np.ascontiguousarray(a) for name, a in arrays.items()}
    nc = bacc.Bacc("TRN2", target_bir_lowering=False, num_devices=1)
    args = [nc.dram_tensor(name, a.shape, F32, kind="ExternalInput").ap() for name, a in arrays.items()]
    out = nc.dram_tensor("out", (B, N, N), F32, kind="ExternalOutput")
    four_blocks(nc, *args, out.ap())
    result = run_bass_kernel_spmd(nc, [arrays], core_ids=[0])
    return result.results[0]["out"]
```
